# Optimizing a Trainium2 kernel written in Bass

```python
import numpy as np
import jax
import jax.numpy as jnp

def _softmax(x, axis=-1):
    return jax.nn.softmax(x, axis=axis)

def _gelu(x):
    return jax.nn.gelu(x, approximate=True)

def _silu(x):
    return jax.nn.silu(x)

def _sigmoid(x):
    return jax.nn.sigmoid(x)

def _layernorm(x, axis=-1, eps=1e-05):
    m = jnp.mean(x, axis=axis, keepdims=True)
    v = jnp.var(x, axis=axis, keepdims=True)
    return (x - m) / jnp.sqrt(v + eps)

def _scatter_add(tgt, idx, src, axis=0):
    return tgt.at[idx].add(src)

def _segment_sum(src, seg, n):
    return jax.ops.segment_sum(src, seg, n)
kernel_name = 'mk_gnn_resnorm_d2_gnn_r8_02097e'

def setup_inputs(seed: int=0):
    np.random.seed(seed)
    _w = jnp.asarray

    def _rec_inputs():
        import jax
        import jax.numpy as jnp
        _gk = jax.random.key(seed)
        x = -0.000202 + 1 * jax.random.normal(jax.random.fold_in(_gk, 1), (12500, 128), jnp.float32)
        _s = jax.random.randint(jax.random.fold_in(_gk, 2), (100000,), 0, 12500, jnp.int32)
        _d = jax.random.randint(jax.random.fold_in(_gk, 3), (100000,), 0, 12500, jnp.int32)
        _loop = jnp.arange(12500, dtype=jnp.int32)
        src = jnp.concatenate([_s, _d, _loop])
        dst = jnp.concatenate([_d, _s, _loop])
        _o = jnp.argsort(dst, stable=True)
        src = src[_o]
        dst = dst[_o]
        edge_type_8 = jax.random.randint(jax.random.fold_in(_gk, 13), (212500,), 0, 8, jnp.int32)
        return (x, src, dst, edge_type_8)
    x, src, dst, edge_type_8 = _rec_inputs()

    def _L0_gnn_setup():
        import jax, jax.numpy as jnp
        import numpy as np
        N_NODES = 6250
        N_EDGES = 100000
        C_IN = 128
        HID = 128
        C_OUT = 128

        def _glorot(key, shape):
            fan_in, fan_out = shape
            lim = (6.0 / (fan_in + fan_out)) ** 0.5
            return jax.random.uniform(key, shape, jnp.float32, -lim, lim)

        def _edge_conv(x, src, dst, W1, b1, W2, b2, n_nodes):
            xi = x[dst]
            xj = x[src]
            m = jnp.concatenate([xi, xj - xi], axis=-1)
            h = jax.nn.relu(m @ W1 + b1) @ W2 + b2
            agg = jax.ops.segment_max(h, dst, num_segments=n_nodes)
            return jnp.where(jnp.isfinite(agg), agg, 0.0)
        key = jax.random.key(seed)
        ks = jax.random.split(key, 8)
        x = jax.random.normal(ks[0], (N_NODES, C_IN), jnp.float32)
        edge_index = jax.random.randint(ks[1], (2, N_EDGES), 0, N_NODES, jnp.int32)
        return {'x': x, 'edge_index': edge_index, 'W1_in': _glorot(ks[2], (2 * C_IN, HID)), 'b1_in': jnp.zeros((HID,), jnp.float32), 'W2_in': _glorot(ks[3], (HID, HID)), 'b2_in': jnp.zeros((HID,), jnp.float32), 'W1_hid': _glorot(ks[4], (2 * HID, HID)), 'b1_hid': jnp.zeros((HID,), jnp.float32), 'W2_hid': _glorot(ks[5], (HID, HID)), 'b2_hid': jnp.zeros((HID,), jnp.float32), 'W1_out': _glorot(ks[6], (2 * HID, HID)), 'b1_out': jnp.zeros((HID,), jnp.float32), 'W2_out': _glorot(ks[7], (HID, C_OUT)), 'b2_out': jnp.zeros((C_OUT,), jnp.float32)}
    _L0_gnn_all = _L0_gnn_setup()
    _L0_gnn_in = {k: v for k, v in _L0_gnn_all.items() if k in ('W1_in', 'b1_in', 'W2_in', 'b2_in', 'W1_hid', 'b1_hid', 'W2_hid', 'b2_hid', 'W1_out', 'b1_out', 'W2_out', 'b2_out')}
    del _L0_gnn_all

    def _L1_gnn_setup():
        import jax, jax.numpy as jnp
        import numpy as np
        N_NODES = 12500
        N_EDGES = 400000
        N_REL = 8
        EMB = 128
        key = jax.random.key(seed)
        k1, k2, k3, k4, k5 = jax.random.split(key, 5)
        node_emb = jax.random.normal(k1, (N_NODES, EMB), dtype=jnp.float32)
        weights = jax.random.normal(k2, (N_REL, EMB, EMB), dtype=jnp.float32)
        src = jax.random.randint(k3, (N_EDGES,), 0, N_NODES, dtype=jnp.int64 if jax.config.jax_enable_x64 else jnp.int32).astype(jnp.int64)
        rel = jax.random.randint(k4, (N_EDGES,), 0, N_REL).astype(jnp.int64)
        dst = jax.random.randint(k5, (N_EDGES,), 0, N_NODES).astype(jnp.int64)
        return {'node_emb': node_emb, 'weights': weights, 'src': src, 'rel': rel, 'dst': dst}
    _L1_gnn_all = _L1_gnn_setup()
    _L1_gnn_in = {k: v for k, v in _L1_gnn_all.items() if k in ('weights',)}
    del _L1_gnn_all
    return {'x': x, 'src': src, 'dst': dst, 'edge_type_8': edge_type_8, 'L0_gnn_W1_in': _L0_gnn_in['W1_in'], 'L0_gnn_b1_in': _L0_gnn_in['b1_in'], 'L0_gnn_W2_in': _L0_gnn_in['W2_in'], 'L0_gnn_b2_in': _L0_gnn_in['b2_in'], 'L0_gnn_W1_hid': _L0_gnn_in['W1_hid'], 'L0_gnn_b1_hid': _L0_gnn_in['b1_hid'], 'L0_gnn_W2_hid': _L0_gnn_in['W2_hid'], 'L0_gnn_b2_hid': _L0_gnn_in['b2_hid'], 'L0_gnn_W1_out': _L0_gnn_in['W1_out'], 'L0_gnn_b1_out': _L0_gnn_in['b1_out'], 'L0_gnn_W2_out': _L0_gnn_in['W2_out'], 'L0_gnn_b2_out': _L0_gnn_in['b2_out'], 'L1_gnn_weights': _L1_gnn_in['weights']}

def reference(x, src, dst, edge_type_8, L0_gnn_W1_in, L0_gnn_b1_in, L0_gnn_W2_in, L0_gnn_b2_in, L0_gnn_W1_hid, L0_gnn_b1_hid, L0_gnn_W2_hid, L0_gnn_b2_hid, L0_gnn_W1_out, L0_gnn_b1_out, L0_gnn_W2_out, L0_gnn_b2_out, L1_gnn_weights):
    import jax
    import jax.numpy as jnp

    def _L0_gnn_ref(x, edge_index, W1_in, b1_in, W2_in, b2_in, W1_hid, b1_hid, W2_hid, b2_hid, W1_out, b1_out, W2_out, b2_out):
        import jax, jax.numpy as jnp
        import numpy as np
        N_NODES = 6250
        N_EDGES = 100000
        C_IN = 128
        HID = 128
        C_OUT = 128

        def _glorot(key, shape):
            fan_in, fan_out = shape
            lim = (6.0 / (fan_in + fan_out)) ** 0.5
            return jax.random.uniform(key, shape, jnp.float32, -lim, lim)

        def _edge_conv(x, src, dst, W1, b1, W2, b2, n_nodes):
            xi = x[dst]
            xj = x[src]
            m = jnp.concatenate([xi, xj - xi], axis=-1)
            h = jax.nn.relu(m @ W1 + b1) @ W2 + b2
            agg = jax.ops.segment_max(h, dst, num_segments=n_nodes)
            return jnp.where(jnp.isfinite(agg), agg, 0.0)
        src, dst = (edge_index[0], edge_index[1])
        n = x.shape[0]
        x = _edge_conv(x, src, dst, W1_in, b1_in, W2_in, b2_in, n)
        x = jax.nn.relu(x)
        x = _edge_conv(x, src, dst, W1_hid, b1_hid, W2_hid, b2_hid, n)
        x = jax.nn.relu(x)
        x = _edge_conv(x, src, dst, W1_out, b1_out, W2_out, b2_out, n)
        return x

    def _L1_gnn_ref(node_emb, weights, src, rel, dst):
        import jax, jax.numpy as jnp
        import numpy as np
        N_NODES = 12500
        N_EDGES = 400000
        N_REL = 8
        EMB = 128
        n, e = node_emb.shape
        r = weights.shape[0]
        row = src + n * rel
        ones = jnp.ones(row.shape, dtype=node_emb.dtype)
        deg = jax.ops.segment_sum(ones, row, num_segments=r * n)
        inv = 1.0 / deg
        msg = node_emb[dst] * inv[row][:, None]
        agg = jax.ops.segment_sum(msg, row, num_segments=r * n)
        agg = agg.reshape(r, n, e)
        out = jnp.einsum('rij,rnj->ni', weights, agg)
        return jax.nn.relu(out)
    edge_index = jnp.stack([src, dst])
    x = _layernorm(x + _L0_gnn_ref(x, edge_index, L0_gnn_W1_in, L0_gnn_b1_in, L0_gnn_W2_in, L0_gnn_b2_in, L0_gnn_W1_hid, L0_gnn_b1_hid, L0_gnn_W2_hid, L0_gnn_b2_hid, L0_gnn_W1_out, L0_gnn_b1_out, L0_gnn_W2_out, L0_gnn_b2_out), axis=-1)
    x = _layernorm(x + _L1_gnn_ref(x, L1_gnn_weights, src, edge_type_8, dst), axis=-1)
    return x

_drawn_inputs = setup_inputs


def setup_inputs(seed=0):
    import zlib

    import numpy as np

    out = dict(_drawn_inputs(seed))
    spreads = {'L0_gnn_b1_in': (0.0, 0.1),
     'L0_gnn_b2_in': (0.0, 0.1),
     'L0_gnn_b1_hid': (0.0, 0.1),
     'L0_gnn_b2_hid': (0.0, 0.1),
     'L0_gnn_b1_out': (0.0, 0.1),
     'L0_gnn_b2_out': (0.0, 0.1)}
    factors = {}
    for name, (base, spread) in spreads.items():
        noise = np.random.default_rng([zlib.crc32(name.encode()), seed]).standard_normal(out[name].shape)
        drawn = base * np.exp(spread * noise) if base else spread * noise
        out[name] = jnp.asarray(drawn.astype(out[name].dtype))
    for name, factor in factors.items():
        out[name] = (out[name] * factor).astype(out[name].dtype)
    return out
```

```python
from contextlib import ExitStack

import numpy as np
import concourse.bass as bass
from concourse import mybir
from concourse.alu_op_type import AluOpType as ALU

F32 = mybir.dt.float32
I32 = mybir.dt.int32
BF16 = mybir.dt.bfloat16
ACT = mybir.ActivationFunctionType
AX_X = mybir.AxisListType.X
PE_ENGINE = mybir.EngineType.PE
DVE_ENGINE = mybir.EngineType.DVE

P = 128
EPS = 1e-5
BIG = 3.3895313892515355e38
OUT_OF_BLOCK = 255
GT = 4
SL = 4
CB = 7
K = 4
WHY = "the block numbers are clamped to the table when they are made"


def gnn_kernel(nc, x, src, dst, etype, params, w_rel, out):
    N, C = x.shape
    E = dst.shape[0]
    R = w_rel.shape[0]
    assert C == P
    NB = -(-N // P)
    NT = -(-((E + NB * (P - 1)) // P) // (GT * SL)) * GT * SL
    NG = NT // GT
    NI = NG // SL
    NQ = -(-NT // P)
    NTP = NQ * P
    ER = -(-(E + 1) // P)
    LC = -(-ER // P)
    ERP = P * LC
    NC = NB // CB
    NBT = NB + 1
    LAST = N - (NB - 1) * P
    NO_BLOCK = (NB + 2) * P
    TRASH = R * N
    W = P + 1
    ZR = GT * 12 * -(-(TRASH + P) // (NI * GT * 12))
    TR = ZR * NI
    assert NB % CB == 0 and NB + 1 <= P and NB % 2 == 0

    ZP = 48
    assert ZR % ZP == 0

    TAIL = ERP * P + P - E
    dst_pad = nc.dram_tensor("dst_pad", (1 + E + TAIL,), I32).ap()
    src_pad = nc.dram_tensor("src_pad", (E + TAIL,), I32).ap()
    typ_pad = nc.dram_tensor("typ_pad", (E + TAIL,), I32).ap()
    row_dst = nc.dram_tensor("row_dst", (NTP, P), BF16).ap()
    row_cut = nc.dram_tensor("row_cut", (NTP, P), BF16).ap()
    row_key = nc.dram_tensor("row_key", (NTP, P), F32).ap()
    col_meta = nc.dram_tensor("col_meta", (P, NTP, 4), I32).ap()
    blk_row = nc.dram_tensor("blk_row", (NQ, P), I32).ap()
    tab_b = nc.dram_tensor("tab_b", (NB * P, P), F32).ap()
    x1_dram = nc.dram_tensor("x1_dram", (NB * P, P), F32).ap()
    rel_tab = [nc.dram_tensor(f"rel_tab{k}", (TR, W), F32).ap() for k in range(K)]

    with ExitStack() as ctx:
        def sb(name, shape, dt=F32):
            return ctx.enter_context(nc.sbuf_tensor(name, shape, dt))

        def sem(name):
            return ctx.enter_context(nc.semaphore(name))

        ps = ctx.enter_context(nc.psum_tensor("ps", [P, 8, 512], F32))
        flat = ps[:, :, :].rearrange("p b c -> p (b c)")
        agg = sb("agg", [P, NBT * P])
        tab_a = sb("tab_a", [P, NBT * 3 * P], BF16)
        blocks = sb("blocks", [1, NTP], I32)
        ident = sb("ident", [P, P])
        iota = sb("iota", [P, P])
        below = sb("below", [P, P])
        pidx = sb("pidx", [P, 1])
        ones = sb("ones", [P, 1])
        ones_b = sb("ones_b", [P, 1], BF16)
        eps = sb("eps", [P, 1])
        zeros = sb("zeros", [P, ZR // ZP * W])
        trash_col = sb("trash_col", [P, 1])
        w1 = sb("w1", [P, 3, 2, P])
        w2 = sb("w2", [P, 3, P])
        wd = sb("wd", [P, 3, P])
        b1row = sb("b1row", [P, 3, P])
        b2col = sb("b2col", [P, 3])
        wr_t = sb("wr_t", [P, R, P])
        WORK = 10240
        work = sb("work", [P, WORK])

        class Area:
            def __init__(self, base, size):
                self.base, self.size, self.at = base, size, 0

            def cut(self, n, dt=F32, parts=P):
                words = n if dt != BF16 else n // 2
                ap = self.base[0:parts, self.at:self.at + words]
                self.at += words
                assert self.at <= self.size, self.at
                return ap if dt == F32 else ap.bitcast(dt)

        a = Area(agg, NBT * P)
        pad_vals = a.cut(2 * TAIL + 1, I32, 1)
        wr_raw = a.cut(R * P).rearrange("p (r j) -> p r j", r=R)
        last_i = a.cut(LC, I32)
        last_f = a.cut(LC)
        thr_row = a.cut(NBT)
        thr_col = a.cut(1, F32, NBT)
        jbase = a.cut(NQ)
        full = a.cut(LC * NBT).rearrange("p (c b) -> p c b", c=LC)
        cnt0 = a.cut(1, F32, NBT)
        win_at = a.cut(1, I32, NBT)
        win_i = a.cut(P, I32, NBT)
        win_f = a.cut(P, F32, NBT)
        cnt1 = a.cut(1, F32, NBT)
        start = a.cut(1, F32, NBT)
        step_mat = a.cut(P)
        upto_mat = a.cut(P)
        deg_b = a.cut(1, F32, NB)
        nt_i = a.cut(1, I32, NB)
        nt_f = a.cut(1, F32, NB)
        upto = a.cut(1, F32, NB)
        shift2 = a.cut(2, F32, NB)
        iota_j = a.cut(NTP, F32, NB)
        past = a.cut(NTP, F32, NB)
        blk_f = a.cut(NQ)
        blk_i = a.cut(NQ, I32)
        base_f = a.cut(NQ)
        from_f = a.cut(NQ)
        from_i = a.cut(NQ, I32)
        trash_row = a.cut(P)
        win_from = [a.cut(1, I32) for _ in range(2)]
        win_base = [a.cut(1) for _ in range(2)]
        dst_w = [a.cut(P + 2, I32) for _ in range(2)]
        src_w = [a.cut(P, I32) for _ in range(2)]
        typ_w = [a.cut(P, I32) for _ in range(2)]
        dst_f = a.cut(P + 2)
        src_f = a.cut(P)
        loc_f = a.cut(P)
        end_f = a.cut(P)
        key_f = a.cut(P)
        tmp_a = a.cut(P)
        tmp_b = a.cut(P)
        tmp_c = a.cut(P)
        loc_b = [a.cut(P, BF16) for _ in range(2)]
        cut_b = [a.cut(P, BF16) for _ in range(2)]
        key_o = [a.cut(P) for _ in range(2)]
        meta_o = [a.cut(P * 4, I32) for _ in range(2)]

        a = Area(work, WORK)
        xin = [a.cut(CB * P).rearrange("p (b f) -> p b f", f=P) for _ in range(2)]
        xs = a.cut(CB * P)
        afull = a.cut(CB * P)
        bout = a.cut(CB * P)
        bad = a.cut(CB * P, I32)
        st6 = a.cut(CB * 6).rearrange("p (b s) -> p b s", s=6)
        mv = a.cut(CB * 2).rearrange("p (b s) -> p b s", s=2)
        dev = a.cut(CB)
        inv_dev = a.cut(CB)

        a = Area(work, WORK)
        meta = [a.cut(GT * 4, I32).rearrange("p (t f) -> p t f", f=4) for _ in range(SL)]
        dst_bc = [a.cut(GT * P, BF16) for _ in range(SL)]
        cut_bc = [a.cut(GT * P, BF16) for _ in range(SL)]
        rows = [a.cut(GT * P).rearrange("p (t f) -> p t f", f=P) for _ in range(SL)]
        hot_t = [a.cut(GT * P, BF16) for _ in range(2)]
        h1 = [a.cut(GT * P) for _ in range(2)]
        h2 = [a.cut(GT * P) for _ in range(2)]
        scan = [a.cut(GT * P) for _ in range(2)]
        h2e = [a.cut(GT * P) for _ in range(2)]
        ends = [a.cut(GT * P).rearrange("p (t n) -> p t n", n=P) for _ in range(2)]

        a = Area(work, WORK)
        r_meta = [a.cut(GT * 4, I32).rearrange("p (t f) -> p t f", f=4) for _ in range(SL)]
        key_bc = [a.cut(GT * P) for _ in range(SL)]
        hot_e = [a.cut(GT * P, BF16).rearrange("p (t n) -> p t n", n=P) for _ in range(2)]
        same = [a.cut(GT * P, BF16).rearrange("p (t n) -> p t n", n=P) for _ in range(2)]
        earlier = a.cut(GT * P).rearrange("p (t n) -> p t n", n=P)
        rank = a.cut(GT)
        first = a.cut(GT)
        kept = a.cut(GT)
        spread = [a.cut(GT * P, BF16) for _ in range(2)]
        msg = [a.cut(GT * W).rearrange("p (t f) -> p t f", f=W) for _ in range(SL)]
        r_row = [a.cut(GT, I32) for _ in range(SL)]

        a = Area(tab_a[:, :].bitcast(F32), NBT * 3 * P // 2)
        part = [a.cut(K * R * W).rearrange("p (k w) -> p k w", k=K) for _ in range(2)]
        a = Area(work, WORK)
        x1_in = [a.cut(P) for _ in range(2)]
        scaled = [a.cut(R * P).rearrange("p (r f) -> p r f", r=R) for _ in range(2)]
        scaled_t = [a.cut(R * P) for _ in range(2)]
        cnt = a.cut(R)
        inv_cnt = a.cut(R)
        y_out = [a.cut(P) for _ in range(2)]
        y_in = a.cut(P)
        o_st6 = a.cut(6)
        o_mv = a.cut(2)
        o_dev = [a.cut(1) for _ in range(2)]
        o_inv = a.cut(1)

        s_pad = sem("s_pad")
        s_w = sem("s_w")
        s_last = sem("s_last")
        s_row0 = sem("s_row0")
        s_gp = sem("s_gp")
        s_pv = sem("s_pv")
        s_pt = sem("s_pt")
        s_blk = sem("s_blk")
        s_from = sem("s_from")
        s_win = [sem(f"s_win{k}") for k in range(2)]
        s_wv = sem("s_wv")
        s_wt = sem("s_wt")
        s_wo = sem("s_wo")
        s_store = [sem(f"s_store{k}") for k in range(2)]
        s_xin = [sem(f"s_xin{k}") for k in range(2)]
        s_xfree = sem("s_xfree")
        s_xt = sem("s_xt")
        s_xs = sem("s_xs")
        s_ta = sem("s_ta")
        s_tb = sem("s_tb")
        s_af = sem("s_af")
        s_hi = sem("s_hi")
        s_re = sem("s_re")
        s_mid = sem("s_mid")
        s_lo = sem("s_lo")
        s_bf = sem("s_bf")
        s_bd = sem("s_bd")
        s_tv = sem("s_tv")
        s_meta = [sem(f"s_meta{k}") for k in range(SL)]
        s_bc = [sem(f"s_bc{k}") for k in range(SL)]
        s_rows = [sem(f"s_rows{k}") for k in range(SL)]
        s_hot = sem("s_hot")
        s_p1 = sem("s_p1")
        s_h1 = sem("s_h1")
        s_p2 = sem("s_p2")
        s_h2 = sem("s_h2")
        s_scan = sem("s_scan")
        s_p3 = sem("s_p3")
        s_h2e = sem("s_h2e")
        s_ends = sem("s_ends")
        s_p4 = sem("s_p4")
        s_agg = sem("s_agg")
        s_zero = sem("s_zero")
        s_cred = sem("s_cred")
        s_ztab = sem("s_ztab")
        s_tick = {e: sem(f"s_tick_{e}") for e in ("pool", "dve", "act", "sp")}
        s_mt = sem("s_mt")
        s_y = sem("s_y")
        s_dev = sem("s_dev")
        s_x1 = sem("s_x1")
        s_x1d = sem("s_x1d")
        s_rl = [sem(f"s_rl{k}") for k in range(SL)]
        s_rh = sem("s_rh")
        s_rv = sem("s_rv")
        s_rid = sem("s_rid")
        s_ra = sem("s_ra")
        s_rs = sem("s_rs")
        s_rb = sem("s_rb")
        s_rm = sem("s_rm")
        s_add = [sem(f"s_add{k}") for k in range(K)]
        s_part = [sem(f"s_part{k}") for k in range(2)]
        s_23 = sem("s_23")
        s_fv = sem("s_fv")
        s_sc = sem("s_sc")
        s_ft = sem("s_ft")
        s_fa = sem("s_fa")
        s_fm = sem("s_fm")
        s_fy = sem("s_fy")
        s_fd = sem("s_fd")
        s_fo = sem("s_fo")
        s_out = [sem(f"s_out{k}") for k in range(2)]

        s_norm = sem("s_norm")

        GP_PAD, GP_ALL = 3, 9
        PV_CONST = 12
        PV_FULL = PV_CONST + 1 + LC
        PV_WIN0 = PV_FULL + 2
        PV_START = PV_WIN0 + 4
        PV_TILES = PV_START + 4
        PV_PAST = PV_TILES + 4
        PV_BLK = PV_PAST + 5
        WV, WVT = 16, 17
        NVC = 4
        NVR = 4
        NVM = NVB = 4
        NVN = 3

        class At:
            def __init__(self, i, k, d=0, first_group=0, first_pass=0):
                self.k = (k - d) % SL
                self.s = (k - d) % 2
                self.i = i + (k - d) // SL
                self.g = self.i * SL + self.k
                self.G = self.g + first_group
                self.n = self.i + first_pass

        def body_groups(i):
            return [(i, k) for k in range(SL)]

        block = ctx.enter_context(nc.Block())

        @block.sync
        def _(sp):
            tick = lambda: sp.sem_inc(s_tick["sp"], 1)
            sp.dma_start(dst_pad[1:1 + E], dst).then_inc(s_pad, 16)
            sp.dma_start(src_pad[0:E], src).then_inc(s_pad, 16)
            sp.dma_start(typ_pad[0:E], etype).then_inc(s_pad, 16)
            sp.wait_ge(s_gp, GP_PAD)
            as_row = lambda v: v.rearrange("(a n) -> a n", a=1)
            sp.dma_start(as_row(dst_pad[0:1]), pad_vals[:, 2 * TAIL:2 * TAIL + 1]).then_inc(s_pad, 16)
            sp.dma_start(as_row(dst_pad[1 + E:1 + E + TAIL]), pad_vals[:, 0:TAIL]).then_inc(s_pad, 16)
            sp.dma_start(as_row(src_pad[E:E + TAIL]), pad_vals[:, TAIL:2 * TAIL]).then_inc(s_pad, 16)
            sp.dma_start(as_row(typ_pad[E:E + TAIL]), pad_vals[:, TAIL:2 * TAIL]).then_inc(s_pad, 16)
            for l in range(3):
                W1, b1, W2, b2 = params[l]
                sp.dma_start(w1[:, l], W1.rearrange("(h i) o -> i h o", h=2)).then_inc(s_w, 16)
                sp.dma_start(w2[:, l], W2).then_inc(s_w, 16)
                sp.dma_start(b1row[:, l], as_row(b1).to_broadcast([P, P])).then_inc(s_w, 16)
                with nc.allow_non_contiguous_dma(reason="a bias as a column, once"):
                    sp.dma_start(b2col[:, l:l + 1], b2.rearrange("(n a) -> n a", a=1)).then_inc(s_w, 16)
            sp.dma_start(wr_raw, w_rel.rearrange("r i j -> i r j")).then_inc(s_w, 16)
            sp.wait_ge(s_pad, 7 * 16)
            with nc.allow_non_contiguous_dma(reason="the last edge of each row of 128, once"):
                sp.dma_start(last_i, dst_pad[P:P + ERP * P].rearrange("(p c e) -> p c e", c=LC, e=P)[:, :, 0]
                             ).then_inc(s_last, 16)
            sp.wait_ge(s_pv, PV_BLK)
            with nc.allow_non_contiguous_dma(reason="the tiles' blocks, once"):
                sp.dma_start(blk_row.rearrange("q p -> p q"), blk_i).then_inc(s_blk, 16)
            sp.wait_ge(s_blk, 16)
            sp.dma_start(blocks[:, :], blk_row.rearrange("q p -> (q p)").rearrange("(a n) -> a n", a=1)
                         ).then_inc(s_blk, 16)
            with sp.Fori(0, NQ // 2) as i:
                for s in range(2):
                    q = 2 * i + s
                    sp.wait_ge(s_wo, q + 1)
                    tick()
                    sp.dma_start(row_dst[bass.ds(q * P, P), :], loc_b[s]).then_inc(s_store[s], 16)
                    sp.dma_start(row_cut[bass.ds(q * P, P), :], cut_b[s]).then_inc(s_store[s], 16)
                    sp.dma_start(row_key[bass.ds(q * P, P), :], key_o[s]).then_inc(s_store[s], 16)
                    sp.dma_start(col_meta[:, bass.ds(q * P, P), :].rearrange("p j f -> p (j f)"),
                                 meta_o[s]).then_inc(s_store[s], 16)

            def x_chunk(i, s, whole=True):
                c = 2 * i + s
                sp.wait_ge(s_xfree, c + 1)
                tick()
                if whole:
                    sp.dma_start(xin[s], x[bass.ds(c * CB * P, CB * P), :].rearrange("(b p) f -> p b f", p=P)
                                 ).then_inc(s_xin[s], 16)
                else:
                    c0 = (NC - 1) * CB * P
                    sp.dma_start(xin[s][:, 0:CB - 1, :],
                                 x[c0:c0 + (CB - 1) * P, :].rearrange("(b p) f -> p b f", p=P)
                                 ).then_inc(s_xin[s], 16)
                    sp.dma_start(xin[s][0:LAST, CB - 1, :], x[c0 + (CB - 1) * P:N, :]).then_inc(s_xin[s], 16)

            def store_b(l, c):
                sp.wait_ge(s_bf, l * NC + c + 1)
                tick()
                sp.dma_start(tab_b[bass.ds(c * CB * P, CB * P), :].rearrange("(b p) f -> p b f", p=P),
                             bout.rearrange("p (b f) -> p b f", f=P)).then_inc(s_bd, 16)

            for l in range(3):
                if l == 0:
                    x_chunk(0, 0)
                    with sp.Fori(0, NC // 2 - 1) as i:
                        x_chunk(i, 1)
                        store_b(0, 2 * i)
                        x_chunk(i + 1, 0)
                        store_b(0, 2 * i + 1)
                    x_chunk(NC // 2 - 1, 1, whole=False)
                    store_b(0, NC - 2)
                    store_b(0, NC - 1)
                else:
                    with sp.Fori(0, NC) as c:
                        store_b(l, c)
                sp.wait_ge(s_lo, NC * (l + 1))
                sp.wait_ge(s_bd, 16 * NC * (l + 1))
                if l == 0:
                    for s in range(2):
                        sp.wait_ge(s_store[s], 64 * (NQ // 2))
                with sp.Fori(0, NI) as i:
                    for _, k in body_groups(i):
                        at = At(i, k, 0, l * NG, l * NI)
                        sp.wait_ge(s_ends, at.G + 1)
                        tick()
                        sp.dma_start(meta[k], col_meta[:, bass.ds(at.g * GT, GT), :]).then_inc(s_meta[k], 16)
                        sp.dma_start(dst_bc[k], row_dst[bass.ds(at.g * GT, GT), :].rearrange("t e -> (t e)")
                                     .partition_broadcast(P)).then_inc(s_bc[k], 16)
                        sp.dma_start(cut_bc[k], row_cut[bass.ds(at.g * GT, GT), :].rearrange("t e -> (t e)")
                                     .partition_broadcast(P)).then_inc(s_bc[k], 16)
            sp.wait_ge(s_agg, GT * NG * 3 + GT)
            base = NC

            def x_again(i, s, whole=True):
                c = 2 * i + s
                sp.wait_ge(s_xfree, base + c + 1)
                tick()
                if whole:
                    sp.dma_start(xin[s], x[bass.ds(c * CB * P, CB * P), :].rearrange("(b p) f -> p b f", p=P)
                                 ).then_inc(s_xin[s], 16)
                else:
                    c0 = (NC - 1) * CB * P
                    sp.dma_start(xin[s][:, 0:CB - 1, :],
                                 x[c0:c0 + (CB - 1) * P, :].rearrange("(b p) f -> p b f", p=P)
                                 ).then_inc(s_xin[s], 16)
                    sp.dma_start(xin[s][0:LAST, CB - 1, :], x[c0 + (CB - 1) * P:N, :]).then_inc(s_xin[s], 16)

            def store_x1(c):
                sp.wait_ge(s_x1, c + 1)
                tick()
                sp.dma_start(x1_dram[bass.ds(c * CB * P, CB * P), :].rearrange("(b p) f -> p b f", p=P),
                             bout.rearrange("p (b f) -> p b f", f=P)).then_inc(s_x1d, 16)

            x_again(0, 0)
            with sp.Fori(0, NC // 2 - 1) as i:
                x_again(i, 1)
                store_x1(2 * i)
                x_again(i + 1, 0)
                store_x1(2 * i + 1)
            x_again(NC // 2 - 1, 1, whole=False)
            store_x1(NC - 2)
            store_x1(NC - 1)
            sp.wait_ge(s_lo, NC * 4)
            sp.wait_ge(s_x1d, 16 * NC)
            with sp.Fori(0, NI) as i:
                for _, k in body_groups(i):
                    at = At(i, k)
                    sp.wait_ge(s_rid, at.g + 1)
                    tick()
                    sp.dma_start(r_meta[k], col_meta[:, bass.ds(at.g * GT, GT), :]).then_inc(s_rl[k], 16)
                    sp.dma_start(key_bc[k], row_key[bass.ds(at.g * GT, GT), :].rearrange("t e -> (t e)")
                                 .partition_broadcast(P)).then_inc(s_rl[k], 16)
            for t in range(K):
                sp.wait_ge(s_add[t], 16 * NG)

            def load_block(b, s):
                sp.wait_ge(s_sc, b + 1)
                sp.wait_ge(s_fo, b + 1)
                tick()
                for k in range(K):
                    view = rel_tab[k][0:R * N, :].rearrange("(r n) w -> n r w", r=R)
                    rows_b = P if isinstance(b, int) is False or b < NB - 1 else LAST
                    if rows_b == P:
                        blk = view[bass.ds(b * P, P), :, :]
                    else:
                        blk = view[b * P:N, :, :]
                    sp.dma_start(part[s][0:rows_b, k, :].rearrange("p (r w) -> p r w", r=R), blk
                                 ).then_inc(s_part[s], 16)
                sp.dma_start(x1_in[s], x1_dram[bass.ds(b * P, P), :]).then_inc(s_part[s], 16)

            def store_out(b, s):
                sp.wait_ge(s_fo, b + 3)
                tick()
                if isinstance(b, int) and b == NB - 1:
                    sp.dma_start(out[b * P:N, :], y_out[s][0:LAST, :]).then_inc(s_out[s], 16)
                else:
                    sp.dma_start(out[bass.ds(b * P, P), :], y_out[s]).then_inc(s_out[s], 16)

            load_block(0, 0)
            load_block(1, 1)
            with sp.Fori(0, NB // 2 - 2) as i:
                for s in range(2):
                    store_out(2 * i + s, s)
                    load_block(2 * i + s + 2, s)
            for b in range(NB - 4, NB - 2):
                store_out(b, b % 2)
                load_block(b + 2, b % 2)
            store_out(NB - 2, 0)
            store_out(NB - 1, 1)
            for s in range(2):
                sp.wait_ge(s_out[s], 16 * (NB // 2))

        @block.gpsimd
        def _(pool):
            g = nc.gpsimd
            tick = lambda: pool.sem_inc(s_tick["pool"], 1)
            g.memset(pad_vals[:, 0:TAIL], NO_BLOCK).then_inc(s_gp, 1)
            g.memset(pad_vals[:, TAIL:2 * TAIL], 0).then_inc(s_gp, 1)
            g.memset(pad_vals[:, 2 * TAIL:2 * TAIL + 1], -1).then_inc(s_gp, 1)
            exact = dict(allow_small_or_imprecise_dtypes=True)
            g.iota(iota[:, :], [[1, P]], base=0, channel_multiplier=0, **exact).then_inc(s_gp, 1)
            g.iota(pidx[:, :], [[0, 1]], base=0, channel_multiplier=1, **exact).then_inc(s_gp, 1)
            g.iota(thr_row, [[P, NBT]], base=0, channel_multiplier=0, **exact).then_inc(s_gp, 1)
            g.iota(thr_col, [[0, 1]], base=0, channel_multiplier=P, **exact).then_inc(s_gp, 1)
            g.iota(jbase, [[P * P, NQ]], base=0, channel_multiplier=P, **exact).then_inc(s_gp, 1)
            g.iota(iota_j, [[1, NTP]], base=0, channel_multiplier=0, **exact).then_inc(s_gp, 1)
            as_elements = lambda v: v.rearrange("(a n) -> a n", a=1)
            pool.wait_ge(s_pad, 7 * 16)
            pool.wait_ge(s_pv, PV_WIN0)
            g.indirect_dma_start(win_i, None, as_elements(dst_pad),
                                 bass.IndirectOffsetOnAxis(ap=win_at, axis=1)).then_inc(s_row0, 16)
            with pool.Fori(0, NQ // 2) as i:
                for s in range(2):
                    q = 2 * i + s
                    pool.wait_ge(s_from, q + 1)
                    tick()
                    for to, of in ((dst_w[s], dst_pad), (src_w[s], src_pad), (typ_w[s], typ_pad)):
                        g.indirect_dma_start(to, None, as_elements(of),
                                             bass.IndirectOffsetOnAxis(ap=win_from[s], axis=1)
                                             ).then_inc(s_win[s], 16)
            for l in range(3):
                pool.wait_ge(s_bd, 16 * NC * (l + 1))
                pool.wait_ge(s_lo, NC * (l + 1))
                with pool.Fori(0, NI) as i:
                    for _, k in body_groups(i):
                        at = At(i, k, 0, l * NG, l * NI)
                        pool.wait_ge(s_meta[k], 16 * (at.n + 1))
                        tick()
                        pool.wait_ge(s_p1, at.G + 1)
                        tick()
                        for t in range(GT):
                            g.indirect_dma_start(rows[k][:, t, :], None, tab_b,
                                                 bass.IndirectOffsetOnAxis(ap=meta[k][:, t, 0:1], axis=0)
                                                 ).then_inc(s_rows[k], 16)
            pool.wait_ge(s_ztab, 16 * K * NI)

            def add_group(i, k, at_start):
                at = At(i, k)
                pool.wait_ge(s_rid, at.g + SL + 1)
                tick()
                pool.wait_ge(s_rm, at.g + 3)
                tick()
                for t in range(GT):
                    if not (at_start and k == 0):
                        pool.wait_ge(s_add[t], 16 * at.g)
                        tick()
                    g.indirect_dma_start(rel_tab[t], bass.IndirectOffsetOnAxis(ap=r_row[k][:, t:t + 1], axis=0),
                                         msg[k][:, t, :], None, compute_op=ALU.add).then_inc(s_add[t], 16)

            for k in range(SL):
                add_group(0, k, True)
            with pool.Fori(1, NI) as i:
                for _, k in body_groups(i):
                    add_group(i, k, False)
            with pool.Fori(0, NB // 2) as i:
                for s in range(2):
                    b = 2 * i + s
                    pool.wait_ge(s_part[s], 16 * (K + 1) * (i + 1))
                    g.tensor_tensor(part[s][:, 2, :], part[s][:, 2, :], part[s][:, 3, :], ALU.add).then_inc(s_23, 1)

        @block.tensor
        def _(pe):
            mm, tr = pe.matmul, pe.transpose
            pe.wait_ge(s_pv, PV_FULL)
            for c in range(LC):
                last = mm(ps[0:NBT, 0, 0:1], full[:, c, :], ones[:, :], start=(c == 0), stop=(c == LC - 1))
            last.then_inc(s_pt, 1)
            pe.wait_ge(s_pv, PV_START)
            mm(ps[0:NB, 1, 0:1], step_mat[0:NBT, 0:NB], start, start=True, stop=True).then_inc(s_pt, 1)
            pe.wait_ge(s_pv, PV_TILES)
            mm(ps[0:NB, 2, 0:1], upto_mat[0:NB, 0:NB], nt_f, start=True, stop=True).then_inc(s_pt, 1)
            pe.wait_ge(s_pv, PV_PAST)
            for q in range(NQ):
                last = mm(ps[:, 3, 2 * q:2 * q + 2], past[:, q * P:(q + 1) * P], shift2, start=True, stop=True)
            last.then_inc(s_pt, 1)
            pe.wait_ge(s_w, 13 * 16)
            for r in range(R):
                last = tr(flat[:, 2048 + r * P:2048 + (r + 1) * P], wr_raw[:, r, :], ident[:, :])
            last.then_inc(s_pt, 1)
            with pe.Fori(0, NQ // 2) as i:
                for s in range(2):
                    q = 2 * i + s
                    pe.wait_ge(s_wv, q * WVT + WV)
                    for f, v in enumerate((src_f, end_f, loc_f, key_f)):
                        last = tr(ps[:, 6 + s, f * P:(f + 1) * P], v, ident[:, :])
                    last.then_inc(s_wt, 1)

            def products(l, c):
                cc = l * NC + c
                pe.wait_ge(s_xs, cc + 1)
                pe.wait_ge(s_af, cc + 1)
                for b in range(CB):
                    last = mm(flat[:, b * P:(b + 1) * P], xs[:, b * P:(b + 1) * P], wd[:, l], start=True, stop=True)
                last.then_inc(s_ta, 1)
                pe.wait_ge(s_bf, cc)
                for b in range(CB):
                    last = mm(flat[:, 1024 + b * P:1024 + (b + 1) * P], xs[:, b * P:(b + 1) * P], w1[:, l, 1],
                              start=True, stop=True)
                last.then_inc(s_tb, 1)

            def turn_x(i, s, extra=0):
                pe.wait_ge(s_xin[s], 16 * (i + 1) + extra)
                pe.wait_ge(s_xs, 2 * i + s)
                for b in range(CB):
                    last = tr(flat[:, 3072 + b * P:3072 + (b + 1) * P], xin[s][:, b, :], ident[:, :])
                last.then_inc(s_xt, 1)

            def turn_y(c):
                pe.wait_ge(s_xs, 3 * NC + c + 1)

                for b in range(CB):
                    last = tr(flat[:, b * P:(b + 1) * P], xs[:, b * P:(b + 1) * P], ident[:, :])
                last.then_inc(s_mt, 1)

            def step(l, i, k, lo=False, hi=False):
                live = lambda d: not ((lo and k < d) or (hi and k >= d))
                if live(0):
                    at = At(i, k, 0, l * NG, l * NI)
                    _, blk = nc.values_load_multi_w_load_instructions(
                        blocks[0:1, bass.ds(at.g * GT, GT)], engines=[PE_ENGINE], min_val=0, max_val=NB,
                        skip_runtime_bounds_check_because=WHY)
                    pe.wait_ge(s_hot, at.G + 1)
                    pe.wait_ge(s_h1, at.G + 1)
                    pe.wait_ge(s_rows[at.k], 64 * (at.n + 1))
                    for t in range(GT):
                        to = ps[:, at.s, t * P:(t + 1) * P]
                        for h in range(3):
                            mm(to, tab_a[:, bass.ds(blk[t] * (3 * P) + h * P, P)], hot_t[at.s][:, t * P:(t + 1) * P],
                               start=(h == 0), stop=False)
                        last = mm(to, rows[at.k][:, t, :], ident[:, :], start=False, stop=True)
                    last.then_inc(s_p1, 1)
                if live(1):
                    at = At(i, k, 1, l * NG)
                    pe.wait_ge(s_h1, at.G + 3)
                    pe.wait_ge(s_h2, at.G + 1)
                    mm(ps[:, 2 + at.s, :], w2[:, l], h1[at.s], start=True, stop=True).then_inc(s_p2, 1)
                if live(2):
                    at = At(i, k, 2, l * NG)
                    pe.wait_ge(s_scan, at.G + 3)
                    pe.wait_ge(s_h2e, at.G + 1)
                    for t in range(GT):
                        last = tr(ps[:, 4 + at.s, t * P:(t + 1) * P], scan[at.s][:, t * P:(t + 1) * P], ident[:, :])
                    last.then_inc(s_p3, 1)
                if live(3):
                    at = At(i, k, 3, l * NG)
                    pe.wait_ge(s_h2e, at.G + 3)
                    pe.wait_ge(s_ends, at.G + SL + 1)
                    pe.wait_ge(s_agg, GT * at.G)
                    for t in range(GT):
                        last = mm(ps[:, 6 + at.s, t * P:(t + 1) * P], h2e[at.s][:, t * P:(t + 1) * P],
                                  ends[at.s][:, t, :], start=True, stop=True)
                    last.then_inc(s_p4, 1)

            pe.sem_inc(s_xfree, 2)
            pe.sem_inc(s_p1, SL)
            for q in (s_p2, s_p3, s_p4):
                pe.sem_inc(q, 2)
            for l in range(3):
                if l == 0:
                    with pe.Fori(0, NC // 2 - 1) as i:
                        for s in range(2):
                            turn_x(i, s)
                            products(0, 2 * i + s)
                    turn_x(NC // 2 - 1, 0)
                    products(0, NC - 2)
                    turn_x(NC // 2 - 1, 1, extra=16)
                    products(0, NC - 1)
                    pe.wait_ge(s_blk, 32)
                else:
                    with pe.Fori(0, NC) as c:
                        products(l, c)
                pe.wait_ge(s_lo, NC * (l + 1))
                for k in range(SL):
                    step(l, 0, k, lo=True)
                with pe.Fori(1, NI) as i:
                    for _, k in body_groups(i):
                        step(l, i, k)
                for k in range(SL - 1):
                    step(l, NI, k, hi=True)
            with pe.Fori(0, NC) as c:
                turn_y(c)
            pe.wait_ge(s_lo, NC * 4)

            def rel_step(i, k, lo=False, hi=False):
                live = lambda d: not ((lo and k < d) or (hi and k >= d))
                if live(0):
                    at = At(i, k)
                    pe.wait_ge(s_rh, at.g + 3)
                    pe.wait_ge(s_rs, at.g + 1)
                    for t in range(GT):
                        last = mm(ps[:, at.s, t * P:(t + 1) * P], hot_e[at.s][:, t, :], same[at.s][:, t, :],
                                  start=True, stop=True)
                    last.then_inc(s_ra, 1)
                if live(1):
                    at = At(i, k, 1)
                    _, blk = nc.values_load_multi_w_load_instructions(
                        blocks[0:1, bass.ds(at.g * GT, GT)], engines=[PE_ENGINE], min_val=0, max_val=NB,
                        skip_runtime_bounds_check_because=WHY)
                    pe.wait_ge(s_rs, at.g + 3)
                    pe.wait_ge(s_rm, at.g + 1)
                    for t in range(GT):
                        by = spread[at.s][:, t * P:(t + 1) * P]
                        for h in range(3):
                            mm(ps[:, 2 + at.s, t * P:(t + 1) * P], by,
                               tab_a[:, bass.ds(blk[t] * (3 * P) + h * P, P)], start=(h == 0), stop=(h == 2))
                        last = mm(ps[:, 4 + at.s, t:t + 1], by, ones_b[:, :], start=True, stop=True)
                    last.then_inc(s_rb, 1)

            for q in (s_ra, s_rb):
                pe.sem_inc(q, 2)
            for k in range(SL):
                rel_step(0, k, lo=True)
            with pe.Fori(1, NI) as i:
                for _, k in body_groups(i):
                    rel_step(i, k)
            rel_step(NI, 0, hi=True)
            for q in (s_ft, s_fm):
                pe.sem_inc(q, 2)

            def turn_block(b, s):
                pe.wait_ge(s_sc, b + 3)
                pe.wait_ge(s_fa, b + 1)
                for r in range(R):
                    last = tr(flat[:, s * 1024 + r * P:s * 1024 + (r + 1) * P], scaled[s][:, r, :], ident[:, :])
                last.then_inc(s_ft, 1)

            def relate_block(b, s):
                pe.wait_ge(s_fa, b + 3)
                pe.wait_ge(s_fo, b + 1)
                for r in range(R):
                    last = mm(ps[:, 4 + s, 0:P], scaled_t[s][:, r * P:(r + 1) * P], wr_t[:, r, :],
                              start=(r == 0), stop=(r == R - 1))
                last.then_inc(s_fm, 1)

            turn_block(0, 0)
            with pe.Fori(0, NB // 2 - 1) as i:
                turn_block(2 * i + 1, 1)
                relate_block(2 * i, 0)
                turn_block(2 * i + 2, 0)
                relate_block(2 * i + 1, 1)
            turn_block(NB - 1, 1)
            relate_block(NB - 2, 0)
            relate_block(NB - 1, 1)

        @block.scalar
        def _(act):
            tick = lambda: act.sem_inc(s_tick["act"], 1)
            a_ = nc.scalar.activation

            def part_view(c, h):
                return tab_a[:, bass.ds(c * (CB * 3 * P), CB * 3 * P)].rearrange(
                    "p (b t f) -> p b t f", t=3, f=P)[:, :, h, :]

            def b_chunk(l, c):
                act.wait_ge(s_tb, l * NC + c + 1)
                act.wait_ge(s_bd, 16 * (l * NC + c))
                tick()
                a_(bout, flat[:, 1024:1024 + CB * P], ACT.Copy).then_inc(s_bf, 1)

            def parts(cc, c):
                act.wait_ge(s_af, cc + 2)
                tick()
                a_(part_view(c, 0), afull.rearrange("p (b f) -> p b f", f=P), ACT.Copy).then_inc(s_hi, 1)
                act.wait_ge(s_re, cc + 1)
                tick()
                a_(part_view(c, 1), afull.rearrange("p (b f) -> p b f", f=P), ACT.Copy).then_inc(s_mid, 1)

            def step(l, i, k, lo=False, hi=False):
                live = lambda d: not ((lo and k < d) or (hi and k >= d))
                if live(0):
                    at = At(i, k, 0, l * NG)
                    act.wait_ge(s_p1, at.G + SL + 1)
                    act.wait_ge(s_p2, at.G + 1)
                    a_(h1[at.s], ps[:, at.s, :], ACT.Relu).then_inc(s_h1, 1)
                if live(1):
                    at = At(i, k, 1, l * NG)
                    act.wait_ge(s_p2, at.G + 3)
                    act.wait_ge(s_scan, at.G + 1)
                    a_(h2[at.s], ps[:, 2 + at.s, :], ACT.Identity, bias=b2col[:, l:l + 1]).then_inc(s_h2, 1)
                if live(2):
                    at = At(i, k, 2, l * NG)
                    act.wait_ge(s_p3, at.G + 3)
                    act.wait_ge(s_p4, at.G + 1)
                    a_(h2e[at.s], ps[:, 4 + at.s, :], ACT.Copy).then_inc(s_h2e, 1)

            def clear(l, i):
                if l < 2:
                    for t in (2 * l, 2 * l + 1):
                        act.dma_start(rel_tab[t][bass.ds(i * ZR, ZR), :].rearrange("(p r) w -> p (r w)", p=ZP),
                                      zeros[0:ZP, :]).then_inc(s_ztab, 16)

            for q in (s_h1, s_h2, s_h2e):
                act.sem_inc(q, 2)
            for l in range(3):
                with act.Fori(0, NC) as c:
                    b_chunk(l, c)
                    parts(l * NC + c, c)
                if l == 0:
                    act.wait_ge(s_pv, PV_CONST)
                    act.wait_ge(s_w, 13 * 16)
                for k in range(SL):
                    step(l, 0, k, lo=True)
                clear(l, 0)
                with act.Fori(1, NI) as i:
                    for _, k in body_groups(i):
                        step(l, i, k)
                    clear(l, i)
                for k in range(SL - 1):
                    step(l, NI, k, hi=True)

            with act.Fori(0, NC) as c:
                act.wait_ge(s_y, c + 1)
                a_(dev, mv[:, :, 1], ACT.Sqrt, bias=eps[:, :]).then_inc(s_dev, 1)
                parts(3 * NC + c, c)
            for q in (s_rs, s_rm):
                act.sem_inc(q, 2)

            def rel_step(i, k, lo=False, hi=False):
                live = lambda d: not ((lo and k < d) or (hi and k >= d))
                if live(0):
                    at = At(i, k)
                    act.wait_ge(s_ra, at.g + 3)
                    act.wait_ge(s_rb, at.g + 1)
                    a_(spread[at.s], ps[:, at.s, :], ACT.Copy).then_inc(s_rs, 1)
                if live(1):
                    at = At(i, k, 1)
                    act.wait_ge(s_rb, at.g + 3)
                    if not lo:
                        for t in range(GT):
                            if hi or k > 0:
                                act.wait_ge(s_add[t], 16 * (at.g - SL + 1))
                                tick()
                    a_(msg[at.k][:, :, 0:P], ps[:, 2 + at.s, :].rearrange("p (t f) -> p t f", f=P), ACT.Copy)
                    a_(msg[at.k][:, :, P], ps[:, 4 + at.s, 0:GT], ACT.Copy).then_inc(s_rm, 1)

            def rel_first(i, k):
                pass

            for k in range(SL):
                rel_step(0, k, lo=True)
            at0 = At(1, 0)
            act.wait_ge(s_ra, at0.g + 3)
            act.wait_ge(s_rb, at0.g + 1)
            a_(spread[0], ps[:, 0, :], ACT.Copy).then_inc(s_rs, 1)
            at1 = At(1, 0, 1)
            act.wait_ge(s_rb, at1.g + 3)
            a_(msg[at1.k][:, :, 0:P], ps[:, 2 + at1.s, :].rearrange("p (t f) -> p t f", f=P), ACT.Copy)
            a_(msg[at1.k][:, :, P], ps[:, 4 + at1.s, 0:GT], ACT.Copy).then_inc(s_rm, 1)
            for k in range(1, SL):
                rel_step(1, k)
            with act.Fori(2, NI) as i:
                for _, k in body_groups(i):
                    at = At(i, k)
                    act.wait_ge(s_ra, at.g + 3)
                    act.wait_ge(s_rb, at.g + 1)
                    a_(spread[at.s], ps[:, at.s, :], ACT.Copy).then_inc(s_rs, 1)
                    at = At(i, k, 1)
                    for t in range(GT):
                        act.wait_ge(s_add[t], 16 * (at.g - SL + 1))
                        tick()
                    act.wait_ge(s_rb, at.g + 3)
                    a_(msg[at.k][:, :, 0:P], ps[:, 2 + at.s, :].rearrange("p (t f) -> p t f", f=P), ACT.Copy)
                    a_(msg[at.k][:, :, P], ps[:, 4 + at.s, 0:GT], ACT.Copy).then_inc(s_rm, 1)
            rel_step(NI, 0, hi=True)
            act.sem_inc(s_fa, 2)

            def turned(b, s):
                act.wait_ge(s_ft, b + 3)
                act.wait_ge(s_fm, b + 1)
                a_(scaled_t[s], flat[:, s * 1024:(s + 1) * 1024], ACT.Copy).then_inc(s_fa, 1)

            def root(b, s):
                act.wait_ge(s_fy, b + 1)
                a_(o_dev[s], o_mv[:, 1:2], ACT.Sqrt, bias=eps[:, :]).then_inc(s_fd, 1)

            turned(0, 0)
            with act.Fori(0, NB // 2 - 1) as i:
                turned(2 * i + 1, 1)
                root(2 * i, 0)
                turned(2 * i + 2, 0)
                root(2 * i + 1, 1)
            turned(NB - 1, 1)
            root(NB - 2, 0)
            root(NB - 1, 1)

        @block.vector
        def _(dve):
            v = nc.vector
            tick = lambda: dve.sem_inc(s_tick["dve"], 1)
            done = [0]

            def pv(ins):
                done[0] += 1
                ins.then_inc(s_pv, 1)
                dve.wait_ge(s_pv, done[0])
                return done[0]

            dve.wait_ge(s_gp, GP_ALL)
            pv(v.tensor_scalar(ident[:, :], iota[:, :], pidx[:, 0:1], None, ALU.is_equal))
            pv(v.tensor_scalar(below[:, :], iota[:, :], pidx[:, 0:1], None, ALU.is_lt))
            pv(v.tensor_scalar(upto_mat, iota[:, :], pidx[:, 0:1], None, ALU.is_ge))
            pv(v.tensor_scalar(tmp_a, iota[:, :], 1.0, pidx[:, 0:1], ALU.add, ALU.is_equal))
            pv(v.tensor_tensor(step_mat, tmp_a, ident[:, :], ALU.subtract))
            pv(v.memset(ones[:, :], 1.0))
            pv(v.memset(ones_b[:, :], 1.0))
            pv(v.memset(eps[:, :], EPS))
            pv(v.memset(zeros[:, :], 0.0))
            pv(v.tensor_scalar(trash_col[:, :], pidx[:, :], float(TRASH), None, ALU.add))
            pv(v.tensor_scalar(trash_row, iota[:, :], float(TRASH), None, ALU.add))
            assert pv(v.memset(tab_a[:, NB * 3 * P:], 0.0)) == PV_CONST
            dve.wait_ge(s_last, 16)
            pv(v.tensor_copy(last_f, last_i))
            for c in range(LC):
                n = pv(v.tensor_scalar(full[:, c, :], thr_row, last_f[:, c:c + 1], None, ALU.is_gt))
            assert n == PV_FULL
            dve.wait_ge(s_pt, 1)
            pv(v.tensor_copy(cnt0, ps[0:NBT, 0, 0:1]))
            assert pv(v.tensor_scalar(win_at, cnt0, float(P), 1.0, ALU.mult, ALU.add)) == PV_WIN0
            dve.wait_ge(s_row0, 16)
            pv(v.tensor_copy(win_f, win_i))
            pv(v.tensor_scalar(win_f, win_f, thr_col, None, ALU.is_lt))
            pv(v.tensor_reduce(cnt1, win_f, AX_X, ALU.add))
            assert pv(v.scalar_tensor_tensor(out=start, in0=cnt0, scalar=float(P), in1=cnt1,
                                             op0=ALU.mult, op1=ALU.add)) == PV_START
            dve.wait_ge(s_pt, 2)
            pv(v.tensor_copy(deg_b, ps[0:NB, 1, 0:1]))
            pv(v.tensor_scalar(nt_i, deg_b, float(P - 1), None, ALU.add))
            pv(v.tensor_scalar(nt_i, nt_i, 7, None, ALU.arith_shift_right))
            assert pv(v.tensor_copy(nt_f, nt_i)) == PV_TILES
            dve.wait_ge(s_pt, 3)
            pv(v.tensor_copy(upto, ps[0:NB, 2, 0:1]))
            pv(v.memset(shift2[:, 0:1], 1.0))
            pv(v.scalar_tensor_tensor(out=shift2[:, 1:2], in0=nt_f, scalar=-float(P), in1=deg_b,
                                      op0=ALU.mult, op1=ALU.add))
            assert pv(v.tensor_scalar(past, iota_j, upto, None, ALU.is_ge)) == PV_PAST
            dve.wait_ge(s_pt, 4)
            found = ps[:, 3, 0:2 * NQ].rearrange("p (q f) -> p q f", f=2)
            pv(v.tensor_copy(blk_f, found[:, :, 0]))
            pv(v.tensor_scalar(base_f, blk_f, float(P), None, ALU.mult))
            pv(v.tensor_tensor(from_f, found[:, :, 1], jbase, ALU.add))
            pv(v.tensor_scalar(from_i, from_f, float(E), None, ALU.min))
            assert pv(v.tensor_copy(blk_i, blk_f)) == PV_BLK
            dve.wait_ge(s_w, 13 * 16)
            for l in range(3):
                pv(v.tensor_tensor(wd[:, l], w1[:, l, 0], w1[:, l, 1], ALU.subtract))
            dve.wait_ge(s_pt, 5)
            pv(v.tensor_copy(wr_t[:, :, :].rearrange("p r j -> p (r j)"), flat[:, 2048:2048 + R * P]))
            with dve.Fori(0, NQ // 2) as i:
                for s in range(2):
                    q = 2 * i + s
                    n = [0]

                    def ch(ins):
                        n[0] += 1
                        ins.then_inc(s_wv, 1)
                        dve.wait_ge(s_wv, q * WVT + n[0])

                    ch(v.tensor_copy(win_base[s], base_f[:, bass.ds(q, 1)]))
                    v.tensor_copy(win_from[s], from_i[:, bass.ds(q, 1)]).then_inc(s_from, 1)
                    dve.wait_ge(s_store[s], 64 * i)
                    tick()
                    dve.wait_ge(s_win[s], 48 * (i + 1))
                    tick()
                    ch(v.tensor_copy(dst_f, dst_w[s]))
                    ch(v.tensor_copy(src_f, src_w[s]))
                    ch(v.tensor_scalar(loc_f, dst_f[:, 1:P + 1], win_base[s], float(OUT_OF_BLOCK),
                                       ALU.subtract, ALU.min))
                    ch(v.tensor_tensor(tmp_a, dst_f[:, 1:P + 1], dst_f[:, 0:P], ALU.not_equal))
                    ch(v.tensor_scalar(tmp_b, tmp_a, -2.0, 1.0, ALU.mult, ALU.add))
                    ch(v.tensor_scalar(cut_b[s], tmp_b, BIG, None, ALU.mult))
                    ch(v.tensor_tensor(tmp_a, dst_f[:, 1:P + 1], dst_f[:, 2:P + 2], ALU.not_equal))
                    ch(v.tensor_scalar(tmp_b, tmp_a, -float(OUT_OF_BLOCK), float(OUT_OF_BLOCK), ALU.mult, ALU.add))
                    ch(v.tensor_tensor(end_f, tmp_b, loc_f, ALU.max))
                    ch(v.tensor_copy(loc_b[s], loc_f))
                    ch(v.scalar_tensor_tensor(out=tmp_a, in0=typ_w[s], scalar=float(N), in1=src_f,
                                              op0=ALU.mult, op1=ALU.add))
                    ch(v.tensor_tensor(tmp_b, tmp_a, trash_row, ALU.subtract))
                    ch(v.scalar_tensor_tensor(out=tmp_c, in0=loc_f, scalar=float(P), in1=tmp_b,
                                              op0=ALU.is_lt, op1=ALU.mult))
                    ch(v.tensor_tensor(key_f, tmp_c, trash_row, ALU.add))
                    ch(v.tensor_copy(key_o[s], key_f))
                    assert n[0] == WV
                    dve.wait_ge(s_wt, q + 1)
                    tick()
                    mo = meta_o[s].rearrange("p (j f) -> p j f", f=4)
                    ch(v.tensor_copy(mo[:, :, 0], ps[:, 6 + s, 0:P]))
                    v.tensor_copy(meta_o[s].bitcast(F32).rearrange("p (j f) -> p f j", f=4)[:, 1:4, :],
                                  ps[:, 6 + s, P:4 * P].rearrange("p (f j) -> p f j", f=3)).then_inc(s_wo, 1)
                    assert n[0] == WVT
            for s in range(2):
                dve.wait_ge(s_store[s], 64 * (NQ // 2))
            dve.wait_ge(s_blk, 32)
            dve.sem_inc(s_scan, 2)
            dve.sem_inc(s_ends, SL)
            dve.sem_inc(s_agg, GT)
            dve.sem_inc(s_af, 1)
            zdone = [0]

            def part_view(c, h):
                return tab_a[:, bass.ds(c * (CB * 3 * P), CB * 3 * P)].rearrange(
                    "p (b t f) -> p b t f", t=3, f=P)[:, :, h, :]

            blocked = lambda ap: ap.rearrange("p (b f) -> p b f", f=P)
            tv = [0]

            def guard(c, count, relu):
                def ch(ins, m):
                    ins.then_inc(s_tv, 1)
                    dve.wait_ge(s_tv, count + m)
                    tick()
                if relu:
                    ch(v.tensor_scalar(xs, agg[:, bass.ds(c * CB * P, CB * P)], 0.0, None, ALU.max), 1)
                else:
                    ch(v.tensor_copy(xs, agg[:, bass.ds(c * CB * P, CB * P)]), 1)
                ch(v.tensor_scalar(bad, xs, 0.0, 0.0, ALU.mult, ALU.not_equal), 2)
                v.copy_predicated(xs, bad, zeros[:, 0:CB * P]).then_inc(s_xs, 1)

            def lower_parts(cc, c):
                dve.wait_ge(s_hi, cc + 1)
                tick()
                v.tensor_tensor(blocked(afull), blocked(afull), part_view(c, 0), ALU.subtract).then_inc(s_re, 1)
                dve.wait_ge(s_mid, cc + 1)
                tick()
                v.tensor_tensor(part_view(c, 2), blocked(afull), part_view(c, 1), ALU.subtract).then_inc(s_lo, 1)

            def table_chunk(l, c, s=None):
                cc = l * NC + c
                if l == 0:
                    dve.wait_ge(s_xt, c + 1)
                    dve.wait_ge(s_tb, c)
                    tick()
                    v.tensor_copy(xs, flat[:, 3072:3072 + CB * P]).then_inc(s_xs, 1)
                    dve.sem_inc(s_xfree, 1)
                else:
                    dve.wait_ge(s_tb, cc)
                    tick()
                    guard(c, 2 * ((l - 1) * NC + c), relu=True)
                dve.wait_ge(s_ta, cc + 1)
                dve.wait_ge(s_lo, cc)
                tick()
                v.tensor_tensor(blocked(afull), blocked(flat[:, 0:CB * P]),
                                b1row[:, l:l + 1, :].to_broadcast([P, CB, P]), ALU.add).then_inc(s_af, 1)
                lower_parts(cc, c)

            def step(l, i, k, lo=False, hi=False):
                live = lambda d: not ((lo and k < d) or (hi and k >= d))
                if live(0):
                    at = At(i, k, 0, l * NG, l * NI)
                    dve.wait_ge(s_bc[at.k], 32 * (at.n + 1))
                    dve.wait_ge(s_p1, at.G + SL - 1)
                    v.tensor_scalar(hot_t[at.s], dst_bc[at.k], pidx[:, 0:1], None, ALU.is_equal).then_inc(s_hot, 1)
                if live(2):
                    at = At(i, k, 2, l * NG)
                    dve.wait_ge(s_h2, at.G + 3)
                    dve.wait_ge(s_p3, at.G + 1)
                    dve.wait_ge(s_scan, at.G + 2)
                    v.tensor_tensor_scan(scan[at.s], cut_bc[at.k], h2[at.s],
                                         scan[1 - at.s][:, GT * P - 1:GT * P], ALU.min, ALU.max).then_inc(s_scan, 1)
                    dve.wait_ge(s_p4, at.G + 1)
                    dve.wait_ge(s_meta[at.k], 16 * (at.i + l * NI + 1))
                    tick()
                    for t in range(GT):
                        last = v.tensor_scalar(ends[at.s][:, t, :], iota[:, :],
                                               meta[at.k].bitcast(F32)[:, t, 1:2], None, ALU.is_equal)
                    last.then_inc(s_ends, 1)
                if live(4):
                    at = At(i, k, 4, l * NG)
                    _, blk = nc.values_load_multi_w_load_instructions(
                        blocks[0:1, bass.ds(at.g * GT, GT)], engines=[DVE_ENGINE], min_val=0, max_val=NB,
                        skip_runtime_bounds_check_because=WHY)
                    dve.wait_ge(s_p4, at.G + 3)
                    tick()
                    for t in range(GT):
                        dve.wait_ge(s_agg, GT * at.G + t + GT)
                        tick()
                        to = agg[:, bass.ds(blk[t] * P, P)]
                        v.tensor_tensor(to, ps[:, 6 + at.s, t * P:(t + 1) * P], to, ALU.add).then_inc(s_agg, 1)

            for l in range(3):
                with dve.Fori(0, NC) as c:
                    table_chunk(l, c)
                dve.wait_ge(s_lo, NC * (l + 1))
                dve.wait_ge(s_tb, NC * (l + 1))
                dve.wait_ge(s_bd, 16 * NC * (l + 1))
                v.memset(scan[1][:, GT * P - 1:GT * P], 0.0).then_inc(s_zero, 1)
                v.memset(agg[:, :], 0.0).then_inc(s_zero, 1)
                dve.wait_ge(s_zero, 2 * (l + 1))
                for k in range(SL):
                    step(l, 0, k, lo=True)
                with dve.Fori(1, NI) as i:
                    for _, k in body_groups(i):
                        step(l, i, k)
                for k in range(SL):
                    step(l, NI, k, hi=True)
                dve.wait_ge(s_agg, GT * NG * (l + 1) + GT)

            def norm_chunk(i, s, extra=0):
                c = 2 * i + s
                cc = 3 * NC + c
                dve.wait_ge(s_mt, c)
                tick()
                guard(c, 2 * (2 * NC + c), relu=False)
                dve.wait_ge(s_mt, c + 1)
                dve.wait_ge(s_xin[s], 16 * (NC // 2 + 1) + 16 * (i + 1) - (16 if s == 0 else 0) + extra)
                dve.wait_ge(s_lo, cc)
                tick()
                m = [0]

                def ch(ins):
                    m[0] += 1
                    ins.then_inc(s_fv, 1)
                    dve.wait_ge(s_fv, c * NVC + m[0])
                    tick()

                ch(v.tensor_tensor(afull, flat[:, 0:CB * P], xin[s].rearrange("p b f -> p (b f)"), ALU.add))
                dve.sem_inc(s_xfree, 1)
                for b in range(CB):
                    last = v.bn_stats(st6[:, b, :], afull[:, b * P:(b + 1) * P])
                ch(last)
                for b in range(CB):
                    last = v.bn_aggr(mv[:, b, :], st6[:, b, :])
                last.then_inc(s_y, 1)
                dve.wait_ge(s_dev, c + 1)
                tick()
                ch(v.reciprocal(inv_dev, dev))
                dve.wait_ge(s_x1d, 16 * c)
                tick()
                for b in range(CB):
                    last = v.tensor_scalar(bout[:, b * P:(b + 1) * P], afull[:, b * P:(b + 1) * P],
                                           mv[:, b, 0:1], inv_dev[:, b:b + 1], ALU.subtract, ALU.mult)
                ch(last)
                last = v.tensor_copy(afull, bout)
                last.then_inc(s_af, 1)
                dve.sem_inc(s_x1, 1)
                assert m[0] == NVC
                lower_parts(cc, c)

            with dve.Fori(0, NC // 2 - 1) as i:
                for s in range(2):
                    norm_chunk(i, s)
            norm_chunk(NC // 2 - 1, 0)
            norm_chunk(NC // 2 - 1, 1, extra=16)
            dve.wait_ge(s_lo, NC * 4)
            dve.wait_ge(s_x1d, 16 * NC)
            dve.sem_inc(s_rh, 2)
            dve.sem_inc(s_rid, SL)

            def rel_group(i, k, lo):
                at = At(i, k)
                m = [0]

                def ch(ins):
                    m[0] += 1
                    ins.then_inc(s_rv, 1)
                    dve.wait_ge(s_rv, at.g * NVR + m[0])

                dve.wait_ge(s_rl[k], 32 * (i + 1))
                tick()
                dve.wait_ge(s_ra, at.g + 1)
                tick()
                for t in range(GT):
                    v.tensor_scalar(hot_e[at.s][:, t, :], iota[:, :], r_meta[k].bitcast(F32)[:, t, 2:3], None,
                                    ALU.is_equal)
                    last = v.tensor_scalar(same[at.s][:, t, :], key_bc[k][:, t * P:(t + 1) * P],
                                           r_meta[k].bitcast(F32)[:, t, 3:4], None, ALU.is_equal)
                last.then_inc(s_rh, 1)
                dve.wait_ge(s_rh, at.g + 3)
                tick()
                ch(v.tensor_tensor(earlier, same[at.s], below[:, :].unsqueeze(1).to_broadcast([P, GT, P]), ALU.mult))
                ch(v.tensor_reduce(rank, earlier, AX_X, ALU.add))
                ch(v.tensor_scalar(first, rank, 0.0, None, ALU.is_equal))
                ch(v.scalar_tensor_tensor(out=kept, in0=r_meta[k].bitcast(F32)[:, :, 3], scalar=trash_col[:, 0:1],
                                          in1=first, op0=ALU.subtract, op1=ALU.mult))
                assert m[0] == NVR
                if not lo:
                    for t in range(GT):
                        dve.wait_ge(s_add[t], 16 * (at.g - SL + 1))
                        tick()
                v.tensor_scalar(r_row[k], kept, trash_col[:, 0:1], None, ALU.add).then_inc(s_rid, 1)

            for k in range(SL):
                rel_group(0, k, True)
            with dve.Fori(1, NI) as i:
                for _, k in body_groups(i):
                    rel_group(i, k, False)
            for t in range(K):
                dve.wait_ge(s_add[t], 16 * NG)
            dve.wait_ge(s_rb, NG + 2)
            dve.sem_inc(s_sc, 2)
            dve.sem_inc(s_fo, 2)
            F0 = NC * NVC

            def mean_block(b, s):
                m = [0]

                def ch(ins):
                    m[0] += 1
                    ins.then_inc(s_fv, 1)
                    dve.wait_ge(s_fv, F0 + b * NVB + m[0])
                    tick()

                i = b // 2 if isinstance(b, int) else None
                ch(v.tensor_tensor(part[s][:, 0, :], part[s][:, 0, :], part[s][:, 1, :], ALU.add))
                dve.wait_ge(s_23, b + 1)
                tick()
                ch(v.tensor_tensor(part[s][:, 0, :], part[s][:, 0, :], part[s][:, 2, :], ALU.add))
                sums = part[s][:, 0, :].rearrange("p (r w) -> p r w", r=R)
                ch(v.tensor_scalar(cnt, sums[:, :, P], 1.0, None, ALU.max))
                ch(v.reciprocal(inv_cnt, cnt))
                dve.wait_ge(s_ft, b + 1)
                tick()
                for r in range(R):
                    last = v.tensor_scalar(scaled[s][:, r, :], sums[:, r, 0:P], inv_cnt[:, r:r + 1], None, ALU.mult)
                last.then_inc(s_sc, 1)
                assert m[0] == NVM

            def norm_block(b, s, first_use):
                m = [NVM]

                def ch(ins):
                    m[0] += 1
                    ins.then_inc(s_fv, 1)
                    dve.wait_ge(s_fv, F0 + b * NVB + m[0] + 0)
                    tick()

                def chn(ins, count):
                    ins.then_inc(s_fn, 1)
                    dve.wait_ge(s_fn, b * NVN + count)
                    tick()

                dve.wait_ge(s_fo, b + 2)
                tick()
                dve.wait_ge(s_fm, b + 3)
                tick()
                chn(v.scalar_tensor_tensor(out=y_in, in0=ps[:, 4 + s, 0:P], scalar=0.0, in1=x1_in[s],
                                           op0=ALU.max, op1=ALU.add), 1)
                chn(v.bn_stats(o_st6, y_in), 2)
                v.bn_aggr(o_mv, o_st6).then_inc(s_fy, 1)
                dve.wait_ge(s_fd, b + 1)
                tick()
                chn(v.reciprocal(o_inv, o_dev[s]), 3)
                if not first_use:
                    dve.wait_ge(s_out[s], 16 * (b // 2 if isinstance(b, int) else first_use_i[0]))
                    tick()
                v.tensor_scalar(y_out[s], y_in, o_mv[:, 0:1], o_inv[:, 0:1], ALU.subtract, ALU.mult
                                ).then_inc(s_fo, 1)

            s_fn = s_norm
            first_use_i = [None]
            dve.wait_ge(s_part[0], 16 * (K + 1))
            mean_block(0, 0)
            with dve.Fori(0, NB // 2 - 1) as i:
                dve.wait_ge(s_part[1], 16 * (K + 1) * (i + 1))
                tick()
                mean_block(2 * i + 1, 1)
                first_use_i[0] = i
                norm_block(2 * i, 0, False)
                dve.wait_ge(s_part[0], 16 * (K + 1) * (i + 2))
                tick()
                mean_block(2 * i + 2, 0)
                norm_block(2 * i + 1, 1, False)
            dve.wait_ge(s_part[1], 16 * (K + 1) * (NB // 2))
            mean_block(NB - 1, 1)
            first_use_i[0] = NB // 2 - 1
            norm_block(NB - 2, 0, False)
            norm_block(NB - 1, 1, False)


_LAYERS = ("in", "hid", "out")
_INS = ["x", "src", "dst", "edge_type_8"] + [
    f"L0_gnn_{p}_{l}" for l in _LAYERS for p in ("W1", "b1", "W2", "b2")] + ["L1_gnn_weights"]


def kernel(**inputs):
    import numpy as _np
    import concourse.bacc as _bacc
    from concourse import mybir as _mybir
    from concourse.bass_utils import run_bass_kernel_spmd as _run

    nc = _bacc.Bacc("TRN2", target_bir_lowering=False, num_devices=1)
    arrays, aps = {}, {}
    for name in _INS:
        a = _np.ascontiguousarray(inputs[name])
        arrays[f"in_{name}"] = a
        aps[name] = nc.dram_tensor(f"in_{name}", a.shape, _mybir.dt.from_np(a.dtype), kind="ExternalInput").ap()
    n, c = inputs["x"].shape
    out = nc.dram_tensor("out_0", (n, c), _mybir.dt.float32, kind="ExternalOutput").ap()
    params = [tuple(aps[f"L0_gnn_{p}_{l}"] for p in ("W1", "b1", "W2", "b2")) for l in _LAYERS]
    gnn_kernel(nc, aps["x"], aps["src"], aps["dst"], aps["edge_type_8"], params, aps["L1_gnn_weights"], out)
    r = _run(nc, [arrays], core_ids=[0])
    return r.results[0]["out_0"]
```

```python
from contextlib import ExitStack

import numpy as np
import concourse.bass as bass
from concourse import mybir
from concourse.alu_op_type import AluOpType as ALU

F32 = mybir.dt.float32
I32 = mybir.dt.int32
BF16 = mybir.dt.bfloat16
ACT = mybir.ActivationFunctionType
AX_X = mybir.AxisListType.X
PE_ENGINE = mybir.EngineType.PE
DVE_ENGINE = mybir.EngineType.DVE

P = 128
EPS = 1e-5
BIG = 3.3895313892515355e38
OUT_OF_BLOCK = 255
GT = 4
SL = 4
CB = 7
K = 4
WHY = "the block numbers are clamped to the table when they are made"


def gnn_kernel(nc, x, src, dst, etype, params, w_rel, out):
    N, C = x.shape
    E = dst.shape[0]
    R = w_rel.shape[0]
    assert C == P
    NB = -(-N // P)
    NT = -(-((E + NB * (P - 1)) // P) // (GT * SL)) * GT * SL
    NG = NT // GT
    NI = NG // SL
    NQ = -(-NT // P)
    NTP = NQ * P
    ER = -(-(E + 1) // P)
    LC = -(-ER // P)
    ERP = P * LC
    NC = NB // CB
    NBT = NB + 1
    LAST = N - (NB - 1) * P
    NO_BLOCK = (NB + 2) * P
    TRASH = R * N
    W = P + 1
    ZR = GT * 12 * -(-(TRASH + P) // (NI * GT * 12))
    TR = ZR * NI
    assert NB % CB == 0 and NB + 1 <= P and NB % 2 == 0

    ZP = 48
    assert ZR % ZP == 0

    TAIL = ERP * P + P - E
    dst_pad = nc.dram_tensor("dst_pad", (1 + E + TAIL,), I32).ap()
    src_pad = nc.dram_tensor("src_pad", (E + TAIL,), I32).ap()
    typ_pad = nc.dram_tensor("typ_pad", (E + TAIL,), I32).ap()
    row_dst = nc.dram_tensor("row_dst", (NTP, P), BF16).ap()
    row_cut = nc.dram_tensor("row_cut", (NTP, P), BF16).ap()
    row_key = nc.dram_tensor("row_key", (NTP, P), F32).ap()
    col_src = nc.dram_tensor("col_src", (P, NTP), I32).ap()
    col_meta = nc.dram_tensor("col_meta", (P, NTP, 3), F32).ap()
    blk_row = nc.dram_tensor("blk_row", (NQ, P), I32).ap()
    tab_b = nc.dram_tensor("tab_b", (NB * P, P), F32).ap()
    x1_dram = nc.dram_tensor("x1_dram", (NB * P, P), F32).ap()
    rel_tab = [nc.dram_tensor(f"rel_tab{k}", (TR, W), F32).ap() for k in range(K)]

    with ExitStack() as ctx:
        def sb(name, shape, dt=F32):
            return ctx.enter_context(nc.sbuf_tensor(name, shape, dt))

        def sem(name):
            return ctx.enter_context(nc.semaphore(name))

        ps = ctx.enter_context(nc.psum_tensor("ps", [P, 8, 512], F32))
        flat = ps[:, :, :].rearrange("p b c -> p (b c)")
        agg = sb("agg", [P, NBT * P])
        tab_a = sb("tab_a", [P, NBT * 3 * P], BF16)
        blocks = sb("blocks", [1, NTP], I32)
        ident = sb("ident", [P, P])
        iota = sb("iota", [P, P])
        below = sb("below", [P, P])
        pidx = sb("pidx", [P, 1])
        ones = sb("ones", [P, 1])
        ones_b = sb("ones_b", [P, 1], BF16)
        eps = sb("eps", [P, 1])
        zeros = sb("zeros", [P, ZR // ZP * W])
        trash_col = sb("trash_col", [P, 1])
        w1 = sb("w1", [P, 3, 2, P])
        w2 = sb("w2", [P, 3, P])
        wd = sb("wd", [P, 3, P])
        b1row = sb("b1row", [P, 3, P])
        b2col = sb("b2col", [P, 3])
        wr_t = sb("wr_t", [P, R, P])
        WORK = 10240
        work = sb("work", [P, WORK])

        class Area:
            def __init__(self, base, size):
                self.base, self.size, self.at = base, size, 0

            def cut(self, n, dt=F32, parts=P):
                words = n if dt != BF16 else n // 2
                ap = self.base[0:parts, self.at:self.at + words]
                self.at += words
                assert self.at <= self.size, self.at
                return ap if dt == F32 else ap.bitcast(dt)

        a = Area(agg, NBT * P)
        pad_vals = a.cut(2 * TAIL + 1, I32, 1)
        wr_raw = a.cut(R * P).rearrange("p (r j) -> p r j", r=R)
        last_i = a.cut(LC, I32)
        last_f = a.cut(LC)
        thr_row = a.cut(NBT)
        thr_col = a.cut(1, F32, NBT)
        jbase = a.cut(NQ)
        full = a.cut(LC * NBT).rearrange("p (c b) -> p c b", c=LC)
        cnt0 = a.cut(1, F32, NBT)
        win_at = a.cut(1, I32, NBT)
        win_i = a.cut(P, I32, NBT)
        win_f = a.cut(P, F32, NBT)
        cnt1 = a.cut(1, F32, NBT)
        start = a.cut(1, F32, NBT)
        step_mat = a.cut(P)
        upto_mat = a.cut(P)
        deg_b = a.cut(1, F32, NB)
        nt_i = a.cut(1, I32, NB)
        nt_f = a.cut(1, F32, NB)
        upto = a.cut(1, F32, NB)
        shift2 = a.cut(2, F32, NB)
        iota_j = a.cut(NTP, F32, NB)
        past = a.cut(NTP, F32, NB)
        blk_f = a.cut(NQ)
        blk_i = a.cut(NQ, I32)
        base_f = a.cut(NQ)
        from_f = a.cut(NQ)
        from_i = a.cut(NQ, I32)
        trash_row = a.cut(P)
        win_from = [a.cut(1, I32) for _ in range(2)]
        win_base = [a.cut(1) for _ in range(2)]
        dst_w = [a.cut(P + 2, I32) for _ in range(2)]
        src_w = [a.cut(P, I32) for _ in range(2)]
        typ_w = [a.cut(P, I32) for _ in range(2)]
        dst_f = a.cut(P + 2)
        src_f = a.cut(P)
        loc_f = a.cut(P)
        end_f = a.cut(P)
        key_f = a.cut(P)
        tmp_a = a.cut(P)
        tmp_b = a.cut(P)
        tmp_c = a.cut(P)
        loc_b = [a.cut(P, BF16) for _ in range(2)]
        cut_b = [a.cut(P, BF16) for _ in range(2)]
        key_o = [a.cut(P) for _ in range(2)]
        meta_o = [a.cut(P * 3) for _ in range(2)]
        src_o = [a.cut(P, I32) for _ in range(2)]

        a = Area(work, WORK)
        xin = [a.cut(CB * P).rearrange("p (b f) -> p b f", f=P) for _ in range(2)]
        xs = a.cut(CB * P)
        afull = a.cut(CB * P)
        bout = a.cut(CB * P)
        bad = a.cut(CB * P, I32)
        st6 = a.cut(CB * 6).rearrange("p (b s) -> p b s", s=6)
        mv = a.cut(CB * 2).rearrange("p (b s) -> p b s", s=2)
        dev = a.cut(CB)
        inv_dev = a.cut(CB)

        a = Area(work, WORK)
        idx = [a.cut(GT, I32) for _ in range(SL)]
        meta = [a.cut(GT * 3).rearrange("p (t f) -> p t f", f=3) for _ in range(SL)]
        dst_bc = [a.cut(GT * P, BF16) for _ in range(SL)]
        cut_bc = [a.cut(GT * P, BF16) for _ in range(SL)]
        rows = [a.cut(GT * P).rearrange("p (t f) -> p t f", f=P) for _ in range(SL)]
        hot_t = [a.cut(GT * P, BF16) for _ in range(2)]
        h1 = [a.cut(GT * P) for _ in range(2)]
        h2 = [a.cut(GT * P) for _ in range(2)]
        scan = [a.cut(GT * P) for _ in range(2)]
        h2e = [a.cut(GT * P) for _ in range(2)]
        ends = [a.cut(GT * P).rearrange("p (t n) -> p t n", n=P) for _ in range(2)]

        a = Area(work, WORK)
        r_meta = [a.cut(GT * 3).rearrange("p (t f) -> p t f", f=3) for _ in range(SL)]
        key_bc = [a.cut(GT * P) for _ in range(SL)]
        hot_e = [a.cut(GT * P, BF16).rearrange("p (t n) -> p t n", n=P) for _ in range(2)]
        same = [a.cut(GT * P, BF16).rearrange("p (t n) -> p t n", n=P) for _ in range(2)]
        earlier = a.cut(GT * P).rearrange("p (t n) -> p t n", n=P)
        rank = a.cut(GT)
        first = a.cut(GT)
        kept = a.cut(GT)
        spread = [a.cut(GT * P, BF16) for _ in range(2)]
        msg = [a.cut(GT * W).rearrange("p (t f) -> p t f", f=W) for _ in range(SL)]
        r_row = [a.cut(GT, I32) for _ in range(SL)]

        a = Area(tab_a[:, :].bitcast(F32), NBT * 3 * P // 2)
        part = [a.cut(K * R * W).rearrange("p (k w) -> p k w", k=K) for _ in range(2)]
        sum01 = [a.cut(R * W) for _ in range(2)]
        sum23 = [a.cut(R * W) for _ in range(2)]
        a = Area(work, WORK)
        x1_in = [a.cut(P) for _ in range(2)]
        mean = [a.cut(R * P).rearrange("p (r f) -> p r f", r=R) for _ in range(2)]
        mean_t = [a.cut(R * P) for _ in range(2)]
        cnt = [a.cut(R) for _ in range(2)]
        inv_cnt = [a.cut(R) for _ in range(2)]
        y_in = [a.cut(P) for _ in range(2)]
        y_out = [a.cut(P) for _ in range(2)]
        o_st6 = [a.cut(6) for _ in range(2)]
        o_mv = [a.cut(2) for _ in range(2)]
        o_dev = [a.cut(1) for _ in range(2)]
        o_inv = [a.cut(1) for _ in range(2)]

        s_pad = sem("s_pad")
        s_w = sem("s_w")
        s_last = sem("s_last")
        s_row0 = sem("s_row0")
        s_gp = sem("s_gp")
        s_pv = sem("s_pv")
        s_pt = sem("s_pt")
        s_blk = sem("s_blk")
        s_from = sem("s_from")
        s_win = [sem(f"s_win{k}") for k in range(2)]
        s_wv = sem("s_wv")
        s_wt = sem("s_wt")
        s_wo = sem("s_wo")
        s_store = [sem(f"s_store{k}") for k in range(2)]
        s_xin = [sem(f"s_xin{k}") for k in range(2)]
        s_xfree = sem("s_xfree")
        s_xt = sem("s_xt")
        s_xs = sem("s_xs")
        s_ta = sem("s_ta")
        s_tb = sem("s_tb")
        s_af = sem("s_af")
        s_hi = sem("s_hi")
        s_re = sem("s_re")
        s_mid = sem("s_mid")
        s_lo = sem("s_lo")
        s_bf = sem("s_bf")
        s_bd = sem("s_bd")
        s_tv = sem("s_tv")
        s_idx = [sem(f"s_idx{k}") for k in range(SL)]
        s_meta = [sem(f"s_meta{k}") for k in range(SL)]
        s_bc = [sem(f"s_bc{k}") for k in range(SL)]
        s_rows = [sem(f"s_rows{k}") for k in range(SL)]
        s_hot = sem("s_hot")
        s_p1 = sem("s_p1")
        s_h1 = sem("s_h1")
        s_p2 = sem("s_p2")
        s_h2 = sem("s_h2")
        s_scan = sem("s_scan")
        s_p3 = sem("s_p3")
        s_h2e = sem("s_h2e")
        s_ends = sem("s_ends")
        s_p4 = sem("s_p4")
        s_agg = sem("s_agg")
        s_zero = sem("s_zero")
        s_cred = sem("s_cred")
        s_ztab = sem("s_ztab")
        s_tick = {e: sem(f"s_tick_{e}") for e in ("pool", "dve", "act", "sp")}
        s_mt = sem("s_mt")
        s_y = sem("s_y")
        s_dev = sem("s_dev")
        s_x1 = sem("s_x1")
        s_x1d = sem("s_x1d")
        s_rl = [sem(f"s_rl{k}") for k in range(SL)]
        s_rh = sem("s_rh")
        s_rv = sem("s_rv")
        s_rid = sem("s_rid")
        s_ra = sem("s_ra")
        s_rs = sem("s_rs")
        s_rb = sem("s_rb")
        s_rm = sem("s_rm")
        s_add = [sem(f"s_add{k}") for k in range(K)]
        s_part = [sem(f"s_part{k}") for k in range(2)]
        s_x1in = [sem(f"s_x1in{k}") for k in range(2)]
        s_01 = sem("s_01")
        s_23 = sem("s_23")
        s_fv = sem("s_fv")
        s_tot = sem("s_tot")
        s_sc = sem("s_sc")
        s_ft = sem("s_ft")
        s_fa = sem("s_fa")
        s_fm = sem("s_fm")
        s_fy = sem("s_fy")
        s_fd = sem("s_fd")
        s_fo = sem("s_fo")
        s_out = [sem(f"s_out{k}") for k in range(2)]
        s_fi = sem("s_fi")
        s_norm = sem("s_norm")

        GP_PAD, GP_ALL = 3, 9
        PV_CONST = 12
        PV_FULL = PV_CONST + 1 + LC
        PV_WIN0 = PV_FULL + 2
        PV_START = PV_WIN0 + 4
        PV_TILES = PV_START + 4
        PV_PAST = PV_TILES + 4
        PV_BLK = PV_PAST + 5
        WV, WVT = 16, 17
        NVC = 4
        NVR = 4
        NVB = 2
        NVN = 2

        class At:
            def __init__(self, i, k, d=0, first_group=0, first_pass=0):
                self.k = (k - d) % SL
                self.s = (k - d) % 2
                self.i = i + (k - d) // SL
                self.g = self.i * SL + self.k
                self.G = self.g + first_group
                self.n = self.i + first_pass

        def loop(eng, first, end):
            return nc.Fori(first, end, engines=[eng.engine], hint_back_edge=True)

        def after(eng, semaphore, value):
            if not (isinstance(value, int) and value <= 0):
                eng.wait_ge(semaphore, value)

        def body_groups(i):
            return [(i, k) for k in range(SL)]

        block = ctx.enter_context(nc.Block())

        @block.sync
        def _(sp):
            tick = lambda: sp.sem_inc(s_tick["sp"], 1)
            sp.dma_start(dst_pad[1:1 + E], dst).then_inc(s_pad, 16)
            sp.dma_start(src_pad[0:E], src).then_inc(s_pad, 16)
            sp.dma_start(typ_pad[0:E], etype).then_inc(s_pad, 16)
            sp.wait_ge(s_gp, GP_PAD)
            as_row = lambda v: v.rearrange("(a n) -> a n", a=1)
            sp.dma_start(as_row(dst_pad[0:1]), pad_vals[:, 2 * TAIL:2 * TAIL + 1]).then_inc(s_pad, 16)
            sp.dma_start(as_row(dst_pad[1 + E:1 + E + TAIL]), pad_vals[:, 0:TAIL]).then_inc(s_pad, 16)
            sp.dma_start(as_row(src_pad[E:E + TAIL]), pad_vals[:, TAIL:2 * TAIL]).then_inc(s_pad, 16)
            sp.dma_start(as_row(typ_pad[E:E + TAIL]), pad_vals[:, TAIL:2 * TAIL]).then_inc(s_pad, 16)
            for l in range(3):
                W1, b1, W2, b2 = params[l]
                sp.dma_start(w1[:, l], W1.rearrange("(h i) o -> i h o", h=2)).then_inc(s_w, 16)
                sp.dma_start(w2[:, l], W2).then_inc(s_w, 16)
                sp.dma_start(b1row[:, l], as_row(b1).to_broadcast([P, P])).then_inc(s_w, 16)
                with nc.allow_non_contiguous_dma(reason="a bias as a column, once"):
                    sp.dma_start(b2col[:, l:l + 1], b2.rearrange("(n a) -> n a", a=1)).then_inc(s_w, 16)
            sp.dma_start(wr_raw, w_rel.rearrange("r i j -> i r j")).then_inc(s_w, 16)
            sp.wait_ge(s_pad, 7 * 16)
            with nc.allow_non_contiguous_dma(reason="the last edge of each row of 128, once"):
                sp.dma_start(last_i, dst_pad[P:P + ERP * P].rearrange("(p c e) -> p c e", c=LC, e=P)[:, :, 0]
                             ).then_inc(s_last, 16)
            sp.wait_ge(s_pv, PV_BLK)
            with nc.allow_non_contiguous_dma(reason="the tiles' blocks, once"):
                sp.dma_start(blk_row.rearrange("q p -> p q"), blk_i).then_inc(s_blk, 16)
            sp.wait_ge(s_blk, 16)
            sp.dma_start(blocks[:, :], blk_row.rearrange("q p -> (q p)").rearrange("(a n) -> a n", a=1)
                         ).then_inc(s_blk, 16)
            with loop(sp, 0, NQ // 2) as i:
                for s in range(2):
                    q = 2 * i + s
                    sp.wait_ge(s_wo, q + 1)
                    tick()
                    sp.dma_start(row_dst[bass.ds(q * P, P), :], loc_b[s]).then_inc(s_store[s], 16)
                    sp.dma_start(row_cut[bass.ds(q * P, P), :], cut_b[s]).then_inc(s_store[s], 16)
                    sp.dma_start(row_key[bass.ds(q * P, P), :], key_o[s]).then_inc(s_store[s], 16)
                    sp.dma_start(col_meta[:, bass.ds(q * P, P), :].rearrange("p j f -> p (j f)"),
                                 meta_o[s]).then_inc(s_store[s], 16)
                    sp.dma_start(col_src[:, bass.ds(q * P, P)], src_o[s]).then_inc(s_store[s], 16)

            def x_chunk(i, s, whole=True):
                c = 2 * i + s
                sp.wait_ge(s_xfree, c + 1)
                tick()
                if whole:
                    sp.dma_start(xin[s], x[bass.ds(c * CB * P, CB * P), :].rearrange("(b p) f -> p b f", p=P)
                                 ).then_inc(s_xin[s], 16)
                else:
                    c0 = (NC - 1) * CB * P
                    sp.dma_start(xin[s][:, 0:CB - 1, :],
                                 x[c0:c0 + (CB - 1) * P, :].rearrange("(b p) f -> p b f", p=P)
                                 ).then_inc(s_xin[s], 16)
                    sp.dma_start(xin[s][0:LAST, CB - 1, :], x[c0 + (CB - 1) * P:N, :]).then_inc(s_xin[s], 16)

            def store_b(l, c):
                sp.wait_ge(s_bf, l * NC + c + 1)
                tick()
                sp.dma_start(tab_b[bass.ds(c * CB * P, CB * P), :].rearrange("(b p) f -> p b f", p=P),
                             bout.rearrange("p (b f) -> p b f", f=P)).then_inc(s_bd, 16)

            for l in range(3):
                if l == 0:
                    x_chunk(0, 0)
                    with loop(sp, 0, NC // 2 - 1) as i:
                        x_chunk(i, 1)
                        store_b(0, 2 * i)
                        x_chunk(i + 1, 0)
                        store_b(0, 2 * i + 1)
                    x_chunk(NC // 2 - 1, 1, whole=False)
                    store_b(0, NC - 2)
                    store_b(0, NC - 1)
                else:
                    with loop(sp, 0, NC) as c:
                        store_b(l, c)
                sp.wait_ge(s_lo, NC * (l + 1))
                sp.wait_ge(s_bd, 16 * NC * (l + 1))
                if l == 0:
                    for s in range(2):
                        sp.wait_ge(s_store[s], 80 * (NQ // 2))
                with loop(sp, 0, NI) as i:
                    for _, k in body_groups(i):
                        at = At(i, k, 0, l * NG, l * NI)
                        sp.wait_ge(s_p1, at.G + 1)
                        tick()
                        sp.dma_start(idx[k], col_src[:, bass.ds(at.g * GT, GT)]).then_inc(s_idx[k], 16)
                        sp.wait_ge(s_ends, at.G + 1)
                        tick()
                        sp.dma_start(meta[k], col_meta[:, bass.ds(at.g * GT, GT), :]).then_inc(s_meta[k], 16)
                        sp.dma_start(dst_bc[k], row_dst[bass.ds(at.g * GT, GT), :].rearrange("t e -> (t e)")
                                     .partition_broadcast(P)).then_inc(s_bc[k], 16)
                        sp.dma_start(cut_bc[k], row_cut[bass.ds(at.g * GT, GT), :].rearrange("t e -> (t e)")
                                     .partition_broadcast(P)).then_inc(s_bc[k], 16)
            sp.wait_ge(s_agg, GT * NG * 3 + GT)
            base = NC

            def x_again(i, s, whole=True):
                c = 2 * i + s
                sp.wait_ge(s_xfree, base + c + 1)
                tick()
                if whole:
                    sp.dma_start(xin[s], x[bass.ds(c * CB * P, CB * P), :].rearrange("(b p) f -> p b f", p=P)
                                 ).then_inc(s_xin[s], 16)
                else:
                    c0 = (NC - 1) * CB * P
                    sp.dma_start(xin[s][:, 0:CB - 1, :],
                                 x[c0:c0 + (CB - 1) * P, :].rearrange("(b p) f -> p b f", p=P)
                                 ).then_inc(s_xin[s], 16)
                    sp.dma_start(xin[s][0:LAST, CB - 1, :], x[c0 + (CB - 1) * P:N, :]).then_inc(s_xin[s], 16)

            def store_x1(c):
                sp.wait_ge(s_x1, c + 1)
                tick()
                sp.dma_start(x1_dram[bass.ds(c * CB * P, CB * P), :].rearrange("(b p) f -> p b f", p=P),
                             bout.rearrange("p (b f) -> p b f", f=P)).then_inc(s_x1d, 16)

            x_again(0, 0)
            with loop(sp, 0, NC // 2 - 1) as i:
                x_again(i, 1)
                store_x1(2 * i)
                x_again(i + 1, 0)
                store_x1(2 * i + 1)
            x_again(NC // 2 - 1, 1, whole=False)
            store_x1(NC - 2)
            store_x1(NC - 1)
            sp.wait_ge(s_lo, NC * 4)
            sp.wait_ge(s_x1d, 16 * NC)
            with loop(sp, 0, NI) as i:
                for _, k in body_groups(i):
                    at = At(i, k)
                    sp.wait_ge(s_rid, at.g + 1)
                    tick()
                    sp.dma_start(r_meta[k], col_meta[:, bass.ds(at.g * GT, GT), :]).then_inc(s_rl[k], 16)
                    sp.dma_start(key_bc[k], row_key[bass.ds(at.g * GT, GT), :].rearrange("t e -> (t e)")
                                 .partition_broadcast(P)).then_inc(s_rl[k], 16)
            for t in range(K):
                sp.wait_ge(s_add[t], 16 * NG)

            def load_parts(b, s):
                after(sp, s_01, b - 1)
                after(sp, s_23, b - 1)
                tick()
                for k in range(K):
                    view = rel_tab[k][0:R * N, :].rearrange("(n r) w -> n (r w)", r=R)
                    if isinstance(b, int) and b == NB - 1:
                        sp.dma_start(part[s][0:LAST, k, :], view[b * P:N, :]).then_inc(s_part[s], 16)
                    else:
                        sp.dma_start(part[s][:, k, :], view[bass.ds(b * P, P), :]).then_inc(s_part[s], 16)

            def load_x1(b, s):
                after(sp, s_fy, b + 1 if not isinstance(b, int) or b >= 2 else 0)
                tick()
                sp.dma_start(x1_in[s], x1_dram[bass.ds(b * P, P), :]).then_inc(s_x1in[s], 16)

            def store_out(b, s):
                sp.wait_ge(s_fo, b + 1)
                tick()
                if isinstance(b, int) and b == NB - 1:
                    sp.dma_start(out[b * P:N, :], y_out[s][0:LAST, :]).then_inc(s_out[s], 16)
                else:
                    sp.dma_start(out[bass.ds(b * P, P), :], y_out[s]).then_inc(s_out[s], 16)

            def last_step(b, s):
                if not isinstance(b, int) or b + 2 < NB:
                    load_parts(b + 2, s)
                if not isinstance(b, int) or 0 <= b - 2 < NB:
                    store_out(b - 2, s)
                if not isinstance(b, int) or b + 1 < NB:
                    load_x1(b + 1, 1 - s)

            load_parts(0, 0)
            load_parts(1, 1)
            load_x1(0, 0)
            for b in range(2):
                last_step(b, b)
            with loop(sp, 1, NB // 2 - 2) as i:
                for s in range(2):
                    last_step(2 * i + s, s)
            for b in range(NB - 4, NB + 2):
                last_step(b, b % 2)
            for s in range(2):
                sp.wait_ge(s_out[s], 16 * (NB // 2))

        @block.gpsimd
        def _(pool):
            g = nc.gpsimd
            tick = lambda: pool.sem_inc(s_tick["pool"], 1)
            g.memset(pad_vals[:, 0:TAIL], NO_BLOCK).then_inc(s_gp, 1)
            g.memset(pad_vals[:, TAIL:2 * TAIL], 0).then_inc(s_gp, 1)
            g.memset(pad_vals[:, 2 * TAIL:2 * TAIL + 1], -1).then_inc(s_gp, 1)
            exact = dict(allow_small_or_imprecise_dtypes=True)
            g.iota(iota[:, :], [[1, P]], base=0, channel_multiplier=0, **exact).then_inc(s_gp, 1)
            g.iota(pidx[:, :], [[0, 1]], base=0, channel_multiplier=1, **exact).then_inc(s_gp, 1)
            g.iota(thr_row, [[P, NBT]], base=0, channel_multiplier=0, **exact).then_inc(s_gp, 1)
            g.iota(thr_col, [[0, 1]], base=0, channel_multiplier=P, **exact).then_inc(s_gp, 1)
            g.iota(jbase, [[P * P, NQ]], base=0, channel_multiplier=P, **exact).then_inc(s_gp, 1)
            g.iota(iota_j, [[1, NTP]], base=0, channel_multiplier=0, **exact).then_inc(s_gp, 1)
            as_elements = lambda v: v.rearrange("(a n) -> a n", a=1)
            pool.wait_ge(s_pad, 7 * 16)
            pool.wait_ge(s_pv, PV_WIN0)
            g.indirect_dma_start(win_i, None, as_elements(dst_pad),
                                 bass.IndirectOffsetOnAxis(ap=win_at, axis=1)).then_inc(s_row0, 16)
            with loop(pool, 0, NQ // 2) as i:
                for s in range(2):
                    q = 2 * i + s
                    pool.wait_ge(s_from, q + 1)
                    tick()
                    for to, of in ((dst_w[s], dst_pad), (src_w[s], src_pad), (typ_w[s], typ_pad)):
                        g.indirect_dma_start(to, None, as_elements(of),
                                             bass.IndirectOffsetOnAxis(ap=win_from[s], axis=1)
                                             ).then_inc(s_win[s], 16)
            for l in range(3):
                pool.wait_ge(s_bd, 16 * NC * (l + 1))
                pool.wait_ge(s_lo, NC * (l + 1))
                with loop(pool, 0, NI) as i:
                    for _, k in body_groups(i):
                        at = At(i, k, 0, l * NG, l * NI)
                        pool.wait_ge(s_idx[k], 16 * (at.n + 1))
                        tick()
                        pool.wait_ge(s_p1, at.G + 1)
                        tick()
                        for t in range(GT):
                            g.indirect_dma_start(rows[k][:, t, :], None, tab_b,
                                                 bass.IndirectOffsetOnAxis(ap=idx[k][:, t:t + 1], axis=0)
                                                 ).then_inc(s_rows[k], 16)
            pool.wait_ge(s_ztab, 16 * K * NI)

            def add_group(i, k, at_start):
                at = At(i, k)
                pool.wait_ge(s_rid, at.g + SL + 1)
                tick()
                pool.wait_ge(s_rm, at.g + 3)
                tick()
                for t in range(GT):
                    if not (at_start and k == 0):
                        pool.wait_ge(s_add[t], 16 * at.g)
                        tick()
                    g.indirect_dma_start(rel_tab[t], bass.IndirectOffsetOnAxis(ap=r_row[k][:, t:t + 1], axis=0),
                                         msg[k][:, t, :], None, compute_op=ALU.add).then_inc(s_add[t], 16)

            for k in range(SL):
                add_group(0, k, True)
            with loop(pool, 1, NI) as i:
                for _, k in body_groups(i):
                    add_group(i, k, False)
            with loop(pool, 0, NB // 2) as i:
                for s in range(2):
                    pool.wait_ge(s_part[s], 16 * K * (i + 1))
                    pool.wait_ge(s_tot, 2 * i + s + 1)
                    g.tensor_tensor(sum23[s], part[s][:, 2, :], part[s][:, 3, :], ALU.add).then_inc(s_23, 1)

        @block.tensor
        def _(pe):
            mm, tr = pe.matmul, pe.transpose
            pe.wait_ge(s_pv, PV_FULL)
            for c in range(LC):
                last = mm(ps[0:NBT, 0, 0:1], full[:, c, :], ones[:, :], start=(c == 0), stop=(c == LC - 1))
            last.then_inc(s_pt, 1)
            pe.wait_ge(s_pv, PV_START)
            mm(ps[0:NB, 1, 0:1], step_mat[0:NBT, 0:NB], start, start=True, stop=True).then_inc(s_pt, 1)
            pe.wait_ge(s_pv, PV_TILES)
            mm(ps[0:NB, 2, 0:1], upto_mat[0:NB, 0:NB], nt_f, start=True, stop=True).then_inc(s_pt, 1)
            pe.wait_ge(s_pv, PV_PAST)
            for q in range(NQ):
                last = mm(ps[:, 3, 2 * q:2 * q + 2], past[:, q * P:(q + 1) * P], shift2, start=True, stop=True)
            last.then_inc(s_pt, 1)
            pe.wait_ge(s_w, 13 * 16)
            for r in range(R):
                last = tr(flat[:, 2048 + r * P:2048 + (r + 1) * P], wr_raw[:, r, :], ident[:, :])
            last.then_inc(s_pt, 1)
            with loop(pe, 0, NQ // 2) as i:
                for s in range(2):
                    q = 2 * i + s
                    pe.wait_ge(s_wv, q * WVT + WV)
                    for f, v in enumerate((src_f, end_f, loc_f, key_f)):
                        last = tr(ps[:, 6 + s, f * P:(f + 1) * P], v, ident[:, :])
                    last.then_inc(s_wt, 1)

            def products(l, c):
                cc = l * NC + c
                pe.wait_ge(s_xs, cc + 1)
                pe.wait_ge(s_af, cc + 1)
                for b in range(CB):
                    last = mm(flat[:, b * P:(b + 1) * P], xs[:, b * P:(b + 1) * P], wd[:, l], start=True, stop=True)
                last.then_inc(s_ta, 1)
                after(pe, s_bf, cc)
                for b in range(CB):
                    last = mm(flat[:, 1024 + b * P:1024 + (b + 1) * P], xs[:, b * P:(b + 1) * P], w1[:, l, 1],
                              start=True, stop=True)
                last.then_inc(s_tb, 1)

            def turn_x(i, s, extra=0):
                pe.wait_ge(s_xin[s], 16 * (i + 1) + extra)
                after(pe, s_xs, 2 * i + s)
                for b in range(CB):
                    last = tr(flat[:, 3072 + b * P:3072 + (b + 1) * P], xin[s][:, b, :], ident[:, :])
                last.then_inc(s_xt, 1)

            def turn_y(c):
                pe.wait_ge(s_xs, 3 * NC + c + 1)

                for b in range(CB):
                    last = tr(flat[:, b * P:(b + 1) * P], xs[:, b * P:(b + 1) * P], ident[:, :])
                last.then_inc(s_mt, 1)

            def step(l, i, k, lo=False, hi=False):
                live = lambda d: not ((lo and k < d) or (hi and k >= d))
                if live(0):
                    at = At(i, k, 0, l * NG, l * NI)
                    _, blk = nc.values_load_multi_w_load_instructions(
                        blocks[0:1, bass.ds(at.g * GT, GT)], engines=[PE_ENGINE], min_val=0, max_val=NB,
                        skip_runtime_bounds_check_because=WHY)
                    pe.wait_ge(s_hot, at.G + 1)
                    pe.wait_ge(s_h1, at.G + 1)
                    pe.wait_ge(s_rows[at.k], 64 * (at.n + 1))
                    for t in range(GT):
                        to = ps[:, at.s, t * P:(t + 1) * P]
                        for h in range(3):
                            mm(to, tab_a[:, bass.ds(blk[t] * (3 * P) + h * P, P)], hot_t[at.s][:, t * P:(t + 1) * P],
                               start=(h == 0), stop=False)
                        last = mm(to, rows[at.k][:, t, :], ident[:, :], start=False, stop=True)
                    last.then_inc(s_p1, 1)
                if live(1):
                    at = At(i, k, 1, l * NG)
                    pe.wait_ge(s_h1, at.G + 3)
                    pe.wait_ge(s_h2, at.G + 1)
                    mm(ps[:, 2 + at.s, :], w2[:, l], h1[at.s], start=True, stop=True).then_inc(s_p2, 1)
                if live(2):
                    at = At(i, k, 2, l * NG)
                    pe.wait_ge(s_scan, at.G + 3)
                    pe.wait_ge(s_h2e, at.G + 1)
                    for t in range(GT):
                        last = tr(ps[:, 4 + at.s, t * P:(t + 1) * P], scan[at.s][:, t * P:(t + 1) * P], ident[:, :])
                    last.then_inc(s_p3, 1)
                if live(3):
                    at = At(i, k, 3, l * NG)
                    pe.wait_ge(s_h2e, at.G + 3)
                    pe.wait_ge(s_ends, at.G + SL + 1)
                    pe.wait_ge(s_agg, GT * at.G)
                    for t in range(GT):
                        last = mm(ps[:, 6 + at.s, t * P:(t + 1) * P], h2e[at.s][:, t * P:(t + 1) * P],
                                  ends[at.s][:, t, :], start=True, stop=True)
                    last.then_inc(s_p4, 1)

            pe.sem_inc(s_xfree, 2)
            pe.sem_inc(s_p1, SL)
            for q in (s_p2, s_p3, s_p4):
                pe.sem_inc(q, 2)
            for l in range(3):
                if l == 0:
                    for s in range(2):
                        turn_x(0, s)
                        products(0, s)
                    with loop(pe, 1, NC // 2 - 1) as i:
                        for s in range(2):
                            turn_x(i, s)
                            products(0, 2 * i + s)
                    turn_x(NC // 2 - 1, 0)
                    products(0, NC - 2)
                    turn_x(NC // 2 - 1, 1, extra=16)
                    products(0, NC - 1)
                    pe.wait_ge(s_blk, 32)
                else:
                    with loop(pe, 0, NC) as c:
                        products(l, c)
                pe.wait_ge(s_lo, NC * (l + 1))
                for k in range(SL):
                    step(l, 0, k, lo=True)
                with loop(pe, 1, NI) as i:
                    for _, k in body_groups(i):
                        step(l, i, k)
                for k in range(SL - 1):
                    step(l, NI, k, hi=True)
            with loop(pe, 0, NC) as c:
                turn_y(c)
            pe.wait_ge(s_lo, NC * 4)

            def rel_step(i, k, lo=False, hi=False):
                live = lambda d: not ((lo and k < d) or (hi and k >= d))
                if live(0):
                    at = At(i, k)
                    pe.wait_ge(s_rh, at.g + 3)
                    pe.wait_ge(s_rs, at.g + 1)
                    for t in range(GT):
                        last = mm(ps[:, at.s, t * P:(t + 1) * P], hot_e[at.s][:, t, :], same[at.s][:, t, :],
                                  start=True, stop=True)
                    last.then_inc(s_ra, 1)
                if live(1):
                    at = At(i, k, 1)
                    _, blk = nc.values_load_multi_w_load_instructions(
                        blocks[0:1, bass.ds(at.g * GT, GT)], engines=[PE_ENGINE], min_val=0, max_val=NB,
                        skip_runtime_bounds_check_because=WHY)
                    pe.wait_ge(s_rs, at.g + 3)
                    pe.wait_ge(s_rm, at.g + 1)
                    for t in range(GT):
                        by = spread[at.s][:, t * P:(t + 1) * P]
                        for h in range(3):
                            mm(ps[:, 2 + at.s, t * P:(t + 1) * P], by,
                               tab_a[:, bass.ds(blk[t] * (3 * P) + h * P, P)], start=(h == 0), stop=(h == 2))
                        last = mm(ps[:, 4 + at.s, t:t + 1], by, ones_b[:, :], start=True, stop=True)
                    last.then_inc(s_rb, 1)

            for q in (s_ra, s_rb):
                pe.sem_inc(q, 2)
            for k in range(SL):
                rel_step(0, k, lo=True)
            with loop(pe, 1, NI) as i:
                for _, k in body_groups(i):
                    rel_step(i, k)
            rel_step(NI, 0, hi=True)
            for q in (s_ft, s_fm):
                pe.sem_inc(q, 2)

            def turn_block(b, s):
                pe.wait_ge(s_sc, b + 3)
                pe.wait_ge(s_fa, b + 1)
                for r in range(R):
                    last = tr(flat[:, s * 1024 + r * P:s * 1024 + (r + 1) * P], mean[s][:, r, :], ident[:, :])
                last.then_inc(s_ft, 1)

            def relate_block(b, s):
                pe.wait_ge(s_fa, b + 3)
                pe.wait_ge(s_fy, b + 1)
                for r in range(R):
                    last = mm(ps[:, 4 + s, 0:P], mean_t[s][:, r * P:(r + 1) * P], wr_t[:, r, :],
                              start=(r == 0), stop=(r == R - 1))
                last.then_inc(s_fm, 1)

            turn_block(0, 0)
            with loop(pe, 0, NB // 2 - 1) as i:
                turn_block(2 * i + 1, 1)
                relate_block(2 * i, 0)
                turn_block(2 * i + 2, 0)
                relate_block(2 * i + 1, 1)
            turn_block(NB - 1, 1)
            relate_block(NB - 2, 0)
            relate_block(NB - 1, 1)

        @block.scalar
        def _(act):
            tick = lambda: act.sem_inc(s_tick["act"], 1)
            a_ = nc.scalar.activation

            def part_view(c, h):
                return tab_a[:, bass.ds(c * (CB * 3 * P), CB * 3 * P)].rearrange(
                    "p (b t f) -> p b t f", t=3, f=P)[:, :, h, :]

            def b_chunk(l, c):
                act.wait_ge(s_tb, l * NC + c + 1)
                after(act, s_bd, 16 * (l * NC + c))
                tick()
                a_(bout, flat[:, 1024:1024 + CB * P], ACT.Copy).then_inc(s_bf, 1)

            def parts(cc, c):
                act.wait_ge(s_af, cc + 2)
                tick()
                a_(part_view(c, 0), afull.rearrange("p (b f) -> p b f", f=P), ACT.Copy).then_inc(s_hi, 1)
                act.wait_ge(s_re, cc + 1)
                tick()
                a_(part_view(c, 1), afull.rearrange("p (b f) -> p b f", f=P), ACT.Copy).then_inc(s_mid, 1)

            def step(l, i, k, lo=False, hi=False):
                live = lambda d: not ((lo and k < d) or (hi and k >= d))
                if live(0):
                    at = At(i, k, 0, l * NG)
                    act.wait_ge(s_p1, at.G + SL + 1)
                    act.wait_ge(s_p2, at.G + 1)
                    a_(h1[at.s], ps[:, at.s, :], ACT.Relu).then_inc(s_h1, 1)
                if live(1):
                    at = At(i, k, 1, l * NG)
                    act.wait_ge(s_p2, at.G + 3)
                    act.wait_ge(s_scan, at.G + 1)
                    a_(h2[at.s], ps[:, 2 + at.s, :], ACT.Identity, bias=b2col[:, l:l + 1]).then_inc(s_h2, 1)
                if live(2):
                    at = At(i, k, 2, l * NG)
                    act.wait_ge(s_p3, at.G + 3)
                    act.wait_ge(s_p4, at.G + 1)
                    a_(h2e[at.s], ps[:, 4 + at.s, :], ACT.Copy).then_inc(s_h2e, 1)

            def clear(l, i):
                if l < 2:
                    for t in (2 * l, 2 * l + 1):
                        act.dma_start(rel_tab[t][bass.ds(i * ZR, ZR), :].rearrange("(p r) w -> p (r w)", p=ZP),
                                      zeros[0:ZP, :]).then_inc(s_ztab, 16)

            for q in (s_h1, s_h2, s_h2e):
                act.sem_inc(q, 2)
            for l in range(3):
                b_chunk(l, 0)
                parts(l * NC, 0)
                with loop(act, 1, NC) as c:
                    b_chunk(l, c)
                    parts(l * NC + c, c)
                if l == 0:
                    act.wait_ge(s_pv, PV_CONST)
                    act.wait_ge(s_w, 13 * 16)
                for k in range(SL):
                    step(l, 0, k, lo=True)
                clear(l, 0)
                with loop(act, 1, NI) as i:
                    for _, k in body_groups(i):
                        step(l, i, k)
                    clear(l, i)
                for k in range(SL - 1):
                    step(l, NI, k, hi=True)

            with loop(act, 0, NC) as c:
                act.wait_ge(s_y, c + 1)
                a_(dev, mv[:, :, 1], ACT.Sqrt, bias=eps[:, :]).then_inc(s_dev, 1)
                parts(3 * NC + c, c)
            for q in (s_rs, s_rm):
                act.sem_inc(q, 2)

            def rel_step(i, k, lo=False, hi=False):
                live = lambda d: not ((lo and k < d) or (hi and k >= d))
                if live(0):
                    at = At(i, k)
                    act.wait_ge(s_ra, at.g + 3)
                    act.wait_ge(s_rb, at.g + 1)
                    a_(spread[at.s], ps[:, at.s, :], ACT.Copy).then_inc(s_rs, 1)
                if live(1):
                    at = At(i, k, 1)
                    if not (isinstance(at.g, int) and at.g < SL):
                        for t in range(GT):
                            act.wait_ge(s_add[t], 16 * (at.g - SL + 1))
                            tick()
                    act.wait_ge(s_rb, at.g + 3)
                    a_(msg[at.k][:, :, 0:P], ps[:, 2 + at.s, :].rearrange("p (t f) -> p t f", f=P), ACT.Copy)
                    a_(msg[at.k][:, :, P], ps[:, 4 + at.s, 0:GT], ACT.Copy).then_inc(s_rm, 1)

            for k in range(SL):
                rel_step(0, k, lo=True)
            for k in range(SL):
                rel_step(1, k)
            with loop(act, 2, NI) as i:
                for _, k in body_groups(i):
                    rel_step(i, k)
            rel_step(NI, 0, hi=True)
            act.sem_inc(s_fa, 2)

            def turned(b, s):
                act.wait_ge(s_ft, b + 3)
                act.wait_ge(s_fm, b + 1)
                a_(mean_t[s], flat[:, s * 1024:(s + 1) * 1024], ACT.Copy).then_inc(s_fa, 1)

            def means(b, s):
                act.wait_ge(s_tot, b + 3)
                act.wait_ge(s_ft, b + 1)
                tick()
                sums = sum01[s].rearrange("p (r w) -> p r w", r=R)
                for r in range(R):
                    last = a_(mean[s][:, r, :], sums[:, r, 0:P], ACT.Copy, scale=inv_cnt[s][:, r:r + 1])
                last.then_inc(s_sc, 1)

            def root(b, s):
                act.wait_ge(s_fy, b + 3)
                a_(o_dev[s], o_mv[s][:, 1:2], ACT.Sqrt, bias=eps[:, :]).then_inc(s_fd, 1)

            def last_step(b, s, low=False):
                if not low:
                    root(b - 1, 1 - s)
                if not isinstance(b, int) or b + 1 < NB:
                    means(b + 1, 1 - s)
                if not isinstance(b, int) or b < NB:
                    turned(b, s)

            act.sem_inc(s_sc, 2)
            means(0, 0)
            last_step(0, 0, low=True)
            last_step(1, 1)
            with loop(act, 1, NB // 2 - 1) as i:
                for s in range(2):
                    last_step(2 * i + s, s)
            for b in range(NB - 2, NB + 1):
                last_step(b, b % 2)

        @block.vector
        def _(dve):
            v = nc.vector
            tick = lambda: dve.sem_inc(s_tick["dve"], 1)
            done = [0]

            def pv(ins):
                done[0] += 1
                ins.then_inc(s_pv, 1)
                dve.wait_ge(s_pv, done[0])
                return done[0]

            dve.wait_ge(s_gp, GP_ALL)
            pv(v.tensor_scalar(ident[:, :], iota[:, :], pidx[:, 0:1], None, ALU.is_equal))
            pv(v.tensor_scalar(below[:, :], iota[:, :], pidx[:, 0:1], None, ALU.is_lt))
            pv(v.tensor_scalar(upto_mat, iota[:, :], pidx[:, 0:1], None, ALU.is_ge))
            pv(v.tensor_scalar(tmp_a, iota[:, :], 1.0, pidx[:, 0:1], ALU.add, ALU.is_equal))
            pv(v.tensor_tensor(step_mat, tmp_a, ident[:, :], ALU.subtract))
            pv(v.memset(ones[:, :], 1.0))
            pv(v.memset(ones_b[:, :], 1.0))
            pv(v.memset(eps[:, :], EPS))
            pv(v.memset(zeros[:, :], 0.0))
            pv(v.tensor_scalar(trash_col[:, :], pidx[:, :], float(TRASH), None, ALU.add))
            pv(v.tensor_scalar(trash_row, iota[:, :], float(TRASH), None, ALU.add))
            assert pv(v.memset(tab_a[:, NB * 3 * P:], 0.0)) == PV_CONST
            dve.wait_ge(s_last, 16)
            pv(v.tensor_copy(last_f, last_i))
            for c in range(LC):
                n = pv(v.tensor_scalar(full[:, c, :], thr_row, last_f[:, c:c + 1], None, ALU.is_gt))
            assert n == PV_FULL
            dve.wait_ge(s_pt, 1)
            pv(v.tensor_copy(cnt0, ps[0:NBT, 0, 0:1]))
            assert pv(v.tensor_scalar(win_at, cnt0, float(P), 1.0, ALU.mult, ALU.add)) == PV_WIN0
            dve.wait_ge(s_row0, 16)
            pv(v.tensor_copy(win_f, win_i))
            pv(v.tensor_scalar(win_f, win_f, thr_col, None, ALU.is_lt))
            pv(v.tensor_reduce(cnt1, win_f, AX_X, ALU.add))
            assert pv(v.scalar_tensor_tensor(out=start, in0=cnt0, scalar=float(P), in1=cnt1,
                                             op0=ALU.mult, op1=ALU.add)) == PV_START
            dve.wait_ge(s_pt, 2)
            pv(v.tensor_copy(deg_b, ps[0:NB, 1, 0:1]))
            pv(v.tensor_scalar(nt_i, deg_b, float(P - 1), None, ALU.add))
            pv(v.tensor_scalar(nt_i, nt_i, 7, None, ALU.arith_shift_right))
            assert pv(v.tensor_copy(nt_f, nt_i)) == PV_TILES
            dve.wait_ge(s_pt, 3)
            pv(v.tensor_copy(upto, ps[0:NB, 2, 0:1]))
            pv(v.memset(shift2[:, 0:1], 1.0))
            pv(v.scalar_tensor_tensor(out=shift2[:, 1:2], in0=nt_f, scalar=-float(P), in1=deg_b,
                                      op0=ALU.mult, op1=ALU.add))
            assert pv(v.tensor_scalar(past, iota_j, upto, None, ALU.is_ge)) == PV_PAST
            dve.wait_ge(s_pt, 4)
            found = ps[:, 3, 0:2 * NQ].rearrange("p (q f) -> p q f", f=2)
            pv(v.tensor_copy(blk_f, found[:, :, 0]))
            pv(v.tensor_scalar(base_f, blk_f, float(P), None, ALU.mult))
            pv(v.tensor_tensor(from_f, found[:, :, 1], jbase, ALU.add))
            pv(v.tensor_scalar(from_i, from_f, float(E), None, ALU.min))
            assert pv(v.tensor_copy(blk_i, blk_f)) == PV_BLK
            dve.wait_ge(s_w, 13 * 16)
            for l in range(3):
                pv(v.tensor_tensor(wd[:, l], w1[:, l, 0], w1[:, l, 1], ALU.subtract))
            dve.wait_ge(s_pt, 5)
            pv(v.tensor_copy(wr_t[:, :, :].rearrange("p r j -> p (r j)"), flat[:, 2048:2048 + R * P]))
            def edge_step(i):
                for s in range(2):
                    q = 2 * i + s
                    n = [0]

                    def ch(ins):
                        n[0] += 1
                        ins.then_inc(s_wv, 1)
                        dve.wait_ge(s_wv, q * WVT + n[0])

                    ch(v.tensor_copy(win_base[s], base_f[:, bass.ds(q, 1)]))
                    v.tensor_copy(win_from[s], from_i[:, bass.ds(q, 1)]).then_inc(s_from, 1)
                    after(dve, s_store[s], 80 * i)
                    tick()
                    dve.wait_ge(s_win[s], 48 * (i + 1))
                    tick()
                    ch(v.tensor_copy(dst_f, dst_w[s]))
                    ch(v.tensor_copy(src_f, src_w[s]))
                    ch(v.tensor_scalar(loc_f, dst_f[:, 1:P + 1], win_base[s], float(OUT_OF_BLOCK),
                                       ALU.subtract, ALU.min))
                    ch(v.tensor_tensor(tmp_a, dst_f[:, 1:P + 1], dst_f[:, 0:P], ALU.not_equal))
                    ch(v.tensor_scalar(tmp_b, tmp_a, -2.0, 1.0, ALU.mult, ALU.add))
                    ch(v.tensor_scalar(cut_b[s], tmp_b, BIG, None, ALU.mult))
                    ch(v.tensor_tensor(tmp_a, dst_f[:, 1:P + 1], dst_f[:, 2:P + 2], ALU.not_equal))
                    ch(v.tensor_scalar(tmp_b, tmp_a, -float(OUT_OF_BLOCK), float(OUT_OF_BLOCK), ALU.mult, ALU.add))
                    ch(v.tensor_tensor(end_f, tmp_b, loc_f, ALU.max))
                    ch(v.tensor_copy(loc_b[s], loc_f))
                    ch(v.scalar_tensor_tensor(out=tmp_a, in0=src_f, scalar=float(R), in1=typ_w[s],
                                              op0=ALU.mult, op1=ALU.add))
                    ch(v.tensor_tensor(tmp_b, tmp_a, trash_row, ALU.subtract))
                    ch(v.scalar_tensor_tensor(out=tmp_c, in0=loc_f, scalar=float(P), in1=tmp_b,
                                              op0=ALU.is_lt, op1=ALU.mult))
                    ch(v.tensor_tensor(key_f, tmp_c, trash_row, ALU.add))
                    ch(v.tensor_copy(key_o[s], key_f))
                    assert n[0] == WV
                    dve.wait_ge(s_wt, q + 1)
                    tick()
                    ch(v.tensor_copy(src_o[s], ps[:, 6 + s, 0:P]))
                    v.tensor_copy(meta_o[s].rearrange("p (j f) -> p f j", f=3),
                                  ps[:, 6 + s, P:4 * P].rearrange("p (f j) -> p f j", f=3)).then_inc(s_wo, 1)
                    assert n[0] == WVT

            edge_step(0)
            with loop(dve, 1, NQ // 2) as i:
                edge_step(i)
            for s in range(2):
                dve.wait_ge(s_store[s], 80 * (NQ // 2))
            dve.wait_ge(s_blk, 32)
            dve.sem_inc(s_scan, 2)
            dve.sem_inc(s_ends, SL)
            dve.sem_inc(s_agg, GT)
            dve.sem_inc(s_af, 1)
            zdone = [0]

            def part_view(c, h):
                return tab_a[:, bass.ds(c * (CB * 3 * P), CB * 3 * P)].rearrange(
                    "p (b t f) -> p b t f", t=3, f=P)[:, :, h, :]

            blocked = lambda ap: ap.rearrange("p (b f) -> p b f", f=P)
            tv = [0]

            def guard(c, count, relu):
                def ch(ins, m):
                    ins.then_inc(s_tv, 1)
                    dve.wait_ge(s_tv, count + m)
                    tick()
                if relu:
                    ch(v.tensor_scalar(xs, agg[:, bass.ds(c * CB * P, CB * P)], 0.0, None, ALU.max), 1)
                else:
                    ch(v.tensor_copy(xs, agg[:, bass.ds(c * CB * P, CB * P)]), 1)
                ch(v.tensor_scalar(bad, xs, 0.0, 0.0, ALU.mult, ALU.not_equal), 2)
                v.copy_predicated(xs, bad, zeros[:, 0:CB * P]).then_inc(s_xs, 1)

            def lower_parts(cc, c):
                dve.wait_ge(s_hi, cc + 1)
                tick()
                v.tensor_tensor(blocked(afull), blocked(afull), part_view(c, 0), ALU.subtract).then_inc(s_re, 1)
                dve.wait_ge(s_mid, cc + 1)
                tick()
                v.tensor_tensor(part_view(c, 2), blocked(afull), part_view(c, 1), ALU.subtract).then_inc(s_lo, 1)

            def table_chunk(l, c, s=None):
                cc = l * NC + c
                if l == 0:
                    dve.wait_ge(s_xt, c + 1)
                    after(dve, s_tb, c)
                    tick()
                    v.tensor_copy(xs, flat[:, 3072:3072 + CB * P]).then_inc(s_xs, 1)
                    dve.sem_inc(s_xfree, 1)
                else:
                    dve.wait_ge(s_tb, cc)
                    tick()
                    guard(c, 2 * ((l - 1) * NC + c), relu=True)
                dve.wait_ge(s_ta, cc + 1)
                after(dve, s_lo, cc)
                tick()
                v.tensor_tensor(blocked(afull), blocked(flat[:, 0:CB * P]),
                                b1row[:, l:l + 1, :].to_broadcast([P, CB, P]), ALU.add).then_inc(s_af, 1)
                lower_parts(cc, c)

            def step(l, i, k, lo=False, hi=False):
                live = lambda d: not ((lo and k < d) or (hi and k >= d))
                if live(0):
                    at = At(i, k, 0, l * NG, l * NI)
                    dve.wait_ge(s_bc[at.k], 32 * (at.n + 1))
                    dve.wait_ge(s_p1, at.G + SL - 1)
                    v.tensor_scalar(hot_t[at.s], dst_bc[at.k], pidx[:, 0:1], None, ALU.is_equal).then_inc(s_hot, 1)
                if live(2):
                    at = At(i, k, 2, l * NG)
                    dve.wait_ge(s_h2, at.G + 3)
                    dve.wait_ge(s_p3, at.G + 1)
                    dve.wait_ge(s_scan, at.G + 2)
                    v.tensor_tensor_scan(scan[at.s], cut_bc[at.k], h2[at.s],
                                         scan[1 - at.s][:, GT * P - 1:GT * P], ALU.min, ALU.max).then_inc(s_scan, 1)
                    dve.wait_ge(s_p4, at.G + 1)
                    dve.wait_ge(s_meta[at.k], 16 * (at.i + l * NI + 1))
                    tick()
                    for t in range(GT):
                        last = v.tensor_scalar(ends[at.s][:, t, :], iota[:, :],
                                               meta[at.k][:, t, 0:1], None, ALU.is_equal)
                    last.then_inc(s_ends, 1)
                if live(4):
                    at = At(i, k, 4, l * NG)
                    _, blk = nc.values_load_multi_w_load_instructions(
                        blocks[0:1, bass.ds(at.g * GT, GT)], engines=[DVE_ENGINE], min_val=0, max_val=NB,
                        skip_runtime_bounds_check_because=WHY)
                    dve.wait_ge(s_p4, at.G + 3)
                    tick()
                    for t in range(GT):
                        dve.wait_ge(s_agg, GT * at.G + t + GT)
                        tick()
                        to = agg[:, bass.ds(blk[t] * P, P)]
                        v.tensor_tensor(to, ps[:, 6 + at.s, t * P:(t + 1) * P], to, ALU.add).then_inc(s_agg, 1)

            for l in range(3):
                table_chunk(l, 0)
                with loop(dve, 1, NC) as c:
                    table_chunk(l, c)
                dve.wait_ge(s_lo, NC * (l + 1))
                dve.wait_ge(s_tb, NC * (l + 1))
                dve.wait_ge(s_bd, 16 * NC * (l + 1))
                v.memset(scan[1][:, GT * P - 1:GT * P], 0.0).then_inc(s_zero, 1)
                v.memset(agg[:, :], 0.0).then_inc(s_zero, 1)
                dve.wait_ge(s_zero, 2 * (l + 1))
                for k in range(SL):
                    step(l, 0, k, lo=True)
                with loop(dve, 1, NI) as i:
                    for _, k in body_groups(i):
                        step(l, i, k)
                for k in range(SL):
                    step(l, NI, k, hi=True)
                dve.wait_ge(s_agg, GT * NG * (l + 1) + GT)

            def norm_chunk(i, s, extra=0):
                c = 2 * i + s
                cc = 3 * NC + c
                after(dve, s_mt, c)
                tick()
                guard(c, 2 * (2 * NC + c), relu=False)
                dve.wait_ge(s_mt, c + 1)
                dve.wait_ge(s_xin[s], 16 * (NC // 2 + 1) + 16 * (i + 1) - (16 if s == 0 else 0) + extra)
                dve.wait_ge(s_lo, cc)
                tick()
                m = [0]

                def ch(ins):
                    m[0] += 1
                    ins.then_inc(s_fv, 1)
                    dve.wait_ge(s_fv, c * NVC + m[0])
                    tick()

                ch(v.tensor_tensor(afull, flat[:, 0:CB * P], xin[s].rearrange("p b f -> p (b f)"), ALU.add))
                dve.sem_inc(s_xfree, 1)
                for b in range(CB):
                    last = v.bn_stats(st6[:, b, :], afull[:, b * P:(b + 1) * P])
                ch(last)
                for b in range(CB):
                    last = v.bn_aggr(mv[:, b, :], st6[:, b, :])
                last.then_inc(s_y, 1)
                dve.wait_ge(s_dev, c + 1)
                tick()
                ch(v.reciprocal(inv_dev, dev))
                after(dve, s_x1d, 16 * c)
                tick()
                for b in range(CB):
                    last = v.tensor_scalar(bout[:, b * P:(b + 1) * P], afull[:, b * P:(b + 1) * P],
                                           mv[:, b, 0:1], inv_dev[:, b:b + 1], ALU.subtract, ALU.mult)
                ch(last)
                last = v.tensor_copy(afull, bout)
                last.then_inc(s_af, 1)
                dve.sem_inc(s_x1, 1)
                assert m[0] == NVC
                lower_parts(cc, c)

            for s in range(2):
                norm_chunk(0, s)
            with loop(dve, 1, NC // 2 - 1) as i:
                for s in range(2):
                    norm_chunk(i, s)
            norm_chunk(NC // 2 - 1, 0)
            norm_chunk(NC // 2 - 1, 1, extra=16)
            dve.wait_ge(s_lo, NC * 4)
            dve.wait_ge(s_x1d, 16 * NC)
            dve.sem_inc(s_rh, 2)
            dve.sem_inc(s_rid, SL)

            def rel_group(i, k, lo):
                at = At(i, k)
                m = [0]

                def ch(ins):
                    m[0] += 1
                    ins.then_inc(s_rv, 1)
                    dve.wait_ge(s_rv, at.g * NVR + m[0])

                dve.wait_ge(s_rl[k], 32 * (i + 1))
                tick()
                dve.wait_ge(s_ra, at.g + 1)
                tick()
                for t in range(GT):
                    v.tensor_scalar(hot_e[at.s][:, t, :], iota[:, :], r_meta[k][:, t, 1:2], None,
                                    ALU.is_equal)
                    last = v.tensor_scalar(same[at.s][:, t, :], key_bc[k][:, t * P:(t + 1) * P],
                                           r_meta[k][:, t, 2:3], None, ALU.is_equal)
                last.then_inc(s_rh, 1)
                dve.wait_ge(s_rh, at.g + 3)
                tick()
                ch(v.tensor_tensor(earlier, same[at.s], below[:, :].unsqueeze(1).to_broadcast([P, GT, P]), ALU.mult))
                ch(v.tensor_reduce(rank, earlier, AX_X, ALU.add))
                ch(v.tensor_scalar(first, rank, 0.0, None, ALU.is_equal))
                ch(v.scalar_tensor_tensor(out=kept, in0=r_meta[k][:, :, 2], scalar=trash_col[:, 0:1],
                                          in1=first, op0=ALU.subtract, op1=ALU.mult))
                assert m[0] == NVR
                if not lo:
                    for t in range(GT):
                        dve.wait_ge(s_add[t], 16 * (at.g - SL + 1))
                        tick()
                v.tensor_scalar(r_row[k], kept, trash_col[:, 0:1], None, ALU.add).then_inc(s_rid, 1)

            for k in range(SL):
                rel_group(0, k, True)
            with loop(dve, 1, NI) as i:
                for _, k in body_groups(i):
                    rel_group(i, k, False)
            for t in range(K):
                dve.wait_ge(s_add[t], 16 * NG)
            dve.wait_ge(s_rb, NG + 2)
            dve.sem_inc(s_tot, 2)
            dve.sem_inc(s_fy, 2)

            def sums(i, s):
                b = 2 * i + s
                m = [0]

                def ch(ins):
                    m[0] += 1
                    ins.then_inc(s_fv, 1)
                    dve.wait_ge(s_fv, NC * NVC + b * NVB + m[0])
                    tick()

                dve.wait_ge(s_part[s], 16 * K * (i + 1))
                dve.wait_ge(s_sc, b + 1)
                tick()
                v.tensor_tensor(sum01[s], part[s][:, 0, :], part[s][:, 1, :], ALU.add).then_inc(s_01, 1)
                dve.wait_ge(s_01, b + 1)
                dve.wait_ge(s_23, b + 1)
                tick()
                ch(v.tensor_tensor(sum01[s], sum01[s], sum23[s], ALU.add))
                ch(v.tensor_scalar(cnt[s], sum01[s].rearrange("p (r w) -> p r w", r=R)[:, :, P], 1.0, None, ALU.max))
                v.reciprocal(inv_cnt[s], cnt[s]).then_inc(s_tot, 1)
                assert m[0] == NVB

            def variance(b, s):
                dve.wait_ge(s_fm, b + 3)
                tick()

                def ch(ins, count):
                    ins.then_inc(s_norm, 1)
                    dve.wait_ge(s_norm, b * NVN + count)
                    tick()

                ch(v.scalar_tensor_tensor(out=y_in[s], in0=ps[:, 4 + s, 0:P], scalar=0.0, in1=x1_in[s],
                                          op0=ALU.max, op1=ALU.add), 1)
                ch(v.bn_stats(o_st6[s], y_in[s]), 2)
                v.bn_aggr(o_mv[s], o_st6[s]).then_inc(s_fy, 1)

            def result(b, i, s):
                dve.wait_ge(s_fd, b + 1)
                tick()
                v.reciprocal(o_inv[s], o_dev[s]).then_inc(s_fi, 1)
                dve.wait_ge(s_fi, b + 1)
                tick()
                after(dve, s_out[s], 16 * i)
                v.tensor_scalar(y_out[s], y_in[s], o_mv[s][:, 0:1], o_inv[s][:, 0:1], ALU.subtract, ALU.mult
                                ).then_inc(s_fo, 1)

            def last_step(i, s, low=False):
                b = 2 * i + s
                if not isinstance(b, int) or b + 1 < NB:
                    sums(*((i, 1) if s == 0 else (i + 1, 0)))
                if not low:
                    result(b - 1, *((i - 1, 1) if s == 0 else (i, 0)))
                if not isinstance(b, int) or b < NB:
                    dve.wait_ge(s_x1in[s], 16 * (i + 1))
                    tick()
                    variance(b, s)

            sums(0, 0)
            last_step(0, 0, low=True)
            last_step(0, 1)
            last_step(1, 0)
            last_step(1, 1)
            with loop(dve, 2, NB // 2 - 1) as i:
                for s in range(2):
                    last_step(i, s)
            last_step(NB // 2 - 1, 0)
            last_step(NB // 2 - 1, 1)
            last_step(NB // 2, 0)


_LAYERS = ("in", "hid", "out")
_INS = ["x", "src", "dst", "edge_type_8"] + [
    f"L0_gnn_{p}_{l}" for l in _LAYERS for p in ("W1", "b1", "W2", "b2")] + ["L1_gnn_weights"]


def kernel(**inputs):
    import numpy as _np
    import concourse.bacc as _bacc
    from concourse import mybir as _mybir
    from concourse.bass_utils import run_bass_kernel_spmd as _run

    nc = _bacc.Bacc("TRN2", target_bir_lowering=False, num_devices=1)
    arrays, aps = {}, {}
    for name in _INS:
        a = _np.ascontiguousarray(inputs[name])
        arrays[f"in_{name}"] = a
        aps[name] = nc.dram_tensor(f"in_{name}", a.shape, _mybir.dt.from_np(a.dtype), kind="ExternalInput").ap()
    n, c = inputs["x"].shape
    out = nc.dram_tensor("out_0", (n, c), _mybir.dt.float32, kind="ExternalOutput").ap()
    params = [tuple(aps[f"L0_gnn_{p}_{l}"] for p in ("W1", "b1", "W2", "b2")) for l in _LAYERS]
    gnn_kernel(nc, aps["x"], aps["src"], aps["dst"], aps["edge_type_8"], params, aps["L1_gnn_weights"], out)
    r = _run(nc, [arrays], core_ids=[0])
    return r.results[0]["out_0"]
```

```python
from contextlib import ExitStack

import numpy as np
import concourse.bass as bass
from concourse import mybir
from concourse.alu_op_type import AluOpType as ALU

F32 = mybir.dt.float32
I32 = mybir.dt.int32
BF16 = mybir.dt.bfloat16
ACT = mybir.ActivationFunctionType
AX_X = mybir.AxisListType.X
PE_ENGINE = mybir.EngineType.PE
DVE_ENGINE = mybir.EngineType.DVE

P = 128
EPS = 1e-5
BIG = 3.3895313892515355e38
OUT_OF_BLOCK = 255
GT = 4
SL = 4
CB = 7
K = 4
WHY = "the block numbers are clamped to the table when they are made"

def gnn_kernel(nc, x, src, dst, etype, params, w_rel, out):
    N, C = x.shape
    E = dst.shape[0]
    R = w_rel.shape[0]
    assert C == P
    NB = -(-N // P)
    NT = -(-((E + NB * (P - 1)) // P) // (GT * SL)) * GT * SL
    NG = NT // GT
    NI = NG // SL
    NQ = -(-NT // P)
    NTP = NQ * P
    ER = -(-(E + 1) // P)
    LC = -(-ER // P)
    ERP = P * LC
    NC = NB // CB
    NBT = NB + 1
    LAST = N - (NB - 1) * P
    NO_BLOCK = (NB + 2) * P
    TRASH = R * N
    W = P + 1
    ZR = GT * 12 * -(-(TRASH + P) // (NI * GT * 12))
    TR = ZR * NI
    assert NB % CB == 0 and NB + 1 <= P and NB % 2 == 0

    ZP = 48
    assert ZR % ZP == 0

    TAIL = ERP * P + P - E
    dst_pad = nc.dram_tensor("dst_pad", (1 + E + TAIL,), I32).ap()
    src_pad = nc.dram_tensor("src_pad", (E + TAIL,), I32).ap()
    typ_pad = nc.dram_tensor("typ_pad", (E + TAIL,), I32).ap()
    row_dst = nc.dram_tensor("row_dst", (NTP, P), BF16).ap()
    row_cut = nc.dram_tensor("row_cut", (NTP, P), BF16).ap()
    row_key = nc.dram_tensor("row_key", (NTP, P), F32).ap()
    col_src = nc.dram_tensor("col_src", (P, NTP), I32).ap()
    col_meta = nc.dram_tensor("col_meta", (P, NTP, 3), F32).ap()
    blk_row = nc.dram_tensor("blk_row", (NQ, P), I32).ap()
    tab_b = nc.dram_tensor("tab_b", (NB * P, P), F32).ap()
    rel_tab = [nc.dram_tensor(f"rel_tab{k}", (TR, W), F32).ap() for k in range(K)]

    with ExitStack() as ctx:
        def sb(name, shape, dt=F32):
            return ctx.enter_context(nc.sbuf_tensor(name, shape, dt))

        def sem(name):
            return ctx.enter_context(nc.semaphore(name))

        ps = ctx.enter_context(nc.psum_tensor("ps", [P, 8, 512], F32))
        flat = ps[:, :, :].rearrange("p b c -> p (b c)")
        agg = sb("agg", [P, NBT * P])
        tab_a = sb("tab_a", [P, NBT * 3 * P], BF16)
        blocks = sb("blocks", [1, NTP], I32)
        ident = sb("ident", [P, P])
        iota = sb("iota", [P, P])
        below = sb("below", [P, P])
        pidx = sb("pidx", [P, 1])
        ones = sb("ones", [P, 1])
        ones_b = sb("ones_b", [P, 1], BF16)
        eps = sb("eps", [P, 1])
        zeros = sb("zeros", [P, ZR // ZP * W])
        trash_col = sb("trash_col", [P, 1])
        w1 = sb("w1", [P, 3, 2, P])
        w2 = sb("w2", [P, 3, P])
        wd = sb("wd", [P, 3, P])
        b1row = sb("b1row", [P, 3, P])
        b2col = sb("b2col", [P, 3])
        wr_t = sb("wr_t", [P, R, P])
        WORK = 10240
        work = sb("work", [P, WORK])

        class Area:
            def __init__(self, base, size):
                self.base, self.size, self.at = base, size, 0

            def cut(self, n, dt=F32, parts=P):
                words = n if dt != BF16 else n // 2
                ap = self.base[0:parts, self.at:self.at + words]
                self.at += words
                assert self.at <= self.size, self.at
                return ap if dt == F32 else ap.bitcast(dt)

        a = Area(agg, NBT * P)
        pad_vals = a.cut(2 * TAIL + 1, I32, 1)
        wr_raw = a.cut(R * P).rearrange("p (r j) -> p r j", r=R)
        last_i = a.cut(LC, I32)
        last_f = a.cut(LC)
        thr_row = a.cut(NBT)
        thr_col = a.cut(1, F32, NBT)
        jbase = a.cut(NQ)
        full = a.cut(LC * NBT).rearrange("p (c b) -> p c b", c=LC)
        cnt0 = a.cut(1, F32, NBT)
        win_at = a.cut(1, I32, NBT)
        win_i = a.cut(P, I32, NBT)
        win_f = a.cut(P, F32, NBT)
        cnt1 = a.cut(1, F32, NBT)
        start = a.cut(1, F32, NBT)
        step_mat = a.cut(P)
        upto_mat = a.cut(P)
        deg_b = a.cut(1, F32, NB)
        nt_i = a.cut(1, I32, NB)
        nt_f = a.cut(1, F32, NB)
        upto = a.cut(1, F32, NB)
        shift2 = a.cut(2, F32, NB)
        iota_j = a.cut(NTP, F32, NB)
        past = a.cut(NTP, F32, NB)
        blk_f = a.cut(NQ)
        blk_i = a.cut(NQ, I32)
        base_f = a.cut(NQ)
        from_f = a.cut(NQ)
        from_i = a.cut(NQ, I32)
        trash_row = a.cut(P)
        win_from = [a.cut(1, I32) for _ in range(2)]
        win_base = [a.cut(1) for _ in range(2)]
        dst_w = [a.cut(P + 2, I32) for _ in range(2)]
        src_w = [a.cut(P, I32) for _ in range(2)]
        typ_w = [a.cut(P, I32) for _ in range(2)]
        dst_f = [a.cut(P + 2) for _ in range(2)]
        src_f = [a.cut(P) for _ in range(2)]
        loc_f = [a.cut(P) for _ in range(2)]
        end_f = [a.cut(P) for _ in range(2)]
        key_f = [a.cut(P) for _ in range(2)]
        starts = [a.cut(P) for _ in range(2)]
        signs = [a.cut(P) for _ in range(2)]
        stops = [a.cut(P) for _ in range(2)]
        no_end = [a.cut(P) for _ in range(2)]
        raw_key = [a.cut(P) for _ in range(2)]
        key_d = [a.cut(P) for _ in range(2)]
        kept_d = [a.cut(P) for _ in range(2)]
        loc_b = [a.cut(P, BF16) for _ in range(2)]
        cut_b = [a.cut(P, BF16) for _ in range(2)]
        src_o = [a.cut(P, I32) for _ in range(2)]

        a = Area(work, WORK)
        xin = [a.cut(CB * P).rearrange("p (b f) -> p b f", f=P) for _ in range(2)]
        xs = [a.cut(CB * P) for _ in range(2)]
        afull = [a.cut(CB * P) for _ in range(2)]
        bout = [a.cut(CB * P) for _ in range(2)]
        resid = bout
        bad = a.cut(CB * P, I32)
        st6 = a.cut(CB * 6).rearrange("p (b s) -> p b s", s=6)
        mv = [a.cut(CB * 2).rearrange("p (b s) -> p b s", s=2) for _ in range(2)]
        dev = [a.cut(CB) for _ in range(2)]
        inv_dev = a.cut(CB)
        meta_o = [a.cut(P * 3) for _ in range(2)]

        a = Area(work, WORK)
        idx = [a.cut(GT, I32) for _ in range(SL)]
        meta = [a.cut(GT * 3).rearrange("p (t f) -> p t f", f=3) for _ in range(SL)]
        dst_bc = [a.cut(GT * P, BF16) for _ in range(SL)]
        cut_bc = [a.cut(GT * P, BF16) for _ in range(SL)]
        rows = [a.cut(GT * P).rearrange("p (t f) -> p t f", f=P) for _ in range(SL)]
        hot_t = [a.cut(GT * P, BF16) for _ in range(2)]
        h1 = [a.cut(GT * P) for _ in range(2)]
        h2 = [a.cut(GT * P) for _ in range(2)]
        scan = [a.cut(GT * P) for _ in range(2)]
        h2e = [a.cut(GT * P) for _ in range(2)]
        ends = [a.cut(GT * P).rearrange("p (t n) -> p t n", n=P) for _ in range(2)]

        a = Area(work, WORK)
        r_meta = [a.cut(GT * 3).rearrange("p (t f) -> p t f", f=3) for _ in range(SL)]
        key_bc = [a.cut(GT * P) for _ in range(SL)]
        hot_e = [a.cut(GT * P, BF16).rearrange("p (t n) -> p t n", n=P) for _ in range(2)]
        same = [a.cut(GT * P, BF16).rearrange("p (t n) -> p t n", n=P) for _ in range(2)]
        earlier = a.cut(GT * P).rearrange("p (t n) -> p t n", n=P)
        rank = a.cut(GT)
        first = a.cut(GT)
        kept = a.cut(GT)
        spread = [a.cut(GT * P, BF16) for _ in range(2)]
        msg = [a.cut(GT * W).rearrange("p (t f) -> p t f", f=W) for _ in range(SL)]
        r_row = [a.cut(GT, I32) for _ in range(SL)]

        a = Area(tab_a[:, :].bitcast(F32), NBT * 3 * P // 2)
        part = [a.cut(K * R * W).rearrange("p (k w) -> p k w", k=K) for _ in range(2)]
        sum01 = [a.cut(R * W) for _ in range(2)]
        sum23 = [a.cut(R * W) for _ in range(2)]
        a = Area(work, WORK)
        mean = [a.cut(R * P).rearrange("p (r f) -> p r f", r=R) for _ in range(2)]
        mean_t = [a.cut(R * P) for _ in range(2)]
        cnt = [a.cut(R) for _ in range(2)]
        inv_cnt = [a.cut(R) for _ in range(2)]
        y_in = [a.cut(P) for _ in range(2)]
        y_out = [a.cut(P) for _ in range(2)]
        o_st6 = [a.cut(6) for _ in range(2)]
        o_mv = [a.cut(2) for _ in range(2)]
        o_dev = [a.cut(1) for _ in range(2)]
        o_inv = [a.cut(1) for _ in range(2)]

        s_padd = sem("s_padd")
        s_pad = sem("s_pad")
        s_w = sem("s_w")
        s_last = sem("s_last")
        s_row0 = sem("s_row0")
        s_gp = sem("s_gp")
        s_pv = sem("s_pv")
        s_pt = sem("s_pt")
        s_blk = sem("s_blk")
        s_from = sem("s_from")
        s_win = [sem(f"s_win{k}") for k in range(2)]
        s_wv = sem("s_wv")
        s_wt = sem("s_wt")
        s_wo = sem("s_wo")
        s_store = [sem(f"s_store{k}") for k in range(2)]
        s_xin = [sem(f"s_xin{k}") for k in range(2)]
        s_xt = sem("s_xt")
        s_xc = sem("s_xc")
        s_xs = sem("s_xs")
        s_ta = sem("s_ta")
        s_tb = sem("s_tb")
        s_af = sem("s_af")
        s_hi = sem("s_hi")
        s_re = sem("s_re")
        s_mid = sem("s_mid")
        s_lo = sem("s_lo")
        s_bf = sem("s_bf")
        s_bd = [sem(f"s_bd{k}") for k in range(2)]
        s_tv = sem("s_tv")
        s_idx = [sem(f"s_idx{k}") for k in range(SL)]
        s_meta = [sem(f"s_meta{k}") for k in range(SL)]
        s_bc = [sem(f"s_bc{k}") for k in range(SL)]
        s_rows = [sem(f"s_rows{k}") for k in range(SL)]
        s_hot = sem("s_hot")
        s_p1 = sem("s_p1")
        s_h1 = sem("s_h1")
        s_p2 = sem("s_p2")
        s_h2 = sem("s_h2")
        s_scan = sem("s_scan")
        s_p3 = sem("s_p3")
        s_h2e = sem("s_h2e")
        s_ends = sem("s_ends")
        s_p4 = sem("s_p4")
        s_agg = sem("s_agg")
        s_zero = sem("s_zero")
        s_ztab = sem("s_ztab")
        s_tick = {e: sem(f"s_tick_{e}") for e in ("pool", "dve", "act", "sp")}
        s_mt = sem("s_mt")
        s_res = sem("s_res")
        s_y = sem("s_y")
        s_dev = sem("s_dev")
        s_rl = [sem(f"s_rl{k}") for k in range(SL)]
        s_rh = sem("s_rh")
        s_rv = sem("s_rv")
        s_rid = sem("s_rid")
        s_ra = sem("s_ra")
        s_rs = sem("s_rs")
        s_rb = sem("s_rb")
        s_rm = sem("s_rm")
        s_add = [sem(f"s_add{k}") for k in range(K)]
        s_landed = sem("s_landed")
        s_part = [sem(f"s_part{k}") for k in range(2)]
        s_01 = sem("s_01")
        s_23 = sem("s_23")
        s_fv = sem("s_fv")
        s_tot = sem("s_tot")
        s_sc = sem("s_sc")
        s_ft = sem("s_ft")
        s_fa = sem("s_fa")
        s_fm = sem("s_fm")
        s_fy = sem("s_fy")
        s_fd = sem("s_fd")
        s_fo = sem("s_fo")
        s_out = [sem(f"s_out{k}") for k in range(2)]
        s_fi = sem("s_fi")
        s_norm = sem("s_norm")

        GP_PAD, GP_ALL = 3, 9
        PV_CONST = 12
        PV_FULL = PV_CONST + 2
        PV_WIN0 = PV_FULL + 2
        PV_START = PV_WIN0 + 4
        PV_TILES = PV_START + 4
        PV_PAST = PV_TILES + 4
        PV_BLK = PV_PAST + 5
        WV = 4
        NVC = 2
        NVR = 4
        NVB = 2
        NVN = 2

        class At:
            def __init__(self, i, k, d=0, first_group=0, first_pass=0):
                self.k = (k - d) % SL
                self.s = (k - d) % 2
                self.i = i + (k - d) // SL
                self.g = self.i * SL + self.k
                self.G = self.g + first_group
                self.n = self.i + first_pass

        def loop(eng, first, end):
            return nc.Fori(first, end, engines=[eng.engine], hint_back_edge=True)

        def after(eng, semaphore, value):
            if not (isinstance(value, int) and value <= 0):
                eng.wait_ge(semaphore, value)

        def blocked(ap):
            return ap.rearrange("p (b f) -> p b f", f=P)

        def part_view(c, h):
            return tab_a[:, bass.ds(c * (CB * 3 * P), CB * 3 * P)].rearrange(
                "p (b t f) -> p b t f", t=3, f=P)[:, :, h, :]

        def chunk_of(ap, c):
            return ap[:, bass.ds(c * CB * P, CB * P)]

        def body_groups(i):
            return [(i, k) for k in range(SL)]

        block = ctx.enter_context(nc.Block())

        @block.sync
        def _(sp):
            tick = lambda: sp.sem_inc(s_tick["sp"], 1)
            sp.dma_start(dst_pad[1:1 + E], dst).then_inc(s_padd, 16)
            sp.wait_ge(s_gp, GP_PAD)
            as_row = lambda v: v.rearrange("(a n) -> a n", a=1)
            sp.dma_start(as_row(dst_pad[0:1]), pad_vals[:, 2 * TAIL:2 * TAIL + 1]).then_inc(s_padd, 16)
            sp.dma_start(as_row(dst_pad[1 + E:1 + E + TAIL]), pad_vals[:, 0:TAIL]).then_inc(s_padd, 16)
            sp.wait_ge(s_padd, 3 * 16)
            with nc.allow_non_contiguous_dma(reason="the last edge of each row of 128, once"):
                sp.dma_start(last_i, dst_pad[P:P + ERP * P].rearrange("(p c e) -> p c e", c=LC, e=P)[:, :, 0]
                             ).then_inc(s_last, 16)
            sp.dma_start(src_pad[0:E], src).then_inc(s_pad, 16)
            sp.dma_start(typ_pad[0:E], etype).then_inc(s_pad, 16)
            sp.dma_start(as_row(src_pad[E:E + TAIL]), pad_vals[:, TAIL:2 * TAIL]).then_inc(s_pad, 16)
            sp.dma_start(as_row(typ_pad[E:E + TAIL]), pad_vals[:, TAIL:2 * TAIL]).then_inc(s_pad, 16)
            for l in range(3):
                W1, b1, W2, b2 = params[l]
                sp.dma_start(w1[:, l], W1.rearrange("(h i) o -> i h o", h=2)).then_inc(s_w, 16)
                sp.dma_start(w2[:, l], W2).then_inc(s_w, 16)
                sp.dma_start(b1row[:, l], as_row(b1).to_broadcast([P, P])).then_inc(s_w, 16)
                with nc.allow_non_contiguous_dma(reason="a bias as a column, once"):
                    sp.dma_start(b2col[:, l:l + 1], b2.rearrange("(n a) -> n a", a=1)).then_inc(s_w, 16)
            sp.dma_start(wr_raw, w_rel.rearrange("r i j -> i r j")).then_inc(s_w, 16)
            sp.wait_ge(s_pv, PV_BLK)
            with nc.allow_non_contiguous_dma(reason="the tiles' blocks, once"):
                sp.dma_start(blk_row.rearrange("q p -> p q"), blk_i).then_inc(s_blk, 16)
            sp.wait_ge(s_blk, 16)
            sp.dma_start(blocks[:, :], blk_row.rearrange("q p -> (q p)").rearrange("(a n) -> a n", a=1)
                         ).then_inc(s_blk, 16)
            with loop(sp, 0, NQ // 2) as i:
                sp.wait_ge(s_wo, i + 1)
                tick()
                for s in range(2):
                    q = 2 * i + s
                    sp.dma_start(row_dst[bass.ds(q * P, P), :], loc_b[s]).then_inc(s_store[s], 16)
                    sp.dma_start(row_cut[bass.ds(q * P, P), :], cut_b[s]).then_inc(s_store[s], 16)
                    sp.dma_start(row_key[bass.ds(q * P, P), :], key_f[s]).then_inc(s_store[s], 16)
                    sp.dma_start(col_meta[:, bass.ds(q * P, P), :].rearrange("p j f -> p (j f)"),
                                 meta_o[s]).then_inc(s_store[s], 16)
                    sp.dma_start(col_src[:, bass.ds(q * P, P)], src_o[s]).then_inc(s_store[s], 16)

            def x_chunk(i, s, free, whole=True):
                c = 2 * i + s
                sp.wait_ge(free, c + 1)
                tick()
                if whole:
                    sp.dma_start(xin[s], x[bass.ds(c * CB * P, CB * P), :].rearrange("(b p) f -> p b f", p=P)
                                 ).then_inc(s_xin[s], 16)
                else:
                    c0 = (NC - 1) * CB * P
                    sp.dma_start(xin[s][:, 0:CB - 1, :],
                                 x[c0:c0 + (CB - 1) * P, :].rearrange("(b p) f -> p b f", p=P)
                                 ).then_inc(s_xin[s], 16)
                    sp.dma_start(xin[s][0:LAST, CB - 1, :], x[c0 + (CB - 1) * P:N, :]).then_inc(s_xin[s], 16)

            def store_b(l, i, s):
                c = 2 * i + s
                sp.wait_ge(s_bf, l * NC + c + 2)
                tick()
                sp.dma_start(tab_b[bass.ds(c * CB * P, CB * P), :].rearrange("(b p) f -> p b f", p=P),
                             bout[s].rearrange("p (b f) -> p b f", f=P)).then_inc(s_bd[s], 16)

            for l in range(3):
                if l == 0:
                    for s in range(2):
                        x_chunk(0, s, s_xt)
                    with loop(sp, 0, NC // 2 - 2) as i:
                        for s in range(2):
                            x_chunk(i + 1, s, s_xt)
                            store_b(0, i, s)
                    x_chunk(NC // 2 - 1, 0, s_xt)
                    store_b(0, NC // 2 - 2, 0)
                    x_chunk(NC // 2 - 1, 1, s_xt, whole=False)
                    store_b(0, NC // 2 - 2, 1)
                    for s in range(2):
                        store_b(0, NC // 2 - 1, s)
                else:
                    with loop(sp, 0, NC // 2) as i:
                        for s in range(2):
                            store_b(l, i, s)
                sp.wait_ge(s_lo, NC * (l + 1) + 2)
                for s in range(2):
                    sp.wait_ge(s_bd[s], 8 * NC * (l + 1))
                if l == 0:
                    for s in range(2):
                        sp.wait_ge(s_store[s], 80 * (NQ // 2))
                with loop(sp, 0, NI) as i:
                    for _, k in body_groups(i):
                        at = At(i, k, 0, l * NG, l * NI)
                        sp.wait_ge(s_p1, at.G + 1)
                        tick()
                        sp.dma_start(idx[k], col_src[:, bass.ds(at.g * GT, GT)]).then_inc(s_idx[k], 16)
                        sp.wait_ge(s_ends, at.G + 1)
                        tick()
                        sp.dma_start(meta[k], col_meta[:, bass.ds(at.g * GT, GT), :]).then_inc(s_meta[k], 16)
                        sp.dma_start(dst_bc[k], row_dst[bass.ds(at.g * GT, GT), :].rearrange("t e -> (t e)")
                                     .partition_broadcast(P)).then_inc(s_bc[k], 16)
                        sp.dma_start(cut_bc[k], row_cut[bass.ds(at.g * GT, GT), :].rearrange("t e -> (t e)")
                                     .partition_broadcast(P)).then_inc(s_bc[k], 16)
            sp.wait_ge(s_agg, GT * NG * 3 + GT)
            for s in range(2):
                x_chunk(0, s, s_res)
            with loop(sp, 1, NC // 2 - 1) as i:
                for s in range(2):
                    x_chunk(i, s, s_res)
            x_chunk(NC // 2 - 1, 0, s_res)
            x_chunk(NC // 2 - 1, 1, s_res, whole=False)
            sp.wait_ge(s_lo, NC * 4 + 2)
            with loop(sp, 0, NI) as i:
                for _, k in body_groups(i):
                    at = At(i, k)
                    sp.wait_ge(s_rid, at.g + 1)
                    tick()
                    sp.dma_start(r_meta[k], col_meta[:, bass.ds(at.g * GT, GT), :]).then_inc(s_rl[k], 16)
                    sp.dma_start(key_bc[k], row_key[bass.ds(at.g * GT, GT), :].rearrange("t e -> (t e)")
                                 .partition_broadcast(P)).then_inc(s_rl[k], 16)
            for t in range(K):
                sp.wait_ge(s_add[t], 16 * NG)

            def load_parts(b, s):
                after(sp, s_01, b - 1)
                after(sp, s_23, b - 1)
                tick()
                for k in range(K):
                    view = rel_tab[k][0:R * N, :].rearrange("(n r) w -> n (r w)", r=R)
                    if isinstance(b, int) and b == NB - 1:
                        sp.dma_start(part[s][0:LAST, k, :], view[b * P:N, :]).then_inc(s_part[s], 16)
                    else:
                        sp.dma_start(part[s][:, k, :], view[bass.ds(b * P, P), :]).then_inc(s_part[s], 16)

            def store_out(b, s):
                sp.wait_ge(s_fo, b + 1)
                tick()
                if isinstance(b, int) and b == NB - 1:
                    sp.dma_start(out[b * P:N, :], y_out[s][0:LAST, :]).then_inc(s_out[s], 16)
                else:
                    sp.dma_start(out[bass.ds(b * P, P), :], y_out[s]).then_inc(s_out[s], 16)

            def last_step(b, s):
                if not isinstance(b, int) or b + 2 < NB:
                    load_parts(b + 2, s)
                if not isinstance(b, int) or b >= 3:
                    store_out(b - 3, 1 - s)

            load_parts(0, 0)
            load_parts(1, 1)
            for b in range(4):
                last_step(b, b % 2)
            with loop(sp, 2, NB // 2 - 2) as i:
                for s in range(2):
                    last_step(2 * i + s, s)
            for b in range(NB - 4, NB + 3):
                last_step(b, b % 2)
            for s in range(2):
                sp.wait_ge(s_out[s], 16 * (NB // 2))

        @block.gpsimd
        def _(pool):
            g = nc.gpsimd
            tick = lambda: pool.sem_inc(s_tick["pool"], 1)
            g.memset(pad_vals[:, 0:TAIL], NO_BLOCK).then_inc(s_gp, 1)
            g.memset(pad_vals[:, TAIL:2 * TAIL], 0).then_inc(s_gp, 1)
            g.memset(pad_vals[:, 2 * TAIL:2 * TAIL + 1], -1).then_inc(s_gp, 1)
            exact = dict(allow_small_or_imprecise_dtypes=True)
            g.iota(iota[:, :], [[1, P]], base=0, channel_multiplier=0, **exact).then_inc(s_gp, 1)
            g.iota(pidx[:, :], [[0, 1]], base=0, channel_multiplier=1, **exact).then_inc(s_gp, 1)
            g.iota(thr_row, [[P, NBT]], base=0, channel_multiplier=0, **exact).then_inc(s_gp, 1)
            g.iota(thr_col, [[0, 1]], base=0, channel_multiplier=P, **exact).then_inc(s_gp, 1)
            g.iota(jbase, [[P * P, NQ]], base=0, channel_multiplier=P, **exact).then_inc(s_gp, 1)
            g.iota(iota_j, [[1, NTP]], base=0, channel_multiplier=0, **exact).then_inc(s_gp, 1)
            as_elements = lambda v: v.rearrange("(a n) -> a n", a=1)
            pool.wait_ge(s_padd, 3 * 16)
            pool.wait_ge(s_pv, PV_WIN0)
            g.indirect_dma_start(win_i, None, as_elements(dst_pad),
                                 bass.IndirectOffsetOnAxis(ap=win_at, axis=1)).then_inc(s_row0, 16)
            pool.wait_ge(s_pad, 4 * 16)
            with loop(pool, 0, NQ // 2) as i:
                pool.wait_ge(s_from, i + 1)
                tick()
                for s in range(2):
                    for to, of in ((dst_w[s], dst_pad), (src_w[s], src_pad), (typ_w[s], typ_pad)):
                        g.indirect_dma_start(to, None, as_elements(of),
                                             bass.IndirectOffsetOnAxis(ap=win_from[s], axis=1)
                                             ).then_inc(s_win[s], 16)

            def low_parts(l):
                with loop(pool, 0, NC // 2) as i:
                    for s in range(2):
                        c = 2 * i + s
                        pool.wait_ge(s_mid, l * NC + c + 1)
                        tick()
                        g.tensor_tensor(part_view(c, 2), blocked(afull[s]), part_view(c, 1), ALU.subtract
                                        ).then_inc(s_lo, 1)

            pool.sem_inc(s_lo, 2)
            for l in range(3):
                low_parts(l)
                for s in range(2):
                    pool.wait_ge(s_bd[s], 8 * NC * (l + 1))
                pool.wait_ge(s_lo, NC * (l + 1) + 2)
                with loop(pool, 0, NI) as i:
                    for _, k in body_groups(i):
                        at = At(i, k, 0, l * NG, l * NI)
                        pool.wait_ge(s_idx[k], 16 * (at.n + 1))
                        tick()
                        pool.wait_ge(s_p1, at.G + 1)
                        tick()
                        for t in range(GT):
                            g.indirect_dma_start(rows[k][:, t, :], None, tab_b,
                                                 bass.IndirectOffsetOnAxis(ap=idx[k][:, t:t + 1], axis=0)
                                                 ).then_inc(s_rows[k], 16)
            low_parts(3)
            pool.wait_ge(s_ztab, 16 * K * NI)

            def add_group(i, k, at_start):
                at = At(i, k)
                pool.wait_ge(s_rid, at.g + SL + 1)
                tick()
                pool.wait_ge(s_rm, at.g + 3)
                tick()
                for t in range(GT):
                    if not (at_start and k == 0):
                        pool.wait_ge(s_add[t], 16 * at.g)
                        if t == GT - 1:
                            pool.sem_inc(s_landed, 1)
                        else:
                            tick()
                    g.indirect_dma_start(rel_tab[t], bass.IndirectOffsetOnAxis(ap=r_row[k][:, t:t + 1], axis=0),
                                         msg[k][:, t, :], None, compute_op=ALU.add).then_inc(s_add[t], 16)

            for k in range(SL):
                add_group(0, k, True)
            with loop(pool, 1, NI) as i:
                for _, k in body_groups(i):
                    add_group(i, k, False)
            with loop(pool, 0, NB // 2) as i:
                for s in range(2):
                    pool.wait_ge(s_part[s], 16 * K * (i + 1))
                    pool.wait_ge(s_tot, 2 * i + s + 1)
                    g.tensor_tensor(sum23[s], part[s][:, 2, :], part[s][:, 3, :], ALU.add).then_inc(s_23, 1)

        @block.tensor
        def _(pe):
            mm, tr = pe.matmul, pe.transpose
            pe.wait_ge(s_pv, PV_FULL)
            for c in range(LC):
                last = mm(ps[0:NBT, 0, 0:1], full[:, c, :], ones[:, :], start=(c == 0), stop=(c == LC - 1))
            last.then_inc(s_pt, 1)
            pe.wait_ge(s_pv, PV_START)
            mm(ps[0:NB, 1, 0:1], step_mat[0:NBT, 0:NB], start, start=True, stop=True).then_inc(s_pt, 1)
            pe.wait_ge(s_pv, PV_TILES)
            mm(ps[0:NB, 2, 0:1], upto_mat[0:NB, 0:NB], nt_f, start=True, stop=True).then_inc(s_pt, 1)
            pe.wait_ge(s_pv, PV_PAST)
            for q in range(NQ):
                last = mm(ps[:, 3, 2 * q:2 * q + 2], past[:, q * P:(q + 1) * P], shift2, start=True, stop=True)
            last.then_inc(s_pt, 1)
            pe.wait_ge(s_w, 13 * 16)
            for r in range(R):
                last = tr(flat[:, 2048 + r * P:2048 + (r + 1) * P], wr_raw[:, r, :], ident[:, :])
            last.then_inc(s_pt, 1)
            with loop(pe, 0, NQ // 2) as i:
                pe.wait_ge(s_wv, (i + 1) * WV)
                for s in range(2):
                    for f, v in enumerate((src_f[s], end_f[s], loc_f[s], key_f[s])):
                        last = tr(ps[:, 6 + s, f * P:(f + 1) * P], v, ident[:, :])
                last.then_inc(s_wt, 1)

            def products(l, i, s, turn=None):
                cc = l * NC + 2 * i + s
                pe.wait_ge(s_xs, cc + 1)
                pe.wait_ge(s_af, cc + 1)
                for b in range(CB):
                    last = mm(flat[:, b * P:(b + 1) * P], xs[s][:, b * P:(b + 1) * P], wd[:, l], start=True, stop=True)
                last.then_inc(s_ta, 1)
                if turn:
                    turn_x(*turn)
                pe.wait_ge(s_bf, cc + 1)
                for b in range(CB):
                    last = mm(flat[:, 1024 + b * P:1024 + (b + 1) * P], xs[s][:, b * P:(b + 1) * P], w1[:, l, 1],
                              start=True, stop=True)
                last.then_inc(s_tb, 1)

            def turn_x(i, s, extra=0):
                pe.wait_ge(s_xin[s], 16 * (i + 1) + extra)
                for b in range(CB):
                    last = tr(flat[:, 3072 + b * P:3072 + (b + 1) * P], xin[s][:, b, :], ident[:, :])
                last.then_inc(s_xt, 1)

            def turn_y(i, s):
                c = 2 * i + s
                pe.wait_ge(s_xs, 3 * NC + c + 1)
                pe.wait_ge(s_res, c + 1)
                for b in range(CB):
                    last = tr(flat[:, s * 1024 + b * P:s * 1024 + (b + 1) * P], xs[s][:, b * P:(b + 1) * P],
                              ident[:, :])
                last.then_inc(s_mt, 1)

            def step(l, i, k, lo=False, hi=False):
                live = lambda d: not ((lo and k < d) or (hi and k >= d))
                if live(0):
                    at = At(i, k, 0, l * NG, l * NI)
                    _, blk = nc.values_load_multi_w_load_instructions(
                        blocks[0:1, bass.ds(at.g * GT, GT)], engines=[PE_ENGINE], min_val=0, max_val=NB,
                        skip_runtime_bounds_check_because=WHY)
                    pe.wait_ge(s_hot, at.G + 1)
                    pe.wait_ge(s_h1, at.G + 1)
                    pe.wait_ge(s_rows[at.k], 64 * (at.n + 1))
                    for t in range(GT):
                        to = ps[:, at.s, t * P:(t + 1) * P]
                        for h in range(3):
                            mm(to, tab_a[:, bass.ds(blk[t] * (3 * P) + h * P, P)], hot_t[at.s][:, t * P:(t + 1) * P],
                               start=(h == 0), stop=False)
                        last = mm(to, rows[at.k][:, t, :], ident[:, :], start=False, stop=True)
                    last.then_inc(s_p1, 1)
                if live(1):
                    at = At(i, k, 1, l * NG)
                    pe.wait_ge(s_h1, at.G + 3)
                    pe.wait_ge(s_h2, at.G + 1)
                    mm(ps[:, 2 + at.s, :], w2[:, l], h1[at.s], start=True, stop=True).then_inc(s_p2, 1)
                if live(2):
                    at = At(i, k, 2, l * NG)
                    pe.wait_ge(s_scan, at.G + 3)
                    pe.wait_ge(s_h2e, at.G + 1)
                    for t in range(GT):
                        last = tr(ps[:, 4 + at.s, t * P:(t + 1) * P], scan[at.s][:, t * P:(t + 1) * P], ident[:, :])
                    last.then_inc(s_p3, 1)
                if live(3):
                    at = At(i, k, 3, l * NG)
                    pe.wait_ge(s_h2e, at.G + 3)
                    pe.wait_ge(s_ends, at.G + SL + 1)
                    pe.wait_ge(s_agg, GT * at.G)
                    for t in range(GT):
                        last = mm(ps[:, 6 + at.s, t * P:(t + 1) * P], h2e[at.s][:, t * P:(t + 1) * P],
                                  ends[at.s][:, t, :], start=True, stop=True)
                    last.then_inc(s_p4, 1)

            for q in (s_xt, s_tb, s_mt):
                pe.sem_inc(q, 2)
            pe.sem_inc(s_p1, SL)
            for q in (s_p2, s_p3, s_p4):
                pe.sem_inc(q, 2)
            for l in range(3):
                if l == 0:
                    turn_x(0, 0)
                    with loop(pe, 0, NC // 2 - 1) as i:
                        products(0, i, 0, turn=(i, 1))
                        products(0, i, 1, turn=(i + 1, 0))
                    products(0, NC // 2 - 1, 0, turn=(NC // 2 - 1, 1, 16))
                    products(0, NC // 2 - 1, 1)
                    pe.wait_ge(s_blk, 32)
                else:
                    with loop(pe, 0, NC // 2) as i:
                        for s in range(2):
                            products(l, i, s)
                pe.wait_ge(s_lo, NC * (l + 1) + 2)
                for k in range(SL):
                    step(l, 0, k, lo=True)
                with loop(pe, 1, NI) as i:
                    for _, k in body_groups(i):
                        step(l, i, k)
                for k in range(SL - 1):
                    step(l, NI, k, hi=True)
            with loop(pe, 0, NC // 2) as i:
                for s in range(2):
                    turn_y(i, s)
            pe.wait_ge(s_lo, NC * 4 + 2)

            def rel_step(i, k, lo=False, hi=False):
                live = lambda d: not ((lo and k < d) or (hi and k >= d))
                if live(0):
                    at = At(i, k)
                    pe.wait_ge(s_rh, at.g + 3)
                    pe.wait_ge(s_rs, at.g + 1)
                    for t in range(GT):
                        last = mm(ps[:, at.s, t * P:(t + 1) * P], hot_e[at.s][:, t, :], same[at.s][:, t, :],
                                  start=True, stop=True)
                    last.then_inc(s_ra, 1)
                if live(1):
                    at = At(i, k, 1)
                    _, blk = nc.values_load_multi_w_load_instructions(
                        blocks[0:1, bass.ds(at.g * GT, GT)], engines=[PE_ENGINE], min_val=0, max_val=NB,
                        skip_runtime_bounds_check_because=WHY)
                    pe.wait_ge(s_rs, at.g + 3)
                    pe.wait_ge(s_rm, at.g + 1)
                    for t in range(GT):
                        by = spread[at.s][:, t * P:(t + 1) * P]
                        for h in range(3):
                            mm(ps[:, 2 + at.s, t * P:(t + 1) * P], by,
                               tab_a[:, bass.ds(blk[t] * (3 * P) + h * P, P)], start=(h == 0), stop=(h == 2))
                        last = mm(ps[:, 4 + at.s, t:t + 1], by, ones_b[:, :], start=True, stop=True)
                    last.then_inc(s_rb, 1)

            for q in (s_ra, s_rb):
                pe.sem_inc(q, 2)
            for k in range(SL):
                rel_step(0, k, lo=True)
            with loop(pe, 1, NI) as i:
                for _, k in body_groups(i):
                    rel_step(i, k)
            rel_step(NI, 0, hi=True)
            for q in (s_ft, s_fm):
                pe.sem_inc(q, 2)

            def turn_block(b, s):
                pe.wait_ge(s_sc, b + 3)
                pe.wait_ge(s_fa, b + 1)
                for r in range(R):
                    last = tr(flat[:, s * 1024 + r * P:s * 1024 + (r + 1) * P], mean[s][:, r, :], ident[:, :])
                last.then_inc(s_ft, 1)

            def relate_block(b, s):
                pe.wait_ge(s_fa, b + 3)
                pe.wait_ge(s_fy, b + 1)
                for r in range(R):
                    last = mm(ps[:, 4 + s, 0:P], mean_t[s][:, r * P:(r + 1) * P], wr_t[:, r, :],
                              start=(r == 0), stop=(r == R - 1))
                last.then_inc(s_fm, 1)

            turn_block(0, 0)
            with loop(pe, 0, NB // 2 - 1) as i:
                turn_block(2 * i + 1, 1)
                relate_block(2 * i, 0)
                turn_block(2 * i + 2, 0)
                relate_block(2 * i + 1, 1)
            turn_block(NB - 1, 1)
            relate_block(NB - 2, 0)
            relate_block(NB - 1, 1)

        @block.scalar
        def _(act):
            tick = lambda: act.sem_inc(s_tick["act"], 1)
            a_ = nc.scalar.activation

            def copy_chunk(l, i, s):
                c = 2 * i + s
                if l == 0:
                    act.wait_ge(s_xt, c + 3)
                if l == 3:
                    act.wait_ge(s_mt, c + 1)
                else:
                    act.wait_ge(s_tb, l * NC + c + 1)
                tick()
                if l == 0:
                    a_(xs[s], flat[:, 3072:3072 + CB * P], ACT.Copy).then_inc(s_xs, 1)
                else:
                    a_(xs[s], chunk_of(agg, c), ACT.Copy if l == 3 else ACT.Relu).then_inc(s_xc, 1)

            def b_chunk(l, i, s):
                cc = l * NC + 2 * i + s
                act.wait_ge(s_tb, cc + 3)
                after(act, s_bd[s], 16 * (l * (NC // 2) + i))
                tick()
                a_(bout[s], flat[:, 1024:1024 + CB * P], ACT.Copy).then_inc(s_bf, 1)

            def high_part(l, i, s):
                c = 2 * i + s
                act.wait_ge(s_af, l * NC + c + 2)
                tick()
                of = afull[s] if l < 3 else chunk_of(agg, c)
                a_(part_view(c, 0), blocked(of), ACT.Copy).then_inc(s_hi, 1)

            def mid_part(l, i, s):
                c = 2 * i + s
                act.wait_ge(s_re, l * NC + c + 1)
                tick()
                a_(part_view(c, 1), blocked(afull[s]), ACT.Copy).then_inc(s_mid, 1)

            def root_chunk(i, s):
                act.wait_ge(s_y, 2 * i + s + 1)
                tick()
                a_(dev[s], mv[s][:, :, 1], ACT.Sqrt, bias=eps[:, :]).then_inc(s_dev, 1)

            def chunk_step(l, i, s, first=False, last=False):
                before = (i, 0) if s == 1 else (i - 1, 1)
                if not first and l < 3:
                    b_chunk(l, *before)
                if not last:
                    copy_chunk(l, *((i, 1) if s == 0 else (i + 1, 0)))
                if l == 3:
                    root_chunk(i, s)
                if not first:
                    mid_part(l, *before)
                high_part(l, i, s)

            def chunks(l):
                copy_chunk(l, 0, 0)
                chunk_step(l, 0, 0, first=True)
                chunk_step(l, 0, 1)
                with loop(act, 1, NC // 2 - 1) as i:
                    for s in range(2):
                        chunk_step(l, i, s)
                chunk_step(l, NC // 2 - 1, 0)
                chunk_step(l, NC // 2 - 1, 1, last=True)
                if l < 3:
                    b_chunk(l, NC // 2 - 1, 1)
                mid_part(l, NC // 2 - 1, 1)

            def step(l, i, k, lo=False, hi=False):
                live = lambda d: not ((lo and k < d) or (hi and k >= d))
                if live(0):
                    at = At(i, k, 0, l * NG)
                    act.wait_ge(s_p1, at.G + SL + 1)
                    act.wait_ge(s_p2, at.G + 1)
                    a_(h1[at.s], ps[:, at.s, :], ACT.Relu).then_inc(s_h1, 1)
                if live(1):
                    at = At(i, k, 1, l * NG)
                    act.wait_ge(s_p2, at.G + 3)
                    act.wait_ge(s_scan, at.G + 1)
                    a_(h2[at.s], ps[:, 2 + at.s, :], ACT.Identity, bias=b2col[:, l:l + 1]).then_inc(s_h2, 1)
                if live(2):
                    at = At(i, k, 2, l * NG)
                    act.wait_ge(s_p3, at.G + 3)
                    act.wait_ge(s_p4, at.G + 1)
                    a_(h2e[at.s], ps[:, 4 + at.s, :], ACT.Copy).then_inc(s_h2e, 1)

            def clear(l, i):
                if l < 2:
                    for t in (2 * l, 2 * l + 1):
                        act.dma_start(rel_tab[t][bass.ds(i * ZR, ZR), :].rearrange("(p r) w -> p (r w)", p=ZP),
                                      zeros[0:ZP, :]).then_inc(s_ztab, 16)

            for q in (s_h1, s_h2, s_h2e):
                act.sem_inc(q, 2)
            act.sem_inc(s_bf, 1)
            for l in range(3):
                if l > 0:
                    act.wait_ge(s_agg, GT * NG * l + GT)
                chunks(l)
                if l == 0:
                    act.wait_ge(s_pv, PV_CONST)
                    act.wait_ge(s_w, 13 * 16)
                act.wait_ge(s_lo, NC * (l + 1) + 2)
                for s in range(2):
                    act.wait_ge(s_bd[s], 8 * NC * (l + 1))
                for k in range(SL):
                    step(l, 0, k, lo=True)
                clear(l, 0)
                with loop(act, 1, NI) as i:
                    for _, k in body_groups(i):
                        step(l, i, k)
                    clear(l, i)
                for k in range(SL - 1):
                    step(l, NI, k, hi=True)

            act.wait_ge(s_agg, GT * NG * 3 + GT)
            chunks(3)
            for q in (s_rs, s_rm):
                act.sem_inc(q, 2)

            act.wait_ge(s_lo, NC * 4 + 2)

            def rel_step(i, k, lo=False, hi=False):
                live = lambda d: not ((lo and k < d) or (hi and k >= d))
                if live(0):
                    at = At(i, k)
                    act.wait_ge(s_ra, at.g + 3)
                    act.wait_ge(s_rb, at.g + 1)
                    a_(spread[at.s], ps[:, at.s, :], ACT.Copy).then_inc(s_rs, 1)
                if live(1):
                    at = At(i, k, 1)
                    if not (isinstance(at.g, int) and at.g < SL):
                        act.wait_ge(s_landed, at.g - SL + 1)
                        tick()
                    act.wait_ge(s_rb, at.g + 3)
                    a_(msg[at.k][:, :, 0:P], ps[:, 2 + at.s, :].rearrange("p (t f) -> p t f", f=P), ACT.Copy)
                    a_(msg[at.k][:, :, P], ps[:, 4 + at.s, 0:GT], ACT.Copy).then_inc(s_rm, 1)

            for k in range(SL):
                rel_step(0, k, lo=True)
            for k in range(SL):
                rel_step(1, k)
            with loop(act, 2, NI) as i:
                for _, k in body_groups(i):
                    rel_step(i, k)
            rel_step(NI, 0, hi=True)
            act.sem_inc(s_fa, 2)

            def turned(b, s):
                act.wait_ge(s_ft, b + 3)
                act.wait_ge(s_fm, b + 1)
                a_(mean_t[s], flat[:, s * 1024:(s + 1) * 1024], ACT.Copy).then_inc(s_fa, 1)

            def means(b, s):
                act.wait_ge(s_tot, b + 3)
                act.wait_ge(s_ft, b + 1)
                tick()
                sums = sum01[s].rearrange("p (r w) -> p r w", r=R)
                for r in range(R):
                    last = a_(mean[s][:, r, :], sums[:, r, 0:P], ACT.Copy, scale=inv_cnt[s][:, r:r + 1])
                last.then_inc(s_sc, 1)

            def root(b, s):
                act.wait_ge(s_fy, b + 3)
                a_(o_dev[s], o_mv[s][:, 1:2], ACT.Sqrt, bias=eps[:, :]).then_inc(s_fd, 1)

            def last_step(b, s):
                if not isinstance(b, int) or b >= 2:
                    root(b - 2, s)
                if not isinstance(b, int) or b + 1 < NB:
                    means(b + 1, 1 - s)
                if not isinstance(b, int) or b < NB:
                    turned(b, s)

            act.sem_inc(s_sc, 2)
            means(0, 0)
            for b in range(4):
                last_step(b, b % 2)
            with loop(act, 2, NB // 2 - 1) as i:
                for s in range(2):
                    last_step(2 * i + s, s)
            for b in range(NB - 2, NB + 2):
                last_step(b, b % 2)

        @block.vector
        def _(dve):
            v = nc.vector
            tick = lambda: dve.sem_inc(s_tick["dve"], 1)
            done = [0]

            def pv(ins):
                done[0] += 1
                ins.then_inc(s_pv, 1)
                dve.wait_ge(s_pv, done[0])
                return done[0]

            dve.wait_ge(s_gp, GP_ALL)
            pv(v.tensor_scalar(ident[:, :], iota[:, :], pidx[:, 0:1], None, ALU.is_equal))
            pv(v.tensor_scalar(below[:, :], iota[:, :], pidx[:, 0:1], None, ALU.is_lt))
            pv(v.tensor_scalar(upto_mat, iota[:, :], pidx[:, 0:1], None, ALU.is_ge))
            pv(v.tensor_scalar(starts[0], iota[:, :], 1.0, pidx[:, 0:1], ALU.add, ALU.is_equal))
            pv(v.tensor_tensor(step_mat, starts[0], ident[:, :], ALU.subtract))
            pv(v.memset(ones[:, :], 1.0))
            pv(v.memset(ones_b[:, :], 1.0))
            pv(v.memset(eps[:, :], EPS))
            pv(v.memset(zeros[:, :], 0.0))
            pv(v.tensor_scalar(trash_col[:, :], pidx[:, :], float(TRASH), None, ALU.add))
            pv(v.tensor_scalar(trash_row, iota[:, :], float(TRASH), None, ALU.add))
            assert pv(v.memset(tab_a[:, NB * 3 * P:], 0.0)) == PV_CONST
            dve.wait_ge(s_last, 16)
            pv(v.tensor_copy(last_f, last_i))
            for c in range(LC):
                compared = v.tensor_scalar(full[:, c, :], thr_row, last_f[:, c:c + 1], None, ALU.is_gt)
            assert pv(compared) == PV_FULL
            dve.wait_ge(s_pt, 1)
            pv(v.tensor_copy(cnt0, ps[0:NBT, 0, 0:1]))
            assert pv(v.tensor_scalar(win_at, cnt0, float(P), 1.0, ALU.mult, ALU.add)) == PV_WIN0
            dve.wait_ge(s_row0, 16)
            pv(v.tensor_copy(win_f, win_i))
            pv(v.tensor_scalar(win_f, win_f, thr_col, None, ALU.is_lt))
            pv(v.tensor_reduce(cnt1, win_f, AX_X, ALU.add))
            assert pv(v.scalar_tensor_tensor(out=start, in0=cnt0, scalar=float(P), in1=cnt1,
                                             op0=ALU.mult, op1=ALU.add)) == PV_START
            dve.wait_ge(s_pt, 2)
            pv(v.tensor_copy(deg_b, ps[0:NB, 1, 0:1]))
            pv(v.tensor_scalar(nt_i, deg_b, float(P - 1), None, ALU.add))
            pv(v.tensor_scalar(nt_i, nt_i, 7, None, ALU.arith_shift_right))
            assert pv(v.tensor_copy(nt_f, nt_i)) == PV_TILES
            dve.wait_ge(s_pt, 3)
            pv(v.tensor_copy(upto, ps[0:NB, 2, 0:1]))
            pv(v.memset(shift2[:, 0:1], 1.0))
            pv(v.scalar_tensor_tensor(out=shift2[:, 1:2], in0=nt_f, scalar=-float(P), in1=deg_b,
                                      op0=ALU.mult, op1=ALU.add))
            assert pv(v.tensor_scalar(past, iota_j, upto, None, ALU.is_ge)) == PV_PAST
            dve.wait_ge(s_pt, 4)
            found = ps[:, 3, 0:2 * NQ].rearrange("p (q f) -> p q f", f=2)
            pv(v.tensor_copy(blk_f, found[:, :, 0]))
            pv(v.tensor_scalar(base_f, blk_f, float(P), None, ALU.mult))
            pv(v.tensor_tensor(from_f, found[:, :, 1], jbase, ALU.add))
            pv(v.tensor_scalar(from_i, from_f, float(E), None, ALU.min))
            assert pv(v.tensor_copy(blk_i, blk_f)) == PV_BLK
            dve.wait_ge(s_w, 13 * 16)
            for l in range(3):
                pv(v.tensor_tensor(wd[:, l], w1[:, l, 0], w1[:, l, 1], ALU.subtract))
            dve.wait_ge(s_pt, 5)
            pv(v.tensor_copy(wr_t[:, :, :].rearrange("p r j -> p (r j)"), flat[:, 2048:2048 + R * P]))
            def windows(i):
                for s in range(2):
                    last = v.tensor_copy(win_from[s], from_i[:, bass.ds(2 * i + s, 1)])
                last.then_inc(s_from, 1)

            def edge_pair(i, last=False):
                n = [0]

                def stage(*parts):
                    for part in parts:
                        for s in range(2):
                            end = part(s)
                    n[0] += 1
                    end.then_inc(s_wv, 1)
                    dve.wait_ge(s_wv, i * WV + n[0])
                    tick()

                for s in range(2):
                    dve.wait_ge(s_win[s], 48 * (i + 1))
                tick()
                stage(
                    lambda s: v.tensor_copy(win_base[s], base_f[:, bass.ds(2 * i + s, 1)]),
                    lambda s: v.tensor_copy(dst_f[s], dst_w[s]),
                    lambda s: v.tensor_copy(src_f[s], src_w[s]),
                    lambda s: v.scalar_tensor_tensor(out=raw_key[s], in0=src_w[s], scalar=float(R), in1=typ_w[s],
                                                     op0=ALU.mult, op1=ALU.add))
                if not last:
                    windows(i + 1)
                stage(
                    lambda s: v.tensor_scalar(loc_f[s], dst_f[s][:, 1:P + 1], win_base[s], float(OUT_OF_BLOCK),
                                              ALU.subtract, ALU.min),
                    lambda s: v.tensor_tensor(starts[s], dst_f[s][:, 1:P + 1], dst_f[s][:, 0:P], ALU.not_equal),
                    lambda s: v.tensor_tensor(stops[s], dst_f[s][:, 1:P + 1], dst_f[s][:, 2:P + 2], ALU.not_equal),
                    lambda s: v.tensor_tensor(key_d[s], raw_key[s], trash_row, ALU.subtract))
                stage(
                    lambda s: v.tensor_scalar(signs[s], starts[s], -2.0, 1.0, ALU.mult, ALU.add),
                    lambda s: v.tensor_scalar(no_end[s], stops[s], -float(OUT_OF_BLOCK), float(OUT_OF_BLOCK),
                                              ALU.mult, ALU.add),
                    lambda s: v.scalar_tensor_tensor(out=kept_d[s], in0=loc_f[s], scalar=float(P), in1=key_d[s],
                                                     op0=ALU.is_lt, op1=ALU.mult))
                for s in range(2):
                    after(dve, s_store[s], 80 * i)
                tick()
                stage(
                    lambda s: v.tensor_tensor(end_f[s], no_end[s], loc_f[s], ALU.max),
                    lambda s: v.tensor_tensor(key_f[s], kept_d[s], trash_row, ALU.add))
                for s in range(2):
                    v.tensor_scalar(cut_b[s], signs[s], BIG, None, ALU.mult)
                    v.tensor_copy(loc_b[s], loc_f[s])
                dve.wait_ge(s_wt, i + 1)
                tick()
                for s in range(2):
                    v.tensor_copy(src_o[s], ps[:, 6 + s, 0:P])
                    end = v.tensor_copy(meta_o[s].rearrange("p (j f) -> p f j", f=3),
                                        ps[:, 6 + s, P:4 * P].rearrange("p (f j) -> p f j", f=3))
                end.then_inc(s_wo, 1)
                assert n[0] == WV

            windows(0)
            edge_pair(0)
            with loop(dve, 1, NQ // 2 - 1) as i:
                edge_pair(i)
            edge_pair(NQ // 2 - 1, last=True)
            for s in range(2):
                dve.wait_ge(s_store[s], 80 * (NQ // 2))
            dve.wait_ge(s_blk, 32)
            dve.sem_inc(s_scan, 2)
            dve.sem_inc(s_ends, SL)
            dve.sem_inc(s_agg, GT)
            dve.sem_inc(s_af, 1)
            def guard(l, i, s):
                c = 2 * i + s
                dve.wait_ge(s_xc, (l - 1) * NC + c + 1)
                tick()
                v.tensor_scalar(bad, xs[s], 0.0, 0.0, ALU.mult, ALU.not_equal).then_inc(s_tv, 1)
                dve.wait_ge(s_tv, (l - 1) * NC + c + 1)
                tick()
                v.copy_predicated(xs[s], bad, zeros[:, 0:CB * P]).then_inc(s_xs, 1)

            def remainder(l, i, s):
                c = 2 * i + s
                dve.wait_ge(s_hi, l * NC + c + 1)
                if l == 3:
                    dve.wait_ge(s_lo, l * NC + c + 1)
                tick()
                of = afull[s] if l < 3 else chunk_of(agg, c)
                v.tensor_tensor(blocked(afull[s]), blocked(of), part_view(c, 0), ALU.subtract).then_inc(s_re, 1)

            def table_step(l, i, s, last=False):
                cc = l * NC + 2 * i + s
                dve.wait_ge(s_ta, cc + 1)
                dve.wait_ge(s_lo, cc + 1)
                tick()
                v.tensor_tensor(blocked(afull[s]), blocked(flat[:, 0:CB * P]),
                                b1row[:, l:l + 1, :].to_broadcast([P, CB, P]), ALU.add).then_inc(s_af, 1)
                if l > 0 and not last:
                    guard(l, *((i, 1) if s == 0 else (i + 1, 0)))
                remainder(l, i, s)

            def step(l, i, k, lo=False, hi=False):
                live = lambda d: not ((lo and k < d) or (hi and k >= d))
                if live(0):
                    at = At(i, k, 0, l * NG, l * NI)
                    dve.wait_ge(s_bc[at.k], 32 * (at.n + 1))
                    dve.wait_ge(s_p1, at.G + SL - 1)
                    v.tensor_scalar(hot_t[at.s], dst_bc[at.k], pidx[:, 0:1], None, ALU.is_equal).then_inc(s_hot, 1)
                if live(2):
                    at = At(i, k, 2, l * NG)
                    dve.wait_ge(s_h2, at.G + 3)
                    dve.wait_ge(s_p3, at.G + 1)
                    dve.wait_ge(s_scan, at.G + 2)
                    v.tensor_tensor_scan(scan[at.s], cut_bc[at.k], h2[at.s],
                                         scan[1 - at.s][:, GT * P - 1:GT * P], ALU.min, ALU.max).then_inc(s_scan, 1)
                    dve.wait_ge(s_p4, at.G + 1)
                    dve.wait_ge(s_meta[at.k], 16 * (at.i + l * NI + 1))
                    tick()
                    for t in range(GT):
                        last = v.tensor_scalar(ends[at.s][:, t, :], iota[:, :],
                                               meta[at.k][:, t, 0:1], None, ALU.is_equal)
                    last.then_inc(s_ends, 1)
                if live(4):
                    at = At(i, k, 4, l * NG)
                    _, blk = nc.values_load_multi_w_load_instructions(
                        blocks[0:1, bass.ds(at.g * GT, GT)], engines=[DVE_ENGINE], min_val=0, max_val=NB,
                        skip_runtime_bounds_check_because=WHY)
                    dve.wait_ge(s_p4, at.G + 3)
                    tick()
                    for t in range(GT):
                        dve.wait_ge(s_agg, GT * at.G + t + GT)
                        tick()
                        to = agg[:, bass.ds(blk[t] * P, P)]
                        v.tensor_tensor(to, ps[:, 6 + at.s, t * P:(t + 1) * P], to, ALU.add).then_inc(s_agg, 1)

            for l in range(3):
                if l > 0:
                    guard(l, 0, 0)
                with loop(dve, 0, NC // 2 - 1) as i:
                    for s in range(2):
                        table_step(l, i, s)
                for s in range(2):
                    table_step(l, NC // 2 - 1, s, last=(s == 1))
                dve.wait_ge(s_lo, NC * (l + 1) + 2)
                dve.wait_ge(s_tb, NC * (l + 1) + 2)
                for s in range(2):
                    dve.wait_ge(s_bd[s], 8 * NC * (l + 1))
                v.memset(scan[1][:, GT * P - 1:GT * P], 0.0).then_inc(s_zero, 1)
                v.memset(agg[:, :], 0.0).then_inc(s_zero, 1)
                dve.wait_ge(s_zero, 2 * (l + 1))
                for k in range(SL):
                    step(l, 0, k, lo=True)
                with loop(dve, 1, NI) as i:
                    for _, k in body_groups(i):
                        step(l, i, k)
                for k in range(SL):
                    step(l, NI, k, hi=True)
                dve.wait_ge(s_agg, GT * NG * (l + 1) + GT)

            dve.sem_inc(s_res, 2)
            guard(3, 0, 0)

            def norm_chunk(i, s, first=False, last=False):
                c = 2 * i + s
                dve.wait_ge(s_mt, c + 3)
                loads = NC // 2 + i + 1 + (1 if s == 1 else 0) + (1 if last else 0)
                dve.wait_ge(s_xin[s], 16 * loads)
                tick()
                m = [0]

                def ch(ins):
                    m[0] += 1
                    ins.then_inc(s_fv, 1)
                    dve.wait_ge(s_fv, c * NVC + m[0])
                    tick()

                v.tensor_tensor(resid[s], flat[:, s * 1024:s * 1024 + CB * P],
                                xin[s].rearrange("p b f -> p (b f)"), ALU.add).then_inc(s_res, 1)
                dve.wait_ge(s_res, c + 3)
                tick()
                for b in range(CB):
                    end = v.bn_stats(st6[:, b, :], resid[s][:, b * P:(b + 1) * P])
                ch(end)
                for b in range(CB):
                    end = v.bn_aggr(mv[s][:, b, :], st6[:, b, :])
                end.then_inc(s_y, 1)
                if not last:
                    guard(3, *((i, 1) if s == 0 else (i + 1, 0)))
                if not first:
                    remainder(3, *((i, 0) if s == 1 else (i - 1, 1)))
                dve.wait_ge(s_dev, c + 1)
                tick()
                ch(v.reciprocal(inv_dev, dev[s]))
                for b in range(CB):
                    end = v.tensor_scalar(agg[:, bass.ds((c * CB + b) * P, P)], resid[s][:, b * P:(b + 1) * P],
                                          mv[s][:, b, 0:1], inv_dev[:, b:b + 1], ALU.subtract, ALU.mult)
                end.then_inc(s_af, 1)
                assert m[0] == NVC

            norm_chunk(0, 0, first=True)
            norm_chunk(0, 1)
            with loop(dve, 1, NC // 2 - 1) as i:
                for s in range(2):
                    norm_chunk(i, s)
            norm_chunk(NC // 2 - 1, 0)
            norm_chunk(NC // 2 - 1, 1, last=True)
            remainder(3, NC // 2 - 1, 1)
            dve.wait_ge(s_lo, NC * 4 + 2)
            dve.sem_inc(s_rh, 2)
            dve.sem_inc(s_rid, SL)

            def rel_group(i, k, lo):
                at = At(i, k)
                m = [0]

                def ch(ins):
                    m[0] += 1
                    ins.then_inc(s_rv, 1)
                    dve.wait_ge(s_rv, at.g * NVR + m[0])

                dve.wait_ge(s_rl[k], 32 * (i + 1))
                tick()
                dve.wait_ge(s_ra, at.g + 1)
                tick()
                for t in range(GT):
                    v.tensor_scalar(hot_e[at.s][:, t, :], iota[:, :], r_meta[k][:, t, 1:2], None,
                                    ALU.is_equal)
                    last = v.tensor_scalar(same[at.s][:, t, :], key_bc[k][:, t * P:(t + 1) * P],
                                           r_meta[k][:, t, 2:3], None, ALU.is_equal)
                last.then_inc(s_rh, 1)
                dve.wait_ge(s_rh, at.g + 3)
                tick()
                ch(v.tensor_tensor(earlier, same[at.s], below[:, :].unsqueeze(1).to_broadcast([P, GT, P]), ALU.mult))
                ch(v.tensor_reduce(rank, earlier, AX_X, ALU.add))
                ch(v.tensor_scalar(first, rank, 0.0, None, ALU.is_equal))
                ch(v.scalar_tensor_tensor(out=kept, in0=r_meta[k][:, :, 2], scalar=trash_col[:, 0:1],
                                          in1=first, op0=ALU.subtract, op1=ALU.mult))
                assert m[0] == NVR
                if not lo:
                    dve.wait_ge(s_landed, at.g - SL + 1)
                    tick()
                v.tensor_scalar(r_row[k], kept, trash_col[:, 0:1], None, ALU.add).then_inc(s_rid, 1)

            for k in range(SL):
                rel_group(0, k, True)
            with loop(dve, 1, NI) as i:
                for _, k in body_groups(i):
                    rel_group(i, k, False)
            for t in range(K):
                dve.wait_ge(s_add[t], 16 * NG)
            dve.wait_ge(s_rb, NG + 2)
            dve.sem_inc(s_tot, 2)
            dve.sem_inc(s_fy, 2)

            def sums(i, s):
                b = 2 * i + s
                m = [0]

                def ch(ins):
                    m[0] += 1
                    ins.then_inc(s_fv, 1)
                    dve.wait_ge(s_fv, NC * NVC + b * NVB + m[0])
                    tick()

                dve.wait_ge(s_part[s], 16 * K * (i + 1))
                dve.wait_ge(s_sc, b + 1)
                tick()
                v.tensor_tensor(sum01[s], part[s][:, 0, :], part[s][:, 1, :], ALU.add).then_inc(s_01, 1)
                dve.wait_ge(s_01, b + 1)
                dve.wait_ge(s_23, b + 1)
                tick()
                ch(v.tensor_tensor(sum01[s], sum01[s], sum23[s], ALU.add))
                ch(v.tensor_scalar(cnt[s], sum01[s].rearrange("p (r w) -> p r w", r=R)[:, :, P], 1.0, None, ALU.max))
                v.reciprocal(inv_cnt[s], cnt[s]).then_inc(s_tot, 1)
                assert m[0] == NVB

            def variance(b, s):
                x1_block = agg[:, bass.ds(b * P, P)]
                dve.wait_ge(s_fm, b + 3)
                tick()

                def ch(ins, count):
                    ins.then_inc(s_norm, 1)
                    dve.wait_ge(s_norm, b * NVN + count)
                    tick()

                ch(v.scalar_tensor_tensor(out=y_in[s], in0=ps[:, 4 + s, 0:P], scalar=0.0, in1=x1_block,
                                          op0=ALU.max, op1=ALU.add), 1)
                ch(v.bn_stats(o_st6[s], y_in[s]), 2)
                v.bn_aggr(o_mv[s], o_st6[s]).then_inc(s_fy, 1)

            def result(b, i, s):
                dve.wait_ge(s_fd, b + 1)
                tick()
                v.reciprocal(o_inv[s], o_dev[s]).then_inc(s_fi, 1)
                dve.wait_ge(s_fi, b + 1)
                tick()
                after(dve, s_out[s], 16 * i)
                v.tensor_scalar(y_out[s], y_in[s], o_mv[s][:, 0:1], o_inv[s][:, 0:1], ALU.subtract, ALU.mult
                                ).then_inc(s_fo, 1)

            def last_step(i, s):
                b = 2 * i + s
                if not isinstance(b, int) or b + 1 < NB:
                    sums(*((i, 1) if s == 0 else (i + 1, 0)))
                if not isinstance(b, int) or b >= 2:
                    result(b - 2, i - 1, s)
                if not isinstance(b, int) or 1 <= b < NB + 1:
                    variance(b - 1, 1 - s)

            sums(0, 0)
            for i in range(2):
                for s in range(2):
                    last_step(i, s)
            with loop(dve, 2, NB // 2 - 1) as i:
                for s in range(2):
                    last_step(i, s)
            for i in range(NB // 2 - 1, NB // 2 + 1):
                for s in range(2):
                    last_step(i, s)


_LAYERS = ("in", "hid", "out")
_INS = ["x", "src", "dst", "edge_type_8"] + [
    f"L0_gnn_{p}_{l}" for l in _LAYERS for p in ("W1", "b1", "W2", "b2")] + ["L1_gnn_weights"]

def kernel(**inputs):
    import numpy as _np
    import concourse.bacc as _bacc
    from concourse import mybir as _mybir
    from concourse.bass_utils import run_bass_kernel_spmd as _run

    nc = _bacc.Bacc("TRN2", target_bir_lowering=False, num_devices=1)
    arrays, aps = {}, {}
    for name in _INS:
        a = _np.ascontiguousarray(inputs[name])
        arrays[f"in_{name}"] = a
        aps[name] = nc.dram_tensor(f"in_{name}", a.shape, _mybir.dt.from_np(a.dtype), kind="ExternalInput").ap()
    n, c = inputs["x"].shape
    out = nc.dram_tensor("out_0", (n, c), _mybir.dt.float32, kind="ExternalOutput").ap()
    params = [tuple(aps[f"L0_gnn_{p}_{l}"] for p in ("W1", "b1", "W2", "b2")) for l in _LAYERS]
    gnn_kernel(nc, aps["x"], aps["src"], aps["dst"], aps["edge_type_8"], params, aps["L1_gnn_weights"], out)
    r = _run(nc, [arrays], core_ids=[0])
    return r.results[0]["out_0"]
```
